# Optimizing a Trainium2 kernel written in Bass

```python
import numpy as np
import jax
import jax.numpy as jnp

def _softmax(x, axis=-1):
    return jax.nn.softmax(x, axis=axis)

def _gelu(x):
    return jax.nn.gelu(x, approximate=True)

def _silu(x):
    return jax.nn.silu(x)

def _sigmoid(x):
    return jax.nn.sigmoid(x)

def _layernorm(x, axis=-1, eps=1e-05):
    m = jnp.mean(x, axis=axis, keepdims=True)
    v = jnp.var(x, axis=axis, keepdims=True)
    return (x - m) / jnp.sqrt(v + eps)

def _scatter_add(tgt, idx, src, axis=0):
    return tgt.at[idx].add(src)

def _segment_sum(src, seg, n):
    return jax.ops.segment_sum(src, seg, n)
kernel_name = 'mk_flamingo_gated_d2_seqx_r8_036ee3'

def setup_inputs(seed: int=0):
    np.random.seed(seed)
    _w = jnp.asarray

    def _rec_inputs():
        import jax
        import jax.numpy as jnp
        _rk = jax.random.key(seed)
        x = -0.0005207 + 1.001 * jax.random.normal(jax.random.fold_in(_rk, 1), (4, 512, 128), jnp.float32)
        _lenS = 512 - jax.random.randint(jax.random.fold_in(_rk, 7), (4,), 0, max(1, 512 // 4) + 1, jnp.int32)
        _lenS2 = 154 - jax.random.randint(jax.random.fold_in(_rk, 8), (4,), 0, max(1, 154 // 4) + 1, jnp.int32)
        _ctx_1024P = jax.random.normal(jax.random.fold_in(_rk, 11), (4, 16, 128), jnp.float32)
        _ctx_1024c = jax.random.dirichlet(jax.random.fold_in(_rk, 511), 0.3 * jnp.ones((16,), jnp.float32), (4, 154))
        _ctx_1024t = jnp.einsum('bsk,bkd->bsd', _ctx_1024c, _ctx_1024P)
        _ctx_1024t = _ctx_1024t * jax.lax.rsqrt(jnp.mean(jnp.square(_ctx_1024t)) + 1e-12) * 0.953939
        ctx_1024 = -1.39393e-06 + 0.999914 * (_ctx_1024t + 0.3 * jax.random.normal(jax.random.fold_in(_rk, 611), (4, 154, 128), jnp.float32))
        itok_BxSx64_0_2047 = jax.random.randint(jax.random.fold_in(_rk, 12), (4, 512, 64), 0, 256, jnp.int32)
        _g = jax.random.normal(jax.random.fold_in(_rk, 9001), (2, 2), jnp.float32)
        _g = jnp.sign(_g) * jnp.maximum(jnp.abs(_g), 1.0) + (_g == 0) * 1.0
        g_xattn = _g[0]
        g_ffn = _g[1]
        return (x, ctx_1024, itok_BxSx64_0_2047, g_xattn, g_ffn)
    x, ctx_1024, itok_BxSx64_0_2047, g_xattn, g_ffn = _rec_inputs()

    def _L0_xattn_setup():
        import jax, jax.numpy as jnp
        import numpy as np
        B, NQ, NKV, K = (2, 128, 256, 64)
        D, H, LAT = (128, 16, 128)
        HD = D // H
        SCALE = 1.0 / np.sqrt(HD)
        key = jax.random.key(seed)
        ks = jax.random.split(key, 7)
        s = lambda fan_in: 1.0 / np.sqrt(fan_in)
        return {'x_q': jax.random.normal(ks[0], (B, NQ, D), jnp.float32), 'x_kv': jax.random.normal(ks[1], (B, NKV, D), jnp.float32), 'indices': jax.random.randint(ks[2], (B, NQ, K), 0, NKV), 'W_q': jax.random.normal(ks[3], (D, D), jnp.float32) * s(D), 'W_kv_down': jax.random.normal(ks[4], (LAT, D), jnp.float32) * s(D), 'W_kv_up': jax.random.normal(ks[5], (2 * D, LAT), jnp.float32) * s(LAT), 'W_out': jax.random.normal(ks[6], (D, D), jnp.float32) * s(D)}
    _L0_xattn_all = _L0_xattn_setup()
    _L0_xattn_in = {k: v for k, v in _L0_xattn_all.items() if k in ('W_q', 'W_kv_down', 'W_kv_up', 'W_out')}
    del _L0_xattn_all

    def _L0_ffn_setup():
        import jax, jax.numpy as jnp
        import numpy as np
        LN_EPS = 1e-05

        def _swiglu(h, w_gate_up, w_down):
            gu = h @ w_gate_up.T
            gate, up = jnp.split(gu, 2, axis=-1)
            return jax.nn.silu(gate) * up @ w_down.T
        key = jax.random.key(seed)
        ks = jax.random.split(key, 6)
        d_model, d_ff, E = (128, 512, 8)
        shared_d_ff = d_ff // 4
        routed_d_ff = d_ff - shared_d_ff
        B, S = (4, 256)
        x = jax.random.normal(ks[0], (B, S, d_model), dtype=jnp.float32)
        ln_gamma = jnp.ones((d_model,), jnp.float32)
        ln_beta = jnp.zeros((d_model,), jnp.float32)
        router_w = jax.random.normal(ks[1], (E, d_model), jnp.float32) * 0.02
        gate_up_w = jax.random.normal(ks[2], (E, 2 * routed_d_ff, d_model), jnp.float32) * (1.0 / np.sqrt(d_model))
        down_w = jax.random.normal(ks[3], (E, d_model, routed_d_ff), jnp.float32) * (1.0 / np.sqrt(routed_d_ff))
        shared_gate_up_w = jax.random.normal(ks[4], (2 * shared_d_ff, d_model), jnp.float32) * (1.0 / np.sqrt(d_model))
        shared_down_w = jax.random.normal(ks[5], (d_model, shared_d_ff), jnp.float32) * (1.0 / np.sqrt(shared_d_ff))
        return dict(x=x, ln_gamma=ln_gamma, ln_beta=ln_beta, router_w=router_w, gate_up_w=gate_up_w, down_w=down_w, shared_gate_up_w=shared_gate_up_w, shared_down_w=shared_down_w)
    _L0_ffn_all = _L0_ffn_setup()
    _L0_ffn_in = {k: v for k, v in _L0_ffn_all.items() if k in ('ln_gamma', 'ln_beta', 'router_w', 'gate_up_w', 'down_w', 'shared_gate_up_w', 'shared_down_w')}
    del _L0_ffn_all

    def _L1_xattn_setup():
        import jax, jax.numpy as jnp
        import numpy as np
        D_MODEL = 128
        NUM_HEADS = 16
        HEAD_DIM = D_MODEL // NUM_HEADS
        SCALE = HEAD_DIM ** (-0.5)
        BIAS_LEN = 128
        ROPE_BASE = 10000.0
        LN_EPS = 1e-05

        def _layernorm(x, gamma, beta):
            mu = jnp.mean(x, axis=-1, keepdims=True)
            var = jnp.mean(jnp.square(x - mu), axis=-1, keepdims=True)
            return (x - mu) * jax.lax.rsqrt(var + LN_EPS) * gamma + beta

        def _rope(x, cos, sin):
            half = HEAD_DIM // 2
            c = cos[None, None, :, :]
            s = sin[None, None, :, :]
            x_even, x_odd = (x[..., :half], x[..., half:])
            return jnp.concatenate([x_even * c - x_odd * s, x_even * s + x_odd * c], axis=-1)

        def _temporal_bias(L_q, L_kv):
            pos = jnp.arange(BIAS_LEN, dtype=jnp.float32)
            dist = jnp.abs(pos[None, :] - pos[:, None])
            bias = jnp.exp(-dist * 0.1) - dist * 0.05
            if L_q <= BIAS_LEN and L_kv <= BIAS_LEN:
                return bias[:L_q, :L_kv]
            return jax.image.resize(bias, (L_q, L_kv), method='bilinear')
        key = jax.random.key(seed)
        ks = jax.random.split(key, 8)
        B, Lq, Lkv = (8, 64, 64)
        return {'decoder_hidden': jax.random.normal(ks[0], (B, Lq, D_MODEL), jnp.float32), 'encoder_output': jax.random.normal(ks[1], (B, Lkv, D_MODEL), jnp.float32), 'Wqkv': jax.random.normal(ks[2], (3 * D_MODEL, D_MODEL), jnp.float32) * 0.02, 'Wout': jax.random.normal(ks[3], (D_MODEL, D_MODEL), jnp.float32) * 0.02, 'b_out': jnp.zeros((D_MODEL,), jnp.float32), 'Wgate': jax.random.normal(ks[4], (D_MODEL, D_MODEL), jnp.float32) * 0.02, 'b_gate': jnp.zeros((D_MODEL,), jnp.float32), 'gamma': jnp.ones((D_MODEL,), jnp.float32), 'beta': jnp.zeros((D_MODEL,), jnp.float32)}
    _L1_xattn_all = _L1_xattn_setup()
    _L1_xattn_in = {k: v for k, v in _L1_xattn_all.items() if k in ('Wqkv', 'Wout', 'b_out', 'Wgate', 'b_gate', 'gamma', 'beta')}
    del _L1_xattn_all

    def _L1_ffn_setup():
        import jax, jax.numpy as jnp
        import numpy as np
        D_MODEL = 128
        FF = 512
        E = 8
        TOP_K = 2
        CAP_FACTOR = 1.25
        B, T = (4, 256)

        def _moe_forward(x, gate_w, gate_b, w1, b1, w2, b2):
            Bb, Tt, d = x.shape
            S = Bb * Tt
            C = int(CAP_FACTOR * S / E)
            xf = x.reshape(S, d)
            logits = xf @ gate_w + gate_b
            probs = jax.nn.softmax(logits, axis=1)
            topk_p, topk_i = jax.lax.top_k(probs, TOP_K)
            topk_pn = topk_p / jnp.sum(topk_p, axis=1, keepdims=True)
            rows = jnp.arange(S)
            w_te = jnp.zeros((S, E), xf.dtype).at[rows[:, None], topk_i].set(topk_pn)
            mask = jnp.zeros((S, E), bool).at[rows[:, None], topk_i].set(True)
            rank = jnp.cumsum(mask.astype(jnp.int32), axis=0)
            slot = jnp.where(mask & (rank <= C), rank - 1, C)
            e_grid = jnp.broadcast_to(jnp.arange(E), (S, E))
            t_grid = jnp.broadcast_to(rows[:, None], (S, E))
            buf = jnp.full((E, C + 1), S, jnp.int32).at[e_grid, slot].set(t_grid)
            idx = buf[:, :C]
            valid = idx < S
            x_pad = jnp.concatenate([xf, jnp.zeros((1, d), xf.dtype)], axis=0)
            xin = x_pad[idx]
            h = jax.nn.relu(jnp.einsum('ecd,edh->ech', xin, w1) + b1[:, None, :])
            out = jnp.einsum('ech,ehd->ecd', h, w2) + b2[:, None, :]
            w_pad = jnp.concatenate([w_te, jnp.zeros((1, E), xf.dtype)], axis=0)
            tok_w = w_pad[idx, jnp.arange(E)[:, None]]
            out = out * jnp.where(valid, tok_w, 0.0)[:, :, None]
            final = jnp.zeros((S + 1, d), xf.dtype).at[idx.reshape(-1)].add(out.reshape(-1, d))[:S]
            return final.reshape(Bb, Tt, d)
        key = jax.random.key(seed)
        ks = jax.random.split(key, 7)
        s = 0.02
        return {'x': jax.random.normal(ks[0], (B, T, D_MODEL), jnp.float32), 'gate_w': jax.random.normal(ks[1], (D_MODEL, E), jnp.float32) * s, 'gate_b': jnp.zeros((E,), jnp.float32), 'w1': jax.random.normal(ks[2], (E, D_MODEL, FF), jnp.float32) * s, 'b1': jnp.zeros((E, FF), jnp.float32), 'w2': jax.random.normal(ks[3], (E, FF, D_MODEL), jnp.float32) * s, 'b2': jnp.zeros((E, D_MODEL), jnp.float32)}
    _L1_ffn_all = _L1_ffn_setup()
    _L1_ffn_in = {k: v for k, v in _L1_ffn_all.items() if k in ('gate_w', 'gate_b', 'w1', 'b1', 'w2', 'b2')}
    del _L1_ffn_all
    return {'x': x, 'ctx_1024': ctx_1024, 'itok_BxSx64_0_2047': itok_BxSx64_0_2047, 'g_xattn': g_xattn, 'g_ffn': g_ffn, 'L0_xattn_W_q': _L0_xattn_in['W_q'], 'L0_xattn_W_kv_down': _L0_xattn_in['W_kv_down'], 'L0_xattn_W_kv_up': _L0_xattn_in['W_kv_up'], 'L0_xattn_W_out': _L0_xattn_in['W_out'], 'L0_ffn_ln_gamma': _L0_ffn_in['ln_gamma'], 'L0_ffn_ln_beta': _L0_ffn_in['ln_beta'], 'L0_ffn_router_w': _L0_ffn_in['router_w'], 'L0_ffn_gate_up_w': _L0_ffn_in['gate_up_w'], 'L0_ffn_down_w': _L0_ffn_in['down_w'], 'L0_ffn_shared_gate_up_w': _L0_ffn_in['shared_gate_up_w'], 'L0_ffn_shared_down_w': _L0_ffn_in['shared_down_w'], 'L1_xattn_Wqkv': _L1_xattn_in['Wqkv'], 'L1_xattn_Wout': _L1_xattn_in['Wout'], 'L1_xattn_b_out': _L1_xattn_in['b_out'], 'L1_xattn_Wgate': _L1_xattn_in['Wgate'], 'L1_xattn_b_gate': _L1_xattn_in['b_gate'], 'L1_xattn_gamma': _L1_xattn_in['gamma'], 'L1_xattn_beta': _L1_xattn_in['beta'], 'L1_ffn_gate_w': _L1_ffn_in['gate_w'], 'L1_ffn_gate_b': _L1_ffn_in['gate_b'], 'L1_ffn_w1': _L1_ffn_in['w1'], 'L1_ffn_b1': _L1_ffn_in['b1'], 'L1_ffn_w2': _L1_ffn_in['w2'], 'L1_ffn_b2': _L1_ffn_in['b2']}

def reference(x, ctx_1024, itok_BxSx64_0_2047, g_xattn, g_ffn, L0_xattn_W_q, L0_xattn_W_kv_down, L0_xattn_W_kv_up, L0_xattn_W_out, L0_ffn_ln_gamma, L0_ffn_ln_beta, L0_ffn_router_w, L0_ffn_gate_up_w, L0_ffn_down_w, L0_ffn_shared_gate_up_w, L0_ffn_shared_down_w, L1_xattn_Wqkv, L1_xattn_Wout, L1_xattn_b_out, L1_xattn_Wgate, L1_xattn_b_gate, L1_xattn_gamma, L1_xattn_beta, L1_ffn_gate_w, L1_ffn_gate_b, L1_ffn_w1, L1_ffn_b1, L1_ffn_w2, L1_ffn_b2):
    import jax
    import jax.numpy as jnp

    def _L0_xattn_ref(x_q, x_kv, indices, W_q, W_kv_down, W_kv_up, W_out):
        import jax, jax.numpy as jnp
        import numpy as np
        B, NQ, NKV, K = (2, 128, 256, 64)
        D, H, LAT = (128, 16, 128)
        HD = D // H
        SCALE = 1.0 / np.sqrt(HD)
        b, nq, d = x_q.shape
        q = (x_q @ W_q.T).reshape(b, nq, H, HD)
        c_kv = x_kv @ W_kv_down.T
        c_sel = c_kv[jnp.arange(b)[:, None, None], indices]
        kv = (c_sel @ W_kv_up.T).reshape(b, nq, K, 2, H, HD)
        k = kv[:, :, :, 0]
        v = kv[:, :, :, 1]
        scores = jnp.einsum('bqhd,bqkhd->bqkh', q, k) * SCALE
        attn = jax.nn.softmax(scores, axis=2)
        out = jnp.einsum('bqkh,bqkhd->bqhd', attn, v).reshape(b, nq, d)
        return out @ W_out.T

    def _L0_ffn_ref(x, ln_gamma, ln_beta, router_w, gate_up_w, down_w, shared_gate_up_w, shared_down_w):
        import jax, jax.numpy as jnp
        import numpy as np
        LN_EPS = 1e-05

        def _swiglu(h, w_gate_up, w_down):
            gu = h @ w_gate_up.T
            gate, up = jnp.split(gu, 2, axis=-1)
            return jax.nn.silu(gate) * up @ w_down.T
        B, S, D = x.shape
        E = router_w.shape[0]
        top_k = 2
        xt = x.reshape(-1, D)
        mu = jnp.mean(xt, axis=-1, keepdims=True)
        var = jnp.mean(jnp.square(xt - mu), axis=-1, keepdims=True)
        normed = (xt - mu) * jax.lax.rsqrt(var + LN_EPS) * ln_gamma + ln_beta
        logits = normed.astype(jnp.float32) @ router_w.T
        probs = jax.nn.softmax(logits, axis=-1)
        top_v, top_i = jax.lax.top_k(probs, top_k)
        gates = jax.nn.softmax(top_v, axis=-1)
        comb = jnp.sum(jax.nn.one_hot(top_i, E, dtype=gates.dtype) * gates[..., None], axis=1)
        out = jnp.zeros_like(normed)
        for e in range(E):
            y = _swiglu(normed, gate_up_w[e], down_w[e])
            out = out + comb[:, e, None] * y
        out = out + _swiglu(normed, shared_gate_up_w, shared_down_w)
        return out.reshape(B, S, D)

    def _L1_xattn_ref(decoder_hidden, encoder_output, Wqkv, Wout, b_out, Wgate, b_gate, gamma, beta):
        import jax, jax.numpy as jnp
        import numpy as np
        D_MODEL = 128
        NUM_HEADS = 16
        HEAD_DIM = D_MODEL // NUM_HEADS
        SCALE = HEAD_DIM ** (-0.5)
        BIAS_LEN = 128
        ROPE_BASE = 10000.0
        LN_EPS = 1e-05

        def _layernorm(x, gamma, beta):
            mu = jnp.mean(x, axis=-1, keepdims=True)
            var = jnp.mean(jnp.square(x - mu), axis=-1, keepdims=True)
            return (x - mu) * jax.lax.rsqrt(var + LN_EPS) * gamma + beta

        def _rope(x, cos, sin):
            half = HEAD_DIM // 2
            c = cos[None, None, :, :]
            s = sin[None, None, :, :]
            x_even, x_odd = (x[..., :half], x[..., half:])
            return jnp.concatenate([x_even * c - x_odd * s, x_even * s + x_odd * c], axis=-1)

        def _temporal_bias(L_q, L_kv):
            pos = jnp.arange(BIAS_LEN, dtype=jnp.float32)
            dist = jnp.abs(pos[None, :] - pos[:, None])
            bias = jnp.exp(-dist * 0.1) - dist * 0.05
            if L_q <= BIAS_LEN and L_kv <= BIAS_LEN:
                return bias[:L_q, :L_kv]
            return jax.image.resize(bias, (L_q, L_kv), method='bilinear')
        B, L_q, _ = decoder_hidden.shape
        L_kv = encoder_output.shape[1]
        residual = decoder_hidden
        q_in = _layernorm(decoder_hidden, gamma, beta)
        kv_in = _layernorm(encoder_output, gamma, beta)
        q = q_in @ Wqkv[:D_MODEL].T
        k = kv_in @ Wqkv[D_MODEL:2 * D_MODEL].T
        v = kv_in @ Wqkv[2 * D_MODEL:].T
        q = q.reshape(B, L_q, NUM_HEADS, HEAD_DIM).transpose(0, 2, 1, 3)
        k = k.reshape(B, L_kv, NUM_HEADS, HEAD_DIM).transpose(0, 2, 1, 3)
        v = v.reshape(B, L_kv, NUM_HEADS, HEAD_DIM).transpose(0, 2, 1, 3)
        L = max(L_q, L_kv)
        inv_freq = 1.0 / ROPE_BASE ** (jnp.arange(0, HEAD_DIM, 2, dtype=jnp.float32) / HEAD_DIM)
        freqs = jnp.arange(L, dtype=jnp.float32)[:, None] * inv_freq[None, :]
        cos, sin = (jnp.cos(freqs), jnp.sin(freqs))
        q = _rope(q, cos[:L_q], sin[:L_q])
        k = _rope(k, cos[:L_kv], sin[:L_kv])
        scores = jnp.einsum('bhqd,bhkd->bhqk', q, k) * SCALE
        scores = scores + _temporal_bias(L_q, L_kv)[None, None, :, :]
        attn = jax.nn.softmax(scores, axis=-1)
        attended = jnp.einsum('bhqk,bhkd->bhqd', attn, v)
        attended = attended.transpose(0, 2, 1, 3).reshape(B, L_q, D_MODEL)
        attended = attended @ Wout.T + b_out
        gate = jax.nn.sigmoid(attended @ Wgate.T + b_gate)
        output = gate * attended + (1.0 - gate) * residual
        return output

    def _L1_ffn_ref(x, gate_w, gate_b, w1, b1, w2, b2):
        import jax, jax.numpy as jnp
        import numpy as np
        D_MODEL = 128
        FF = 512
        E = 8
        TOP_K = 2
        CAP_FACTOR = 1.25
        B, T = (4, 256)

        def _moe_forward(x, gate_w, gate_b, w1, b1, w2, b2):
            Bb, Tt, d = x.shape
            S = Bb * Tt
            C = int(CAP_FACTOR * S / E)
            xf = x.reshape(S, d)
            logits = xf @ gate_w + gate_b
            probs = jax.nn.softmax(logits, axis=1)
            topk_p, topk_i = jax.lax.top_k(probs, TOP_K)
            topk_pn = topk_p / jnp.sum(topk_p, axis=1, keepdims=True)
            rows = jnp.arange(S)
            w_te = jnp.zeros((S, E), xf.dtype).at[rows[:, None], topk_i].set(topk_pn)
            mask = jnp.zeros((S, E), bool).at[rows[:, None], topk_i].set(True)
            rank = jnp.cumsum(mask.astype(jnp.int32), axis=0)
            slot = jnp.where(mask & (rank <= C), rank - 1, C)
            e_grid = jnp.broadcast_to(jnp.arange(E), (S, E))
            t_grid = jnp.broadcast_to(rows[:, None], (S, E))
            buf = jnp.full((E, C + 1), S, jnp.int32).at[e_grid, slot].set(t_grid)
            idx = buf[:, :C]
            valid = idx < S
            x_pad = jnp.concatenate([xf, jnp.zeros((1, d), xf.dtype)], axis=0)
            xin = x_pad[idx]
            h = jax.nn.relu(jnp.einsum('ecd,edh->ech', xin, w1) + b1[:, None, :])
            out = jnp.einsum('ech,ehd->ecd', h, w2) + b2[:, None, :]
            w_pad = jnp.concatenate([w_te, jnp.zeros((1, E), xf.dtype)], axis=0)
            tok_w = w_pad[idx, jnp.arange(E)[:, None]]
            out = out * jnp.where(valid, tok_w, 0.0)[:, :, None]
            final = jnp.zeros((S + 1, d), xf.dtype).at[idx.reshape(-1)].add(out.reshape(-1, d))[:S]
            return final.reshape(Bb, Tt, d)
        return _moe_forward(x, gate_w, gate_b, w1, b1, w2, b2)
    x = x + jnp.tanh(g_xattn[0]) * _L0_xattn_ref(_layernorm(x, axis=-1), ctx_1024, itok_BxSx64_0_2047, L0_xattn_W_q, L0_xattn_W_kv_down, L0_xattn_W_kv_up, L0_xattn_W_out)
    x = x + jnp.tanh(g_ffn[0]) * _L0_ffn_ref(_layernorm(x, axis=-1), L0_ffn_ln_gamma, L0_ffn_ln_beta, L0_ffn_router_w, L0_ffn_gate_up_w, L0_ffn_down_w, L0_ffn_shared_gate_up_w, L0_ffn_shared_down_w)
    x = x + jnp.tanh(g_xattn[1]) * _L1_xattn_ref(_layernorm(x, axis=-1), ctx_1024, L1_xattn_Wqkv, L1_xattn_Wout, L1_xattn_b_out, L1_xattn_Wgate, L1_xattn_b_gate, L1_xattn_gamma, L1_xattn_beta)
    x = x + jnp.tanh(g_ffn[1]) * _L1_ffn_ref(_layernorm(x, axis=-1), L1_ffn_gate_w, L1_ffn_gate_b, L1_ffn_w1, L1_ffn_b1, L1_ffn_w2, L1_ffn_b2)
    return x

_drawn_inputs = setup_inputs


def setup_inputs(seed=0):
    import zlib

    import numpy as np

    out = dict(_drawn_inputs(seed))
    spreads = {'g_ffn': (-1.0, 0.6),
     'L0_ffn_ln_gamma': (1.0, 0.2),
     'L0_ffn_ln_beta': (0.0, 0.1),
     'L1_xattn_b_out': (0.0, 0.1),
     'L1_xattn_b_gate': (0.0, 0.1),
     'L1_xattn_gamma': (1.0, 0.6),
     'L1_xattn_beta': (0.0, 0.8),
     'L1_ffn_gate_b': (0.0, 0.1),
     'L1_ffn_b1': (0.0, 0.453),
     'L1_ffn_b2': (0.0, 0.1)}
    factors = {'L1_xattn_Wqkv': 2.882, 'L1_xattn_Wout': 2.831, 'L1_xattn_Wgate': 5.22}
    for name, (base, spread) in spreads.items():
        noise = np.random.default_rng([zlib.crc32(name.encode()), seed]).standard_normal(out[name].shape)
        drawn = base * np.exp(spread * noise) if base else spread * noise
        out[name] = jnp.asarray(drawn.astype(out[name].dtype))
    for name, factor in factors.items():
        out[name] = (out[name] * factor).astype(out[name].dtype)
    return out
```

```python
import concourse.bass as bass
from concourse import mybir
from contextlib import ExitStack
import numpy as np

fp32, bf16, fp16, i32 = mybir.dt.float32, mybir.dt.bfloat16, mybir.dt.float16, mybir.dt.int32
ALU = mybir.AluOpType
ACT = mybir.ActivationFunctionType
AX = mybir.AxisListType

P = 128
D = 128
B, LQ, NK = 4, 512, 154
T = B * LQ // P
TB = LQ // P
NR = 32
NP = P + NR
H, HD = 16, 8
SCALE = HD ** -0.5
KSEL = 64
E = 8
FF0, FF1 = 384, 512
F0, F1 = FF0 // P, FF1 // P
CAP = int(1.25 * B * LQ / E)
EPS = 1e-5
BIG = 60000.0
SL = 6
Q_PART = (0, 0, 0, 1, 1, 2)
K_PART = (0, 1, 2, 0, 1, 0)
MROW = SL * HD
KCON = MROW + 1
GQ = 4
NLO = 32
NHI = 5
NCH = 256

WQ0, WDOWN, WUPK, WUPV, WOUT0, WQ1, WK1, WV1, WOUT1, WGATE, SG, SU, SD, SMALL, EXP0 = range(15)
B1C, G0C, BE0C, G1C, BE1C, RTC = 0, E * F1, E * F1 + 1, E * F1 + 2, E * F1 + 3, E * F1 + 4
NSMALL = RTC + E
NBLK = EXP0 + 9 * E


class Ring:

    def __init__(self, slots, full, free):
        self.slots, self.full, self.free, self.made, self.used = slots, full, free, 0, 0

    def next_free(self, pe):
        n = len(self.slots)
        if self.made >= n:
            pe.wait_ge(self.free, self.made - n + 1)
        self.made += 1
        return self.slots[(self.made - 1) % n]

    def next_full(self, eng):
        self.used += 1
        eng.wait_ge(self.full, self.used)
        return self.slots[(self.used - 1) % len(self.slots)]


class Chain:

    def __init__(self, eng, step):
        self.eng, self.step, self.count, self.last = eng, step, {}, None

    def do(self, ins, sem=None):
        sem = self.step if sem is None else sem
        k = id(sem)
        self.count[k] = self.count.get(k, 0) + 1
        ins.then_inc(sem, 1)
        self.last = (sem, self.count[k])

    def own(self):
        self.eng.wait_ge(*self.last)


def build(nc, ins, out, stop=4):
    ctx = ExitStack()
    with ctx:
        def sb(name, shape, dt=fp32):
            return ctx.enter_context(nc.sbuf_tensor(name, shape, dt))

        def pb(name, n=512):
            return ctx.enter_context(nc.psum_tensor(name, [P, n], fp32))

        sems = {}
        at = {}

        def sem(name):
            if name not in sems:
                sems[name] = ctx.enter_context(nc.semaphore("s_" + name))
            return sems[name]

        X = sb("X", [P, T, D])
        XN = sb("XN", [P, T, D])
        NT = sb("NT", [P, B, LQ])
        NWB = sb("NWB", [P, 27 * P])
        NW = NWB[:, :].rearrange("p (s k n) -> p s k n", s=3, k=9)
        SGM = NWB[:, 0:1024].rearrange("p (s q) -> p s q", s=2)
        XM = NWB[:, 1024:1536].rearrange("p (t d) -> p t d", t=TB)
        AC = NWB[:, 1536:2048].rearrange("p (t d) -> p t d", t=TB)
        O = NWB[:, 2048:2560].rearrange("p (t h d) -> p t h d", t=TB, h=H)
        OT = NWB[:, 2560:3072]
        MX = NWB[:, 3072:3136].rearrange("p (t h) -> p t h", t=TB)
        LG = NWB[:, 3136:3264].rearrange("p (t e) -> p t e", t=T)
        CB = NWB[:, 3264:3392].rearrange("p (t e) -> p t e", t=T)
        WT = sb("WT", [P, NBLK, P])
        W1 = WT[:, EXP0:EXP0 + E * F1, :].rearrange("p (e k) n -> p e (k n)", e=E)
        W2 = WT[:, EXP0 + E * F1:EXP0 + 2 * E * F1, :].rearrange("p (e k) n -> p e k n", e=E)
        WR = sb("WR", [P, 2, P])
        QSB = sb("QSB", [P, 4096])
        QS = QSB[:, :].bitcast(bf16).rearrange("p (i j q) -> p i j q", i=2, j=H // 2)
        KS = sb("KS", [P, 2, H // 2, B * NP], bf16)
        V = sb("V", [P, 2, B * H, HD + 1])
        VR = sb("VR", [P, 2, B, 4, 4, HD + 1])
        LBB = sb("LBB", [P, 4096])
        LB = LBB[:, :].bitcast(fp16).rearrange("p (s q) -> p s q", s=4)
        BIAS = sb("BIAS", [P, 4, LQ], fp16)
        BG = sb("BG", [P, 10240])
        ONEH = BG[:, 0:4096].bitcast(bf16).rearrange("p (g b q) -> p g b q", b=NLO, q=GQ)
        CNT = BG[:, 4096:9216].bitcast(bf16).rearrange("p (g c) -> p g c", c=NHI * GQ)
        PM = BG[:, 0:8192].rearrange("p (h q) -> p h q", h=H)
        PR = BG[:, 8192:10240].rearrange("p (g q) -> p g q", g=4)
        HB = BG[:, 0:4096].rearrange("p (s q) -> p s q", s=8)
        ONEA = LBB[:, 0:640].bitcast(bf16).rearrange("p (a q) -> p a q", a=NHI)
        DIG = LBB[:, 1024:2048].bitcast(bf16).rearrange("p (i q) -> p i q", i=2)
        DIGT = LBB[:, 2048:3072].bitcast(bf16).rearrange("p (i q) -> p i q", i=2)
        IDX = NT[:, 0:2, :].rearrange("p b q -> p (b q)").bitcast(i32)
        IDW = NT[:, 2:4, :].rearrange("p b q -> p (b q)").bitcast(i32)
        CTX = QSB[:, 0:1024].rearrange("p (m b d) -> p m b d", m=2, b=B)
        CTN = QSB[:, 1024:2048].rearrange("p (m b d) -> p m b d", m=2, b=B)
        CXT = QSB[:, 2048:2048 + B * NP]
        CLT = QSB[:, 2048 + B * NP:2048 + 2 * B * NP]
        PRT = sb("PRT", [P, 3, B * NP], bf16)
        TF = sb("TF", [P, 2, B * NP])
        COS = sb("COS", [P, LQ])
        SIN = sb("SIN", [P, LQ])
        ID32 = sb("ID32", [P, P])
        ID16 = sb("ID16", [P, P], fp16)
        IDB = sb("IDB", [P, P], bf16)
        TRI = sb("TRI", [P, P], bf16)
        ONB = sb("ONB", [P, P], bf16)
        ONF = sb("ONF", [1, P])
        KEY = sb("KEY", [P, T, E])
        ROW = sb("ROW", [E + 2, P])
        GBR = sb("GBR", [1, E])
        GW = sb("GW", [P, E])
        TG = sb("TG", [P, 4])
        ST = sb("ST", [P, 8, 6])
        MV = sb("MV", [P, 8, 2])
        RS = sb("RS", [P, 8])
        EPT = sb("EPT", [P, 8])
        NHF = sb("NHF", [P, 8])
        MS = sb("MS", [H, LQ], bf16)
        RC = sb("RC", [P, TB, H])
        RT = sb("RT", [P, 5, T, E])
        R1 = sb("R1", [P, 4, T])
        MK = sb("MK", [P, T, E], bf16)

        A = ctx.enter_context(nc.psum_tensor("A", [P, 4, 512], fp32))
        S = [pb(f"PS{i}") for i in range(2)]
        R = [pb(f"PR{i}") for i in range(2)]
        rS = Ring([s[:, :] for s in S], sem("S_full"), sem("S_free"))
        rR = Ring([r[:, :] for r in R], sem("R_full"), sem("R_free"))
        rA = Ring([A[:, 0:2, :], A[:, 2:4, :]], sem("A_full"), sem("A_free"))
        rE = Ring([A[:, 0, :], A[:, 2, :]], sem("E_full"), sem("E_free"))
        rO = Ring([A[:, 1, :], A[:, 3, :]], sem("O_full"), sem("O_free"))

        kd = [nc.dram_tensor(f"kd{l}", [3, P, B * NP], bf16).ap() for l in range(2)]
        qd = [nc.dram_tensor(f"qd{i}", [3, P, LQ], bf16).ap() for i in range(2 * B)]

        DVE_W = [g for g in range(29) if g % 2]
        GROUPS = [(3 * g, min(3 * g + 3, EXP0)) for g in range(5)] + \
                 [(EXP0 + 3 * g, EXP0 + 3 * g + 3) for g in range(24)]

        def staged(blk):
            if blk < EXP0:
                return NW[:, blk // 9, blk % 9, :]
            e, j = divmod(blk - EXP0, 9)
            return NW[:, (2 + e) % 3, j, :]

        def cnt_group(i):
            ch, r = divmod(i, 2 * NCH // 64)
            half, q = divmod(r, NCH // 64)
            return half * 256 + ch * (NCH // GQ) + q * 16

        def ctx_norm(dve, c, v, nstat):
            for t in range(8):
                rows = P if t < 4 else NR
                c.do(v.bn_stats(ST[0:rows, t, :], CTX[0:rows, t // 4, t % 4, :]))
            c.do(v.memset(MV[:, 4:8, :], 0.0)); c.own()
            for t in range(8):
                rows = P if t < 4 else NR
                c.do(v.bn_aggr(MV[0:rows, t, :], ST[0:rows, t, :]), sem("stats") if t == 7 else None)
            nstat[0] += 1
            dve.wait_ge(sem("rstd"), nstat[0])
            for t in range(8):
                rows = P if t < 4 else NR
                c.do(v.tensor_scalar(CTN[0:rows, t // 4, t % 4, :], CTX[0:rows, t // 4, t % 4, :],
                                     MV[0:rows, t, 0:1], RS[0:rows, t:t + 1], ALU.subtract, ALU.mult),
                     sem("ctn") if t == 7 else None)

        block = ctx.enter_context(nc.Block())

        @block.tensor
        def _(pe):
            mm, tr = nc.tensor.matmul, nc.tensor.transpose

            pe.wait_ge(sem("idb"), 16)
            pe.wait_ge(sem("digits"), 2)
            for i in range(2):
                z = rR.next_free(pe).bitcast(bf16)
                for t in range(8):
                    last = tr(z[:, P * t:P * t + P], DIG[:, i, P * t:P * t + P], IDB[:, :])
                last.then_inc(rR.full, 1)

            def weights(groups, first):
                for g, (lo, hi) in enumerate(groups, first):
                    r = rR if g in DVE_W else rS
                    z = r.next_free(pe)
                    for k in range(lo, hi):
                        last = tr(z[:, P * (k - lo):P * (k - lo) + P], staged(k), ID32[:, :])
                    last.then_inc(r.full, 1)
                    at["weights", g] = (r.full, r.made)
            pe.wait_ge(sem("id32"), 16)
            pe.wait_ge(sem("wmisc"), 16 * 19)
            weights(GROUPS[:5], 0)

            def transposed(src, nbanks=2):
                for i in range(2):
                    z = rR.next_free(pe)
                    for b in range(2):
                        tr(z[:, NP * b:NP * b + P], src[:, 0, 2 * i + b, :], ID32[:, :])
                        last = tr(z[:, NP * b + P:NP * b + NP], src[0:NR, 1, 2 * i + b, :], ID32[0:NR, 0:NR])
                    last.then_inc(rR.full, 1)

            def evacuated():
                pe.wait_ge(rR.free, rR.made)

            def project(lhsT, src):
                for i in range(2):
                    z = rR.next_free(pe)
                    mm(z[:, 0:2 * NP], lhsT, src[:, 2 * NP * i:2 * NP * i + 2 * NP], start=True, stop=True).then_inc(rR.full, 1)

            def values(src, wv):
                z = rR.next_free(pe)
                for b in range(B):
                    last = mm(z[:, P * b:P * b + P], src[:, NP * b:NP * b + P], wv, start=True, stop=True)
                last.then_inc(rR.full, 1)
                z = rR.next_free(pe)
                for j in range(4):
                    for b in range(B):
                        last = mm(z[32 * j:32 * j + 32, P * b:P * b + P], src[:, NP * b + P:NP * b + NP], wv, start=True, stop=True)
                last.then_inc(rR.full, 1)

            pe.wait_ge(sem("ctx"), 32)
            transposed(CTX)
            pe.wait_ge(rS.free, 3)
            evacuated()
            project(WT[:, WDOWN, :], CXT)
            evacuated()
            project(WT[:, WUPK, :], CLT)
            values(CLT, WT[:, WUPV, :])
            pe.wait_ge(sem("ctn"), 1)
            transposed(CTN)
            evacuated()
            pe.wait_ge(sem("rotated"), 2)
            for i in range(2):
                for w in (WT[:, WK1, :], WR[:, 1, :]):
                    z = rR.next_free(pe)
                    mm(z[:, 0:2 * NP], w, CXT[:, 2 * NP * i:2 * NP * i + 2 * NP], start=True, stop=True).then_inc(rR.full, 1)
            values(CXT, WT[:, WV1, :])

            for e in range(E):
                z_ = (2 + e) % 3
                pe.wait_ge(sem("wexp%d" % z_), 32 * (e // 3 + 1))
                weights(GROUPS[5 + 3 * e:8 + 3 * e], 5 + 3 * e)

            for ch in range(1024 // NCH):
                pe.wait_ge(sem("onehot"), ch + 1)
                for i in range(2 * NCH // 64):
                    half, q = divmod(i, NCH // 64)
                    r = rR if i % 2 else rS
                    z = r.next_free(pe)
                    p0 = 64 * half
                    for g in range(16):
                        t0 = 64 * q + GQ * g
                        last = mm(z[:, 20 * g:20 * g + 20], ONEH[p0:p0 + 64, t0 // GQ, :, :].rearrange("p b q -> p (b q)"), ONEA[p0:p0 + 64, :, t0:t0 + GQ],
                                  start=True, stop=True)
                    last.then_inc(r.full, 1)
            pe.wait_ge(rR.free, rR.made)
            pe.wait_ge(rS.free, rS.made)
            for b in range(B):
                z0 = rR.next_free(pe)
                for r in range(GQ):
                    sel = IDB[:, r:P:GQ]
                    for a in range(4):
                        last = mm(z0[32 * a:32 * a + 32, P * r:P * r + P], sel, CNT[:, P * b:P * b + P, GQ * a + r], start=True, stop=True)
                last.then_inc(rR.full, 1)
                z1 = rR.next_free(pe)
                for r in range(GQ):
                    sel = IDB[:, r:P:GQ]
                    for a in range(4):
                        last = mm(z1[32 * a:32 * a + 32, P * r:P * r + P], sel, CNT[:, P * b:P * b + P, GQ * 4 + r], start=True, stop=True)
                last.then_inc(rR.full, 1)

            xn = [0]

            def tokens_t(s, b):
                xn[0] += 1
                pe.wait_ge(sem("xn"), xn[0])
                z = rR.next_free(pe)
                for t in range(TB):
                    src = XM[:, t, :] if s in (1, 2) else XN[:, TB * b + t, :]
                    last = tr(z[:, P * t:P * t + P], src, ID32[:, :])
                last.then_inc(rR.full, 1)
                evacuated()

            def q_proj(l, b):
                for w in ((WT[:, WQ0, :],) if l == 0 else (WT[:, WQ1, :], WR[:, 0, :])):
                    z = rR.next_free(pe)
                    mm(z, w, NT[:, b, :], start=True, stop=True).then_inc(rR.full, 1)

            def pick(r):
                return ID32[0:E + 2, r:r + 1].broadcast_to([E + 2, P])

            def twice(ap):
                return ap.rearrange("p (a n) -> p a n", a=1).broadcast_to([ap.shape[0], 2, ap.shape[1]])

            def nat(l, b, i):
                t, g = divmod(i, 4)
                if i == 0:
                    pe.wait_ge(sem("spread_q%d" % ((l * B + b) % 2)), 16 * 2 * SL * ((l * B + b) // 2 + 1))
                z = rA.next_free(pe)
                qs, ks = QS[:, (l * B + b) % 2, :, P * t:P * t + P], KS[:, l, :, NP * b:NP * b + NK]
                for a in range(2):
                    zz = z[:, a, :].rearrange("p (h n) -> p h n", h=2)
                    if l == 0:
                        q0 = LQ * b + P * t
                        mm(zz[:, :, P:NK], LB[0:NR, 2, q0:q0 + P], twice(ID16[0:NR, 0:NK - P]), start=True, stop=False, skip_group_check=True)
                        mm(zz[:, :, 0:P], LB[:, 0, q0:q0 + P], twice(ID16[:, :]), start=False, stop=False, skip_group_check=True)
                    p0 = 64 * a
                    for h in range(2):
                        last = mm(zz[:, h, 0:NK], qs[p0:p0 + MROW, 2 * g + h, :], ks[p0:p0 + MROW, 2 * g + h, :],
                                  start=(l == 1 and h == 0), stop=(h == 1), skip_group_check=True)
                last.then_inc(rA.full, 1)

            def m_tr(l, b):
                pe.wait_ge(rA.free, rA.made)
                z = rR.next_free(pe)
                for t in range(TB):
                    last = tr(z[0:H, P * t:P * t + P], MX[:, t, :], ID32[:, :])
                last.then_inc(rR.full, 1)
                at["maxima", l * B + b] = rR.made

            def scores(l, b, h):
                i = l * B + b
                if h == 0:
                    pe.wait_ge(sem("m_in"), 32 * (i + 1))
                qs, ks = QS[:, i % 2, :, :], KS[:, l, :, :]
                bm = LB[:, :, LQ * b:LQ * b + LQ] if l == 0 else BIAS[:, :, :]
                p0 = 64 * (h % 2)
                z = rS.next_free(pe)
                mm(z, ks[p0:p0 + KCON, h // 2, NP * b:NP * b + P], qs[p0:p0 + KCON, h // 2, :], start=True, stop=False)
                mm(z, ID16[:, :], bm[:, 0, :], start=False, stop=False)
                mm(z, ID16[:, :], bm[:, 1, :], start=False, stop=True).then_inc(rS.full, 1)
                if h % 4 == 3:
                    z = rS.next_free(pe)
                    g = h // 4
                    p0 = 64 * (g % 2)
                    for j in range(4):
                        pair = 4 * (g // 2) + j
                        mm(z[32 * j:32 * j + 32, :], ks[p0:p0 + KCON, pair, NP * b + P:NP * b + NP], qs[p0:p0 + KCON, pair, :],
                           start=True, stop=False, skip_group_check=True)
                    mm(z, ID16[:, :], bm[:, 2, :], start=False, stop=False, skip_group_check=True)
                    mm(z, ID16[:, :], bm[:, 3, :], start=False, stop=True, skip_group_check=True).then_inc(rS.full, 1)
                    at["scores", i] = (rS.full, rS.made)

            def weighted(l, b):
                pe.wait_ge(rS.free, rS.made)
                for t in range(TB):
                    z = rR.next_free(pe)
                    q = slice(P * t, P * t + P)
                    for g in range(4):
                        zg = z[:, 72 * (g // 2):72 * (g // 2) + 72].rearrange("p (j u d) -> p u j d", u=2, d=HD + 1)[:, g % 2]
                        mm(zg, PR[:, g, q], VR[:, l, b, g, :, :],
                           start=(g == 0), stop=False, skip_group_check=True)
                    for h in range(H):
                        last = mm(z[:, 9 * h:9 * h + 9], PM[:, h, q], V[:, l, H * b + h, :], start=False, stop=(h == H - 1), skip_group_check=True)
                    last.then_inc(rR.full, 1)
                at["weighted", l * B + b] = (rR.full, rR.made)

            def out_proj(l, b):
                evacuated()
                z = rR.next_free(pe)
                for t in range(TB):
                    last = tr(z[:, P * t:P * t + P], O[:, t, :, :].rearrange("p h d -> p (h d)"), ID32[:, :])
                last.then_inc(rR.full, 1)
                evacuated()
                z = rR.next_free(pe)
                for t in range(TB):
                    last = mm(z[:, P * t:P * t + P], OT[:, P * t:P * t + P], WT[:, WOUT0 if l == 0 else WOUT1, :], start=True, stop=(l == 0))
                    if l:
                        last = mm(z[:, P * t:P * t + P], pick(E), ROW[:, :], start=False, stop=True)
                last.then_inc(rR.full, 1)
                if l == 0:
                    return
                evacuated()
                z = rR.next_free(pe)
                for t in range(TB):
                    last = tr(z[:, P * t:P * t + P], SGM[:, 0, P * t:P * t + P], ID32[:, :])
                last.then_inc(rR.full, 1)
                evacuated()
                z = rR.next_free(pe)
                for t in range(TB):
                    mm(z[:, P * t:P * t + P], SGM[:, 1, P * t:P * t + P], WT[:, WGATE, :], start=True, stop=False)
                    last = mm(z[:, P * t:P * t + P], pick(E + 1), ROW[:, :], start=False, stop=True)
                last.then_inc(rR.full, 1)
                at["gate", b] = rR.made

            def attention(l):
                if l == 0:
                    pe.wait_ge(sem("consts"), 16 * 13)
                    pe.wait_ge(sem("lb"), B)
                    pe.wait_ge(sem("spread_k"), 16 * 2 * SL * 2)
                    pe.wait_ge(sem("ones"), 2)
                tokens_t(2 * l, 0)
                q_proj(l, 0)
                for i in range(16):
                    nat(l, 0, i)
                m_tr(l, 0)
                for b in range(B):
                    if b + 1 < B:
                        tokens_t(2 * l, b + 1)
                        q_proj(l, b + 1)
                    for i in range(16):
                        scores(l, b, i)
                        if b + 1 < B:
                            nat(l, b + 1, i)
                    if b + 1 < B:
                        m_tr(l, b + 1)
                    weighted(l, b)
                    out_proj(l, b)

            attention(0)
            if stop <= 1:
                return

            def router(l, b):
                z = rR.next_free(pe)
                for t in range(TB):
                    w = WT[:, SMALL, RTC:RTC + E] if l == 0 else GW[:, :]
                    last = mm(z[:, E * t:E * t + E], NT[:, b, P * t:P * t + P], w, start=True, stop=(l == 0))
                    if l:
                        last = mm(z[:, E * t:E * t + E], ONF[:, :], GBR[:, :], start=False, stop=True)
                last.then_inc(rR.full, 1)

            def ffn0():
                for b in range(B):
                    tokens_t(1, b)
                    router(0, b)
                hid = [rA.made]

                def down(b, e):
                    n = F0 if e < E else 1
                    hid[0] += n
                    pe.wait_ge(rA.free, hid[0])
                    z = rR.next_free(pe)
                    for t in range(TB):
                        for j in range(n):
                            w = WT[:, EXP0 + 9 * e + 6 + j, :] if e < E else WT[:, SD, :]
                            last = mm(z[:, P * t:P * t + P], HB[:, (b * (E + 1) + e) % 2 * 3 + j, P * t:P * t + P], w, start=(j == 0), stop=(j == n - 1))
                    last.then_inc(rR.full, 1)
                pend = None
                for b in range(B):
                    for e in range(E + 1):
                        for j in range(F0 if e < E else 1):
                            z = rA.next_free(pe)
                            g, u = (EXP0 + 9 * e + j, EXP0 + 9 * e + F0 + j) if e < E else (SG, SU)
                            mm(z[:, 0, :], WT[:, g, :], NT[:, b, :], start=True, stop=True)
                            mm(z[:, 1, :], WT[:, u, :], NT[:, b, :], start=True, stop=True).then_inc(rA.full, 1)
                            if j == 0 and pend:
                                down(*pend)
                        pend = (b, e)
                down(*pend)
                at["ffn0", 0] = (rR.full, rR.made)

            def ffn1():
                for b in range(B):
                    tokens_t(3, b)
                    router(1, b)
                pe.wait_ge(sem("mask"), 1)
                z = rR.next_free(pe)
                mk = MK[:, :, :]
                mm(z[:, 0:T * E], TRI[:, :], mk.rearrange("p t e -> p (t e)"), start=True, stop=False, skip_group_check=True)
                for t in range(T - 1):
                    n = T - 1 - t
                    last = mm(z[:, E * (t + 1):E * T].rearrange("p (t e) -> p t e", e=E), ONB[:, :], mk[:, t:t + 1, :].broadcast_to([P, n, E]),
                              start=False, stop=(t == T - 2), skip_group_check=True)
                last.then_inc(rR.full, 1)
                pe.wait_ge(sem("w12"), 16 * 2 * E)

                def down(b, e):
                    pe.wait_ge(rE.free, 2 * (b * E + e + 1))
                    pe.wait_ge(rO.free, 2 * (b * E + e + 1))
                    z = rR.next_free(pe)
                    for t in range(TB):
                        mm(z[:, P * t:P * t + P], pick(e), ROW[:, :], start=True, stop=False)
                        for j in range(F1):
                            last = mm(z[:, P * t:P * t + P], HB[:, (e % 2) * 4 + j, P * t:P * t + P], W2[:, e, j, :], start=False, stop=(j == F1 - 1))
                    last.then_inc(rR.full, 1)
                    at["down1", b * E + e] = (rR.full, rR.made)
                pend = None
                for b in range(B):
                    for e in range(E):
                        for j in range(F1):
                            r = rO if j % 2 else rE
                            z = r.next_free(pe)
                            mm(z, W1[:, e, P * j:P * j + P], NT[:, b, :], start=True, stop=True).then_inc(r.full, 1)
                            if j == 1 and pend:
                                down(*pend)
                        pend = (b, e)
                down(*pend)
            ffn0()
            if stop <= 2:
                return
            attention(1)
            if stop <= 3:
                return
            ffn1()

        @block.sync
        def _(sp):
            xin = ins["x"].rearrange("b (t p) d -> p (b t) d", p=P)
            sp.dma_start(IDX, ins["itok_BxSx64_0_2047"].rearrange("b (t p) k -> p (b t) k", p=P)
                         ).then_inc(sem("idx"), 16)
            sp.dma_start(IDB[:, :], ins["c_idb"].bitcast(bf16)).then_inc(sem("idb"), 16)
            sp.dma_start(ID32[:, :], ins["c_id32"]).then_inc(sem("id32"), 16)

            def w(blk, src, rows=P, at=0):
                return sp.dma_start(NW[at:at + rows, blk // 9, blk % 9, :], src).then_inc(sem("wmisc"), 16)
            w(WQ0, ins["L0_xattn_W_q"])
            w(WDOWN, ins["L0_xattn_W_kv_down"])
            up = ins["L0_xattn_W_kv_up"].rearrange("(k p) d -> p k d", p=P)
            w(WUPK, up[:, 0, :])
            w(WUPV, up[:, 1, :])
            w(WOUT0, ins["L0_xattn_W_out"])
            qkv = ins["L1_xattn_Wqkv"].rearrange("(k p) d -> p k d", p=P)
            for i in range(3):
                w(WQ1 + i, qkv[:, i, :])
            w(WOUT1, ins["L1_xattn_Wout"])
            w(WGATE, ins["L1_xattn_Wgate"])
            sgu = ins["L0_ffn_shared_gate_up_w"].rearrange("(k p) d -> p k d", p=P)
            w(SG, sgu[:, 0, :])
            w(SU, sgu[:, 1, :])
            w(SD, ins["L0_ffn_shared_down_w"])
            sp.wait_ge(sem("small_clear"), 1)
            w(SMALL, ins["L1_ffn_b1"].rearrange("e (k p) -> (e k) p", p=P), E * F1, B1C)
            for c, n in ((G0C, "L0_ffn_ln_gamma"), (BE0C, "L0_ffn_ln_beta"), (G1C, "L1_xattn_gamma"), (BE1C, "L1_xattn_beta")):
                w(SMALL, ins[n].rearrange("(a n) -> a n", a=1), 1, c)
            w(SMALL, ins["L0_ffn_router_w"], E, RTC)
            sp.wait_ge(sem("ctx_clear"), 1)
            sp.dma_start(CTX[:, 0, :, :], ins["ctx_1024"][:, 0:P, :].rearrange("b n d -> n b d")).then_inc(sem("ctx"), 16)
            sp.dma_start(CTX[0:NK - P, 1, :, :], ins["ctx_1024"][:, P:NK, :].rearrange("b n d -> n b d")).then_inc(sem("ctx"), 16)
            for b in range(B):
                sp.dma_start(X[:, TB * b:TB * b + TB, :], xin[:, TB * b:TB * b + TB, :]).then_inc(sem("x_in%d" % b), 16)
            sp.dma_start(ID16[:, :], ins["c_id16"]).then_inc(sem("consts"), 16)
            sp.dma_start(COS[:, :], ins["c_cos"]).then_inc(sem("consts"), 16)
            sp.dma_start(SIN[:, :], ins["c_sin"]).then_inc(sem("consts"), 16)
            sp.dma_start(TRI[:, :], ins["c_tri"].bitcast(bf16)).then_inc(sem("consts"), 16)
            sp.dma_start(KEY[:, :, :], ins["c_key"]).then_inc(sem("consts"), 16)
            sp.dma_start(BIAS[:, :, :], ins["c_bias"]).then_inc(sem("consts"), 16)
            sp.dma_start(ROW[0:E, :], ins["L1_ffn_b2"]).then_inc(sem("consts"), 16)
            sp.dma_start(ROW[E:E + 1, :], ins["L1_xattn_b_out"].rearrange("(a n) -> a n", a=1)).then_inc(sem("consts"), 16)
            sp.dma_start(ROW[E + 1:E + 2, :], ins["L1_xattn_b_gate"].rearrange("(a n) -> a n", a=1)).then_inc(sem("consts"), 16)
            sp.dma_start(GBR[:, :], ins["L1_ffn_gate_b"].rearrange("(a n) -> a n", a=1)).then_inc(sem("consts"), 16)
            sp.dma_start(GW[:, :], ins["L1_ffn_gate_w"]).then_inc(sem("consts"), 16)
            sp.dma_start(TG[:, 0:2], ins["g_xattn"].partition_broadcast(P)).then_inc(sem("consts"), 16)
            sp.dma_start(TG[:, 2:4], ins["g_ffn"].partition_broadcast(P)).then_inc(sem("consts"), 16)

            def spread(name, n, part, dst, dram, there):
                sp.wait_ge(sem("part_" + name), n)
                sp.dma_start(dram.rearrange("s p n -> p s n"), part).then_inc(sem("stored_" + name), 16)
                sp.wait_ge(sem("stored_" + name), 16 * n)
                for hp in range(2):
                    for s in range(SL):
                        src = dram[(Q_PART if name == "q" else K_PART)[s], :, :].rearrange(
                            "(j h d) n -> h d j n", h=2, d=HD)[hp]
                        r = 64 * hp + HD * s
                        sp.dma_start(dst[r:r + HD, :, :], src).then_inc(sem(there), 16)

            sp.wait_ge(sem("ks_ones"), 1)
            spread("k", 1, PRT[:, :, :], KS[:, 0, :, :], kd[0], "spread_k")

            def expert(e):
                if e >= 1:
                    sp.wait_ge(*at["weights", 4 if e < 3 else 4 + 3 * (e - 2)])
                z = (2 + e) % 3
                sp.dma_start(NW[:, z, 0:6, :], ins["L0_ffn_gate_up_w"][e].rearrange("(k p) d -> p k d", p=P)).then_inc(sem("wexp%d" % z), 16)
                sp.dma_start(NW[:, z, 6:9, :], ins["L0_ffn_down_w"][e].rearrange("p (k n) -> p k n", k=F0)).then_inc(sem("wexp%d" % z), 16)
            for e in range(3):
                expert(e)
            spread("k", 2, PRT[:, :, :], KS[:, 1, :, :], kd[1], "spread_k")
            for e in range(3, E):
                expert(e)

            for l in range(2):
                for b in range(B):
                    i = l * B + b
                    if i >= 2:
                        sp.wait_ge(*at["scores", i - 2])
                    spread("q", i + 1, PRT[:, :, 0:LQ], QS[:, i % 2, :, :], qd[i], "spread_q%d" % (i % 2))
                    sp.wait_ge(rR.free, at["maxima", i])
                    for hp in range(2):
                        sp.dma_start(QS[64 * hp + MROW:64 * hp + MROW + 1, i % 2, :, :], MS[hp:H:2, :]).then_inc(sem("m_in"), 16)
                if l == 0 and stop > 2:
                    sp.wait_ge(*at["ffn0", 0])
                    w1 = ins["L1_ffn_w1"].rearrange("e d f -> d e f")
                    w2 = ins["L1_ffn_w2"].rearrange("e (k p) d -> p e k d", p=P)
                    for e in range(E):
                        sp.dma_start(W1[:, e, :], w1[:, e, :]).then_inc(sem("w12"), 16)
                        sp.dma_start(W2[:, e, :, :], w2[:, e, :, :]).then_inc(sem("w12"), 16)
                if l == 0 and stop <= 2:
                    break
            o = out.rearrange("b (t p) d -> p (b t) d", p=P)
            for b in range(B):
                sp.wait_ge(sem("x_out"), b + 1)
                sp.dma_start(o[:, TB * b:TB * b + TB, :], X[:, TB * b:TB * b + TB, :]).then_inc(sem("stored"), 16)
            sp.wait_ge(sem("stored"), 16 * B)

        @block.gpsimd
        def _(pool):
            c = Chain(pool, sem("pool_step"))
            c.do(pool.memset(NW[:, SMALL // 9, SMALL % 9, :], 0.0), sem("small_clear")); c.own()
            c.do(pool.memset(CTX[0:NR, 1, :, :], 0.0), sem("ctx_clear")); c.own()
            c.do(pool.memset(EPT[:, :], EPS)); c.own()
            c.do(pool.memset(NHF[:, :], -0.5)); c.own()
            c.do(pool.memset(ONB[:, :], 1.0), sem("ones")); c.own()
            c.do(pool.memset(ONF[:, :], 1.0), sem("ones")); c.own()
            c.do(pool.memset(KS[:, :, :, :], 1.0), sem("ks_ones")); c.own()
            c.do(pool.memset(VR[:, :, :, :, :, :], 0.0)); c.own()
            for j in range(4):
                for l in range(2):
                    c.do(pool.memset(VR[32 * j:32 * j + 32, l, :, :, j, HD], 1.0), sem("v_ones"))
                    c.own()
            c.do(pool.memset(V[:, :, :, HD], 1.0), sem("v_ones"))

            def rstd(k, n):
                pool.wait_ge(sem("stats"), k)
                c.do(nc.gpsimd.tensor_tensor(RS[:, 0:n], MV[:, 0:n, 1], EPT[:, 0:n], ALU.add))
                c.own()
                c.do(nc.gpsimd.tensor_tensor(RS[:, 0:n], RS[:, 0:n], NHF[:, 0:n], ALU.pow), sem("rstd"))
            rstd(1, 8)
            n = 1
            LN = [(0, 1), (1, 2), (2, 2), (3, 1)]
            for s, (_, cnt) in enumerate(LN):
                if s >= stop:
                    break
                for _ in range(B * cnt):
                    n += 1
                    rstd(n, TB)

        @block.scalar
        def _(act):
            c = Chain(act, sem("act_step"))
            act.wait_ge(sem("consts"), 16 * 13)
            c.do(nc.scalar.activation(TG[:, :], TG[:, :], ACT.Tanh), sem("tanh"))
            for g, (lo, hi) in enumerate(GROUPS):
                if g not in DVE_W:
                    z = rS.next_full(act)
                    c.do(nc.scalar.activation(WT[:, lo:hi, :].rearrange("p k n -> p (k n)"), z[:, 0:(hi - lo) * P], ACT.Copy), rS.free)
            for i in range(16):
                z = rS.next_full(act)
                c.do(nc.scalar.activation(CNT[:, cnt_group(2 * i):cnt_group(2 * i) + 16, :].rearrange("p g c -> p (g c)"),
                                          z[:, 0:16 * NHI * GQ], ACT.Copy), rS.free)
            for b in range(B):
                act.wait_ge(sem("cnt_ready"), b + 1)
                c.do(nc.scalar.activation(TF[:, :, 0:LQ], TF[:, :, 0:LQ], ACT.Ln), sem("ln_ready"))

            def exps(l, b):
                if l * B + b:
                    act.wait_ge(*at["weighted", l * B + b - 1])
                for h in range(H):
                    z = rS.next_full(act)
                    c.do(nc.scalar.activation(PM[:, h, :], z, ACT.Exp), rS.free)
                    if h % 4 == 3:
                        z = rS.next_full(act)
                        c.do(nc.scalar.activation(PR[:, h // 4, :], z, ACT.Exp), rS.free)
            for b in range(B):
                exps(0, b)
            if stop <= 1:
                return
            act.wait_ge(sem("lg_ready"), 1)
            c.do(nc.scalar.activation(RT[:, 0], RT[:, 0], ACT.Exp), sem("lg_exp"))
            act.wait_ge(sem("lg_ready"), 2)
            c.do(nc.scalar.activation(R1[:, 2, :], R1[:, 2, :], ACT.Exp), sem("lg_exp"))
            n = B * 16
            k = 0
            for b in range(B):
                for e in range(E + 1):
                    for j in range(F0 if e < E else 1):
                        act.wait_ge(rA.full, n + k + 1)
                        if k >= 2:
                            act.wait_ge(rA.free, n + k - 1)
                        c.do(nc.scalar.activation(SGM[:, k % 2, :], A[:, 2 * ((n + k) % 2), :], ACT.Silu), sem("silu"))
                        k += 1
            if stop <= 2:
                return

            def gate(b):
                act.wait_ge(rR.free, at["gate", b])
                c.do(nc.scalar.activation(OT[:, :], OT[:, :], ACT.Exp, scale=-1.0), sem("gate_exp"))
            for b in range(B):
                exps(1, b)
                gate(b)
            if stop <= 3:
                return
            act.wait_ge(sem("lg_ready"), 3)
            c.do(nc.scalar.activation(RT[:, 0], RT[:, 0], ACT.Exp), sem("lg_exp"))
            for b in range(B):
                for e in range(E):
                    if b * E + e >= 2:
                        act.wait_ge(*at["down1", b * E + e - 2])
                    for j in range(0, F1, 2):
                        z = rE.next_full(act)
                        c.do(nc.scalar.activation(HB[:, (e % 2) * 4 + j, :], z, ACT.Relu,
                                                  bias=WT[:, SMALL, B1C + e * F1 + j:B1C + e * F1 + j + 1]), rE.free)

        @block.vector
        def _(dve):
            c = Chain(dve, sem("dve_step"))
            v = nc.vector

            dve.wait_ge(sem("idx"), 16)
            c.do(v.tensor_scalar(IDW, IDX, 0, float(NK), ALU.is_lt, ALU.mult)); c.own()
            c.do(v.tensor_tensor(IDX, IDX, IDW, ALU.add)); c.own()
            c.do(v.tensor_scalar(IDX, IDX, 0, float(NK - 1), ALU.max, ALU.min)); c.own()
            src = IDX.rearrange("p (h t k) -> p t h k", h=2, k=KSEL)
            hi = DIG[:, 0, :].rearrange("p (t h k) -> p t h k", h=2, k=KSEL)
            lo = DIG[:, 1, :].rearrange("p (t h k) -> p t h k", h=2, k=KSEL)
            c.do(v.tensor_single_scalar(IDW, IDX, 5, ALU.arith_shift_right)); c.own()
            idw = IDW.rearrange("p (h t k) -> p t h k", h=2, k=KSEL)
            for h in range(2):
                c.do(v.tensor_copy(hi[:, :, h, :], idw[:, :, h, :]))
            c.own()
            c.do(v.tensor_single_scalar(IDW, IDX, NLO - 1, ALU.bitwise_and)); c.own()
            for h in range(2):
                c.do(v.tensor_copy(lo[:, :, h, :], idw[:, :, h, :]), sem("digits"))
            for i in range(2):
                z = rR.next_full(dve)
                c.do(v.tensor_copy(DIGT[:, i, :], z.bitcast(bf16)), rR.free)
            c.own()

            for g, (lo_, hi_) in enumerate(GROUPS[:5]):
                if g in DVE_W:
                    z = rR.next_full(dve)
                    c.do(v.tensor_copy(WT[:, lo_:hi_, :].rearrange("p k n -> p (k n)"), z[:, 0:(hi_ - lo_) * P]), rR.free)

            def one_hots(ch):
                for a in range(NHI):
                    c.do(v.tensor_scalar(ONEA[:, a, :], DIGT[:, 0, NCH * ch:NCH * ch + NCH], float(a), None, ALU.is_equal))
                for a in range(NLO):
                    c.do(v.tensor_scalar(ONEH[:, :, a, :], DIGT[:, 1, NCH * ch:NCH * ch + NCH].rearrange("p (g q) -> p g q", q=GQ), float(a), None, ALU.is_equal),
                         sem("onehot") if a == NLO - 1 else None)
            one_hots(0)

            nstat = [0]

            def norm(dst, src, n, done=None):
                for t in range(n):
                    c.do(v.bn_stats(ST[:, t, :], src(t)))
                c.own()
                for t in range(n):
                    c.do(v.bn_aggr(MV[:, t, :], ST[:, t, :]), sem("stats") if t == n - 1 else None)
                nstat[0] += 1
                dve.wait_ge(sem("rstd"), nstat[0])
                for t in range(n):
                    c.do(v.tensor_scalar(dst(t), src(t), MV[:, t, 0:1], RS[:, t:t + 1], ALU.subtract, ALU.mult),
                         done if t == n - 1 else None)
                c.own()

            def parts(src, n, free, name):
                ap, sc = src
                c.do(v.tensor_scalar(PRT[:, 0, n], ap, sc, None, ALU.mult)); c.own()
                c.do(v.scalar_tensor_tensor(TF[:, 1, n], ap, sc, PRT[:, 0, n], ALU.mult, ALU.subtract), free); c.own()
                c.do(v.tensor_copy(PRT[:, 1, n], TF[:, 1, n])); c.own()
                c.do(v.tensor_tensor(PRT[:, 2, n], TF[:, 1, n], PRT[:, 1, n], ALU.subtract), name)

            def kv_values(l):
                z = rR.next_full(dve)
                dve.wait_ge(sem("v_ones"), 9)
                c.do(v.tensor_copy(V[:, l, :, 0:HD], z.rearrange("p (h d) -> p h d", d=HD)), rR.free)
                z = rR.next_full(dve)
                for j in range(4):
                    src_ = z[32 * j:32 * j + 32, :].rearrange("p (g j u d) -> p g j u d", j=4, u=2, d=HD)[:, :, j]
                    dst = VR[32 * j:32 * j + 32, l, :, :, j, 0:HD].rearrange("p b (g u) d -> p (b g) u d", u=2)
                    c.do(v.tensor_copy(dst, src_), rR.free if j == 3 else None)

            halves = [slice(0, 2 * NP), slice(2 * NP, 4 * NP)]
            for i in range(2):
                z = rR.next_full(dve)
                c.do(v.tensor_copy(CXT[:, halves[i]], z[:, 0:2 * NP]), rR.free)
            for i in range(2):
                z = rR.next_full(dve)
                c.do(v.tensor_copy(CLT[:, halves[i]], z[:, 0:2 * NP]), rR.free)
            for i in range(2):
                z = rR.next_full(dve)
                parts((z[:, 0:2 * NP], 1.0), halves[i], rR.free, sem("part_k") if i else None)
            kv_values(0)
            dve.wait_ge(sem("ctx"), 32)
            ctx_norm(dve, c, v, nstat)
            dve.wait_ge(sem("consts"), 16 * 13)
            for i, blk in enumerate((WQ1, WK1)):
                s4 = WT[:, blk, :].rearrange("p (h e d) -> p h e d", e=2, d=HD // 2)
                d4 = WR[:, i, :].rearrange("p (h e d) -> p h e d", e=2, d=HD // 2)
                dve.wait_ge(rS.free, 3)
                c.do(v.tensor_scalar(d4[:, :, 0, :], s4[:, :, 1, :], -1.0, None, ALU.mult))
                c.do(v.tensor_copy(d4[:, :, 1, :], s4[:, :, 0, :]), sem("rotated"))
            g1, b1 = WT[:, SMALL, G1C:G1C + 1], WT[:, SMALL, BE1C:BE1C + 1]
            for i in range(2):
                z = rR.next_full(dve)
                c.do(v.tensor_scalar(CXT[:, halves[i]], z[:, 0:2 * NP], g1, b1, ALU.mult, ALU.add), rR.free)
            for i in range(2):
                zc = rR.next_full(dve)
                for b in range(2):
                    c.do(v.tensor_tensor(TF[:, 0, NP * b:NP * b + NP], zc[:, NP * b:NP * b + NP], COS[:, 0:NP], ALU.mult), rR.free if b else None)
                zs = rR.next_full(dve)
                for b in range(2):
                    c.do(v.tensor_tensor(TF[:, 0, 2 * NP + NP * b:3 * NP + NP * b], zs[:, NP * b:NP * b + NP], SIN[:, 0:NP], ALU.mult), rR.free if b else None)
                c.own()
                c.do(v.tensor_tensor(CLT[:, halves[i]], TF[:, 0, 0:2 * NP], TF[:, 0, 2 * NP:4 * NP], ALU.add)); c.own()
                if i == 0:
                    dve.wait_ge(sem("stored_k"), 16)
                parts((CLT[:, halves[i]], 1.0), halves[i], None, sem("part_k") if i else None)
            kv_values(1)

            for g, (lo_, hi_) in enumerate(GROUPS):
                if g >= 5 and g in DVE_W:
                    z = rR.next_full(dve)
                    c.do(v.tensor_copy(WT[:, lo_:hi_, :].rearrange("p k n -> p (k n)"), z[:, 0:(hi_ - lo_) * P]), rR.free)

            for ch in range(1024 // NCH):
                if ch:
                    one_hots(ch)
                for i in range(NCH // 64):
                    z = rR.next_full(dve)
                    g0 = cnt_group(2 * (NCH // 64 * ch + i) + 1)
                    c.do(v.tensor_copy(CNT[:, g0:g0 + 16, :].rearrange("p g c -> p (g c)"), z[:, 0:16 * NHI * GQ]), rR.free)
            for b in range(B):
                z0 = rR.next_full(dve)
                z1 = rR.next_full(dve)
                zz = [z.rearrange("p (r g) -> p g r", r=GQ) for z in (z0, z1)]
                for i in range(2):
                    c.do(v.tensor_scalar(TF[:, i, 0:LQ].rearrange("p (g r) -> p g r", r=GQ), zz[i], 1.0, None, ALU.max),
                         sem("cnt_ready") if i else None)
                for i in range(2):
                    c.do(v.tensor_scalar(SGM[:, i, :].rearrange("p (g r) -> p g r", r=GQ), zz[i], 0.5, -BIG, ALU.is_lt, ALU.mult), rR.free)
                c.own()
                dve.wait_ge(sem("ln_ready"), b + 1)
                c.do(v.tensor_tensor(TF[:, :, 0:LQ], TF[:, :, 0:LQ], SGM[:, :, :], ALU.add)); c.own()
                dst = LB[:, :, LQ * b:LQ * b + LQ].rearrange("p (m s) q -> p s m q", s=2)
                c.do(v.tensor_copy(dst[:, 0], TF[:, :, 0:LQ])); c.own()
                c.do(v.tensor_tensor(dst[:, 1], TF[:, :, 0:LQ], dst[:, 0], ALU.subtract), sem("lb")); c.own()

            def norms(s, b):
                if s == 0:
                    dve.wait_ge(sem("x_in%d" % b), 16)
                t0 = TB * b
                twice = s in (1, 2)
                norm(lambda t: XN[:, t0 + t, :], lambda t: X[:, t0 + t, :], TB, None if twice else sem("xn"))
                if twice:
                    norm(lambda t: XM[:, t, :], lambda t: XN[:, t0 + t, :], TB, sem("xn"))
                g = {1: G0C, 2: G1C}.get(s)
                z = rR.next_full(dve)
                if g is None:
                    c.do(v.tensor_copy(NT[:, b, :], z), rR.free)
                else:
                    c.do(v.tensor_scalar(NT[:, b, :], z, WT[:, SMALL, g:g + 1], WT[:, SMALL, g + 1:g + 2], ALU.mult, ALU.add), rR.free)

            def q_parts(l, b):
                i = l * B + b
                if l == 0:
                    z = rR.next_full(dve)
                    src_, free = z, rR.free
                else:
                    z = rR.next_full(dve)
                    c.do(v.tensor_tensor(TF[:, 0, 0:LQ], z, COS[:, :], ALU.mult), rR.free)
                    z = rR.next_full(dve)
                    c.do(v.tensor_tensor(TF[:, 1, 0:LQ], z, SIN[:, :], ALU.mult), rR.free); c.own()
                    c.do(v.tensor_tensor(TF[:, 0, 0:LQ], TF[:, 0, 0:LQ], TF[:, 1, 0:LQ], ALU.add)); c.own()
                    src_, free = TF[:, 0, 0:LQ], None
                dve.wait_ge(sem("stored_q") if i else sem("stored_k"), 16 * i if i else 32)
                parts((src_, SCALE), slice(0, LQ), free, sem("part_q"))

            def max_unit(i):
                z = rA.next_full(dve)
                t, g = divmod(i, 4)
                zz = z.rearrange("p a (h n) -> p a h n", h=2)[:, :, :, 0:NK]
                c.do(v.tensor_reduce(MX[:, t, 4 * g:4 * g + 4].rearrange("p (h a) -> p a h", a=2), zz, AX.X, ALU.max), rA.free)

            def m_rows(l, b):
                i = l * B + b
                z = rR.next_full(dve)
                if i:
                    dve.wait_ge(sem("m_in"), 32 * i)
                c.do(v.tensor_scalar(MS[:, :], z[0:H, :], -1.0, None, ALU.mult), rR.free)

            def attended(b):
                for t in range(TB):
                    z = rR.next_full(dve)
                    zz = z[:, 0:H * (HD + 1)].rearrange("p (h d) -> p h d", d=HD + 1)
                    c.do(v.reciprocal(RC[:, t, :], zz[:, :, HD])); c.own()
                    c.do(v.tensor_tensor(O[:, t, :, :], zz[:, :, 0:HD],
                                         RC[:, t, :].rearrange("p (h a) -> p h a", a=1).broadcast_to([P, H, HD]), ALU.mult), rR.free)
                z = rR.next_full(dve)
                c.do(v.tensor_copy(OT[:, :], z), rR.free); c.own()

            def residual(b, z, free, g, last):
                xs = X[:, TB * b:TB * b + TB, :].rearrange("p t d -> p (t d)")
                out_sem = sem("x_out") if last and free is None else free
                c.do(v.scalar_tensor_tensor(xs, z, TG[:, g:g + 1], xs, ALU.mult, ALU.add), out_sem); c.own()
                if last and free is not None:
                    c.do(v.tensor_copy(RC[:, 0, 0:1], MV[:, 0, 0:1]), sem("x_out")); c.own()

            dve.wait_ge(sem("tanh"), 1)

            def attention(l):
                def pre(b):
                    norms(2 * l, b)
                    q_parts(l, b)
                last = stop == 2 * l + 1
                pre(0)
                for i in range(16):
                    max_unit(i)
                m_rows(l, 0)
                for b in range(B):
                    if b + 1 < B:
                        pre(b + 1)
                        for i in range(16):
                            max_unit(i)
                        m_rows(l, b + 1)
                    attended(b)
                    z = rR.next_full(dve)
                    if l == 0:
                        residual(b, z, rR.free, 0, last)
                        continue
                    rs = XN[:, TB * b:TB * b + TB, :].rearrange("p t d -> p (t d)")
                    c.do(v.tensor_copy(SGM[:, 0, :], z), rR.free); c.own()
                    z = rR.next_full(dve)
                    c.do(v.tensor_copy(SGM[:, 1, :], z), rR.free)
                    z = rR.next_full(dve)
                    c.do(v.tensor_copy(OT[:, :], z), rR.free); c.own()
                    c.do(v.tensor_tensor(SGM[:, 0, :], SGM[:, 0, :], rs, ALU.subtract))
                    dve.wait_ge(sem("gate_exp"), b + 1)
                    c.do(v.tensor_scalar(OT[:, :], OT[:, :], 1.0, None, ALU.add)); c.own()
                    c.do(v.reciprocal(OT[:, :], OT[:, :])); c.own()
                    c.do(v.tensor_tensor(SGM[:, 0, :], SGM[:, 0, :], OT[:, :], ALU.mult)); c.own()
                    c.do(v.tensor_tensor(SGM[:, 0, :], SGM[:, 0, :], rs, ALU.add)); c.own()
                    residual(b, SGM[:, 0, :], None, 1, last)

            attention(0)
            if stop <= 1:
                return

            def bc(ap):
                return ap.rearrange("p (t a) -> p t a", a=1).broadcast_to([P, T, E])

            def op(out_, a, b, f, done=None):
                c.do(v.tensor_tensor(out_, a, b, f), done); c.own()

            def one(out_, a, s1, s2, f1, f2=None):
                c.do(v.tensor_scalar(out_, a, s1, s2, f1, f2) if f2 is not None else v.tensor_scalar(out_, a, s1, None, f1)); c.own()

            def red(out_, a, f):
                c.do(v.tensor_reduce(out_, a, AX.X, f)); c.own()

            def top(p, onehot, best, tmp):
                red(best, p, ALU.max)
                op(tmp, p, bc(best), ALU.is_equal)
                op(tmp, tmp, KEY[:, :, :], ALU.mult)
                red(R1[:, 3, :], tmp, ALU.max)
                op(onehot, tmp, bc(R1[:, 3, :]), ALU.is_equal)

            def routing(l):
                p, o1, o2, tmp = RT[:, 0], RT[:, 1], RT[:, 2], RT[:, 3]
                red(R1[:, 0, :], LG[:, :, :], ALU.max)
                op(p, LG[:, :, :], bc(R1[:, 0, :]), ALU.subtract, sem("lg_ready"))
                dve.wait_ge(sem("lg_exp"), 2 * l + 1)
                red(R1[:, 0, :], p, ALU.add)
                c.do(v.reciprocal(R1[:, 0, :], R1[:, 0, :])); c.own()
                op(p, p, bc(R1[:, 0, :]), ALU.mult)
                top(p, o1, R1[:, 1, :], tmp)
                one(tmp, o1, -2.0, None, ALU.mult)
                op(RT[:, 4], p, tmp, ALU.add)
                top(RT[:, 4], o2, R1[:, 2, :], tmp)
                if l == 0:
                    op(R1[:, 2, :], R1[:, 2, :], R1[:, 1, :], ALU.subtract, sem("lg_ready"))
                    dve.wait_ge(sem("lg_exp"), 2)
                    one(R1[:, 1, :], R1[:, 2, :], 1.0, None, ALU.add)
                    c.do(v.reciprocal(R1[:, 1, :], R1[:, 1, :])); c.own()
                    op(R1[:, 2, :], R1[:, 2, :], R1[:, 1, :], ALU.mult)
                else:
                    op(R1[:, 0, :], R1[:, 1, :], R1[:, 2, :], ALU.add)
                    c.do(v.reciprocal(R1[:, 0, :], R1[:, 0, :])); c.own()
                    op(R1[:, 1, :], R1[:, 1, :], R1[:, 0, :], ALU.mult)
                    op(R1[:, 2, :], R1[:, 2, :], R1[:, 0, :], ALU.mult)
                op(tmp, o1, bc(R1[:, 1, :]), ALU.mult)
                op(CB[:, :, :], o2, bc(R1[:, 2, :]), ALU.mult)
                op(CB[:, :, :], CB[:, :, :], tmp, ALU.add)
                if l == 1:
                    op(MK[:, :, :], o1, o2, ALU.add, sem("mask"))
                    z = rR.next_full(dve)
                    c.do(v.tensor_scalar(tmp, z[:, 0:T * E].rearrange("p (t e) -> p t e", e=E), CAP + 0.5, None, ALU.is_lt), rR.free); c.own()
                    op(CB[:, :, :], CB[:, :, :], tmp, ALU.mult)

            def ffn(l):
                last = stop == 2 * l + 2
                for b in range(B):
                    norms(2 * l + 1, b)
                    z = rR.next_full(dve)
                    c.do(v.tensor_copy(LG[:, TB * b:TB * b + TB, :].rearrange("p t e -> p (t e)"), z[:, 0:TB * E]), rR.free)
                c.own()
                routing(l)
                n_e = E + 1 if l == 0 else E
                k = 0

                def accumulate(b, e):
                    z = rR.next_full(dve)
                    for t in range(TB):
                        zt = z[:, P * t:P * t + P]
                        w = 1.0 if e == E else CB[:, TB * b + t, e:e + 1]
                        f = rR.free if t == TB - 1 else None
                        if e == 0:
                            c.do(v.tensor_scalar(AC[:, t, :], zt, w, None, ALU.mult), f)
                        else:
                            c.do(v.scalar_tensor_tensor(AC[:, t, :], zt, w, AC[:, t, :], ALU.mult, ALU.add), f)
                    c.own()
                    if e == n_e - 1:
                        residual(b, AC[:, :, :].rearrange("p t d -> p (t d)"), None, 2 + l, last)

                pend = None
                nh = 0
                for b in range(B):
                    for e in range(n_e):
                        if l == 0:
                            for j in range(F0 if e < E else 1):
                                rA.next_full(dve)
                                slot = (rA.used - 1) % 2
                                nh += 1
                                dve.wait_ge(sem("silu"), nh)
                                c.do(v.tensor_tensor(HB[:, (b * n_e + e) % 2 * 3 + j, :], SGM[:, (nh - 1) % 2, :], A[:, 2 * slot + 1, :], ALU.mult), rA.free)
                                if j == 0 and pend:
                                    accumulate(*pend)
                                    pend = None
                        else:
                            for j in range(1, F1, 2):
                                z = rO.next_full(dve)
                                bb = WT[:, SMALL, B1C + e * F1 + j:B1C + e * F1 + j + 1]
                                c.do(v.tensor_scalar(HB[:, (e % 2) * 4 + j, :], z, bb, 0.0, ALU.add, ALU.max), rO.free)
                                if j == 1 and pend:
                                    accumulate(*pend)
                                    pend = None
                        pend = (b, e)
                accumulate(*pend)

            ffn(0)
            if stop <= 2:
                return
            attention(1)
            if stop <= 3:
                return
            ffn(1)


_INS = ['x', 'ctx_1024', 'itok_BxSx64_0_2047', 'g_xattn', 'g_ffn', 'L0_xattn_W_q', 'L0_xattn_W_kv_down', 'L0_xattn_W_kv_up', 'L0_xattn_W_out', 'L0_ffn_ln_gamma', 'L0_ffn_ln_beta', 'L0_ffn_router_w', 'L0_ffn_gate_up_w', 'L0_ffn_down_w', 'L0_ffn_shared_gate_up_w', 'L0_ffn_shared_down_w', 'L1_xattn_Wqkv', 'L1_xattn_Wout', 'L1_xattn_b_out', 'L1_xattn_Wgate', 'L1_xattn_b_gate', 'L1_xattn_gamma', 'L1_xattn_beta', 'L1_ffn_gate_w', 'L1_ffn_gate_b', 'L1_ffn_w1', 'L1_ffn_b1', 'L1_ffn_w2', 'L1_ffn_b2']


def _constants():
    f = np.float32
    one16 = 0x3F80
    pos = np.arange(LQ, dtype=f)
    inv = (1.0 / np.power(f(10000.0), np.arange(0, HD, 2, dtype=f) / f(HD))).astype(f)
    ang = (pos[:, None] * inv[None, :]).astype(f)
    rows = np.arange(P) % HD % (HD // 2)
    cos = np.cos(ang.astype(np.float64)).astype(f).T[rows]
    sin = np.sin(ang.astype(np.float64)).astype(f).T[rows]
    p = np.arange(P, dtype=np.float64)
    dist = np.abs(p[None, :] - p[:, None])
    small = np.exp(-dist * 0.1) - dist * 0.05

    def resize(n):
        at = (np.arange(n) + 0.5) * (P / n) - 0.5
        w = np.maximum(0.0, 1.0 - np.abs(at[:, None] - np.arange(P)[None, :]))
        return w / w.sum(1, keepdims=True)
    bias = (resize(LQ) @ small @ resize(NK).T).T
    full = np.full((NP, LQ), -BIG)
    full[:NK] = bias
    hi = full.astype(np.float16)
    lo = (full - hi.astype(np.float64)).astype(np.float16)
    rest = [np.tile(a[P:NP], (P // NR, 1)) for a in (hi, lo)]
    return {
        "c_id32": np.eye(P, dtype=f), "c_id16": np.eye(P, dtype=np.float16),
        "c_idb": (np.eye(P) * one16).astype(np.uint16),
        "c_tri": (np.triu(np.ones((P, P))) * one16).astype(np.uint16),
        "c_key": np.broadcast_to(np.arange(E, 0, -1, dtype=f), (P, T, E)).copy(),
        "c_cos": cos.copy(), "c_sin": sin.copy(),
        "c_bias": np.stack([hi[:P], lo[:P], rest[0], rest[1]], axis=1).copy(),
    }


STOP = 4


def kernel(**inputs):
    import concourse.bacc as bacc
    from concourse.bass_utils import run_bass_kernel_spmd

    nc = bacc.Bacc("TRN2", target_bir_lowering=False, num_devices=1)
    arrays, aps = {}, {}
    given = {n: np.ascontiguousarray(inputs[n]) for n in _INS}
    given.update(_constants())
    for n, a in given.items():
        arrays["in_" + n] = a
        aps[n] = nc.dram_tensor("in_" + n, a.shape, mybir.dt.from_np(a.dtype), kind="ExternalInput").ap()
    out = nc.dram_tensor("out_x", (B, LQ, D), fp32, kind="ExternalOutput").ap()
    build(nc, aps, out, STOP)
    r = run_bass_kernel_spmd(nc, [arrays], core_ids=[0])
    return r.results[0]["out_x"]
```

```python
import concourse.bass as bass
from concourse import mybir
from contextlib import ExitStack
import numpy as np

fp32, bf16, fp16, i32 = mybir.dt.float32, mybir.dt.bfloat16, mybir.dt.float16, mybir.dt.int32
ALU = mybir.AluOpType
ACT = mybir.ActivationFunctionType
AX = mybir.AxisListType

P = 128
D = 128
B, LQ, NK = 4, 512, 154
T = B * LQ // P
TB = LQ // P
NR = 32
NP = P + NR
H, HD = 16, 8
SCALE = HD ** -0.5
KSEL = 64
E = 8
FF0, FF1 = 384, 512
F0, F1 = FF0 // P, FF1 // P
CAP = int(1.25 * B * LQ / E)
EPS = 1e-5
BIG = 60000.0
SL = 6
SLOTS = ((0, 3, 0), (3, 2, 1), (5, 1, 2))
MROW = SL * HD
KCON = MROW + 1
GQ = 4
NLO = 32
NHI = 5
NCH = 256

WQ0, WDOWN, WUPK, WUPV, WOUT0, WQ1, WK1, WV1, WOUT1, WGATE, SG, SU, SD, SMALL, EXP0 = range(15)
B1C, G0C, BE0C, G1C, BE1C, RTC = 0, E * F1, E * F1 + 1, E * F1 + 2, E * F1 + 3, E * F1 + 4
NSMALL = RTC + E
NBLK = EXP0 + 9 * E
NWMISC = 23


class Ring:

    def __init__(self, slots, full, free):
        self.slots, self.full, self.free, self.made, self.used = slots, full, free, 0, 0

    def next_free(self, pe):
        n = len(self.slots)
        if self.made >= n:
            pe.wait_ge(self.free, self.made - n + 1)
        self.made += 1
        return self.slots[(self.made - 1) % n]

    def next_full(self, eng):
        self.used += 1
        eng.wait_ge(self.full, self.used)
        return self.slots[(self.used - 1) % len(self.slots)]


class Chain:

    def __init__(self, eng, step):
        self.eng, self.step, self.count, self.last = eng, step, {}, None

    def do(self, ins, sem=None):
        sem = self.step if sem is None else sem
        k = id(sem)
        self.count[k] = self.count.get(k, 0) + 1
        ins.then_inc(sem, 1)
        self.last = (sem, self.count[k])

    def own(self):
        self.eng.wait_ge(*self.last)


def build(nc, ins, out, stop=4):
    ctx = ExitStack()
    with ctx:
        def sb(name, shape, dt=fp32):
            return ctx.enter_context(nc.sbuf_tensor(name, shape, dt))

        def pb(name, n=512):
            return ctx.enter_context(nc.psum_tensor(name, [P, n], fp32))

        sems = {}
        at = {}

        def sem(name):
            if name not in sems:
                sems[name] = ctx.enter_context(nc.semaphore("s_" + name))
            return sems[name]

        X = sb("X", [P, T, D])
        XN = sb("XN", [P, T, D])
        NT = sb("NT", [P, B, LQ])
        NWB = sb("NWB", [P, 27 * P])
        NW = NWB[:, :].rearrange("p (s k n) -> p s k n", s=3, k=9)
        SGM = NWB[:, 0:1024].rearrange("p (s q) -> p s q", s=2)
        XM = NWB[:, 1024:1536].rearrange("p (t d) -> p t d", t=TB)
        AC = NWB[:, 1536:2048].rearrange("p (t d) -> p t d", t=TB)
        OT = NWB[:, 2048:2560]
        ZG = NWB[:, 2560:3072]
        MX = NWB[:, 3072:3136].rearrange("p (t h) -> p t h", t=TB)
        LG = NWB[:, 3136:3264].rearrange("p (t e) -> p t e", t=T)
        CB = NWB[:, 3264:3392].rearrange("p (t e) -> p t e", t=T)
        WT = sb("WT", [P, NBLK, P])
        W1 = WT[:, EXP0:EXP0 + E * F1, :].rearrange("p (e k) n -> p e (k n)", e=E)
        W2 = WT[:, EXP0 + E * F1:EXP0 + 2 * E * F1, :].rearrange("p (e k) n -> p e k n", e=E)
        WR = WT[:, WDOWN:WDOWN + 2, :]
        QSB = sb("QSB", [P, 4096])
        QS = QSB[:, :].bitcast(bf16).rearrange("p (i j q) -> p i j q", i=2, j=H // 2)
        KS = sb("KS", [P, 2, H // 2, B * NP], bf16)
        V = sb("V", [P, 2, B, P])
        VR = sb("VR", [P, 2, B, 4 * HD])
        VS = sb("VS", [P, 5, 4, 64])
        LBB = sb("LBB", [P, 4096])
        LB = LBB[:, :].bitcast(fp16).rearrange("p (s q) -> p s q", s=4)
        BIAS = sb("BIAS", [P, 2, LQ])
        BG = sb("BG", [P, 10240])
        ONEH = BG[:, 0:4096].bitcast(bf16).rearrange("p (g b q) -> p g b q", b=NLO, q=GQ)
        CNT = BG[:, 4096:9216].bitcast(bf16).rearrange("p (g c) -> p g c", c=NHI * GQ)
        PM = BG[:, 0:8192].rearrange("p (h q) -> p h q", h=H)
        PR = BG[:, 8192:10240].rearrange("p (g q) -> p g q", g=4)
        HB = BG[:, 0:4096].rearrange("p (s q) -> p s q", s=8)
        RT = BG[:, 4096:4096 + 5 * T * E].rearrange("p (r t e) -> p r t e", r=5, t=T)
        ONEA = LBB[:, 0:640].bitcast(bf16).rearrange("p (a q) -> p a q", a=NHI)
        DIG = LBB[:, 1024:2048].bitcast(bf16).rearrange("p (i q) -> p i q", i=2)
        DIGT = LBB[:, 2048:3072].bitcast(bf16).rearrange("p (i q) -> p i q", i=2)
        IDX = NT[:, 0:2, :].rearrange("p b q -> p (b q)").bitcast(i32)
        IDW = NT[:, 2:4, :].rearrange("p b q -> p (b q)").bitcast(i32)
        CTX = QSB[:, 0:1024].rearrange("p (m b d) -> p m b d", m=2, b=B)
        CTN = QSB[:, 1024:2048].rearrange("p (m b d) -> p m b d", m=2, b=B)
        CXT = QSB[:, 2048:2048 + B * NP]
        CLT = QSB[:, 2048 + B * NP:2048 + 2 * B * NP]
        PRT = sb("PRT", [P, 3, B * NP], bf16)
        TF = sb("TF", [P, 2, B * NP])
        COS = sb("COS", [P, LQ])
        SIN = sb("SIN", [P, LQ])
        ID32 = sb("ID32", [P, P])
        ID16 = sb("ID16", [P, P], fp16)
        IDB = sb("IDB", [P, P], bf16)
        TRI = sb("TRI", [P, P], bf16)
        ONB = sb("ONB", [P, P], bf16)
        ONF = sb("ONF", [1, P])
        KEY = sb("KEY", [P, T, E])
        ROW = sb("ROW", [E + 2, P])
        GBR = sb("GBR", [1, E])
        GW = sb("GW", [P, E])
        TG = sb("TG", [P, 4])
        ST = sb("ST", [P, 8, 6])
        MV = sb("MV", [P, 8, 2])
        RS = sb("RS", [P, 8])
        EPT = sb("EPT", [P, 8])
        NHF = sb("NHF", [P, 8])
        MS = sb("MS", [H, LQ], bf16)
        DUM = sb("DUM", [P, 1])
        O = sb("O", [P, TB, P])
        RC = sb("RC", [P, 2, 2 * TB, 4])
        R1 = sb("R1", [P, 4, T])
        MK = sb("MK", [P, T, E], bf16)

        A = ctx.enter_context(nc.psum_tensor("A", [P, 4, 512], fp32))
        S = [pb(f"PS{i}") for i in range(2)]
        R = [pb(f"PR{i}") for i in range(2)]
        rS = Ring([s[:, :] for s in S], sem("S_full"), sem("S_free"))
        rR = Ring([r[:, :] for r in R], sem("R_full"), sem("R_free"))
        rA = Ring([A[:, 0:2, :], A[:, 2:4, :]], sem("A_full"), sem("A_free"))
        rE = Ring([A[:, 0, :], A[:, 2, :]], sem("E_full"), sem("E_free"))
        rO = Ring([A[:, 1, :], A[:, 3, :]], sem("O_full"), sem("O_free"))

        kd = [nc.dram_tensor(f"kd{l}", [3, P, B * NP], bf16).ap() for l in range(2)]
        qd = [nc.dram_tensor(f"qd{i}", [3, P, LQ], bf16).ap() for i in range(2 * B)]

        DVE_W = [g for g in range(29) if g % 2]
        GROUPS = [(3 * g, min(3 * g + 3, EXP0)) for g in range(5)] + \
                 [(EXP0 + 3 * g, EXP0 + 3 * g + 3) for g in range(24)]

        def staged(blk):
            if blk in (WOUT0, WOUT1):
                return NW[:, 1, 5 + (blk == WOUT1), :]
            if blk < EXP0:
                return NW[:, blk // 9, blk % 9, :]
            e, j = divmod(blk - EXP0, 9)
            return NW[:, (2 + e) % 3, j, :]

        def cnt_group(i):
            ch, r = divmod(i, 2 * NCH // 64)
            half, q = divmod(r, NCH // 64)
            return half * 256 + ch * (NCH // GQ) + q * 16

        def ctx_norm(dve, c, v, nstat):
            for t in range(8):
                rows = P if t < 4 else NR
                c.do(v.bn_stats(ST[0:rows, t, :], CTX[0:rows, t // 4, t % 4, :]))
            c.do(v.memset(MV[:, 4:8, :], 0.0)); c.own()
            for t in range(8):
                rows = P if t < 4 else NR
                c.do(v.bn_aggr(MV[0:rows, t, :], ST[0:rows, t, :]), sem("stats") if t == 7 else None)
            nstat[0] += 1
            dve.wait_ge(sem("rstd"), nstat[0])
            for t in range(8):
                rows = P if t < 4 else NR
                c.do(v.tensor_scalar(CTN[0:rows, t // 4, t % 4, :], CTX[0:rows, t // 4, t % 4, :],
                                     MV[0:rows, t, 0:1], RS[0:rows, t:t + 1], ALU.subtract, ALU.mult),
                     sem("ctn") if t == 7 else None)

        block = ctx.enter_context(nc.Block())

        @block.tensor
        def _(pe):
            mm, tr = nc.tensor.matmul, nc.tensor.transpose

            pe.wait_ge(sem("idb"), 16)
            pe.wait_ge(sem("digits"), 2)
            for i in range(2):
                z = rR.next_free(pe).bitcast(bf16)
                for t in range(8):
                    last = tr(z[:, P * t:P * t + P], DIG[:, i, P * t:P * t + P], IDB[:, :])
                last.then_inc(rR.full, 1)

            def weights(groups, first):
                for g, (lo, hi) in enumerate(groups, first):
                    r = rR if g in DVE_W else rS
                    z = r.next_free(pe)
                    for k in range(lo, hi):
                        last = tr(z[:, P * (k - lo):P * (k - lo) + P], staged(k), ID32[:, :])
                    last.then_inc(r.full, 1)
                    at["weights", g] = (r.full, r.made)
            pe.wait_ge(sem("id32"), 16)
            pe.wait_ge(sem("wmisc"), 16 * NWMISC)
            pe.wait_ge(sem("wout"), 8)
            weights(GROUPS[:5], 0)

            def transposed(src, nbanks=2):
                for i in range(2):
                    z = rR.next_free(pe)
                    for b in range(2):
                        tr(z[:, NP * b:NP * b + P], src[:, 0, 2 * i + b, :], ID32[:, :])
                        last = tr(z[:, NP * b + P:NP * b + NP], src[0:NR, 1, 2 * i + b, :], ID32[0:NR, 0:NR])
                    last.then_inc(rR.full, 1)

            def evacuated():
                pe.wait_ge(rR.free, rR.made)

            def project(lhsT, src):
                for i in range(2):
                    z = rR.next_free(pe)
                    mm(z[:, 0:2 * NP], lhsT, src[:, 2 * NP * i:2 * NP * i + 2 * NP], start=True, stop=True).then_inc(rR.full, 1)

            def values(src, wv):
                z = rR.next_free(pe)
                for b in range(B):
                    last = mm(z[:, P * b:P * b + P], src[:, NP * b:NP * b + P], wv, start=True, stop=True)
                last.then_inc(rR.full, 1)
                z = rR.next_free(pe)
                for j in range(4):
                    for b in range(B):
                        last = mm(z[32 * j:32 * j + 32, P * b:P * b + P], src[:, NP * b + P:NP * b + NP], wv, start=True, stop=True)
                last.then_inc(rR.full, 1)

            pe.wait_ge(sem("ctx"), 32)
            transposed(CTX)
            pe.wait_ge(rS.free, 3)
            evacuated()
            project(WT[:, WDOWN, :], CXT)
            evacuated()
            project(WT[:, WUPK, :], CLT)
            values(CLT, WT[:, WUPV, :])
            pe.wait_ge(sem("ctn"), 1)
            transposed(CTN)
            evacuated()
            pe.wait_ge(sem("rotated"), 2)
            for i in range(2):
                for w in (WT[:, WK1, :], WR[:, 1, :]):
                    z = rR.next_free(pe)
                    mm(z[:, 0:2 * NP], w, CXT[:, 2 * NP * i:2 * NP * i + 2 * NP], start=True, stop=True).then_inc(rR.full, 1)
            values(CXT, WT[:, WV1, :])
            at["values", 0] = rR.made

            for e in range(E):
                z_ = (2 + e) % 3
                pe.wait_ge(sem("wexp%d" % z_), 32 * (e // 3 + 1))
                weights(GROUPS[5 + 3 * e:8 + 3 * e], 5 + 3 * e)

            for ch in range(1024 // NCH):
                pe.wait_ge(sem("onehot"), ch + 1)
                for i in range(2 * NCH // 64):
                    half, q = divmod(i, NCH // 64)
                    r = rR if i % 2 else rS
                    z = r.next_free(pe)
                    p0 = 64 * half
                    for g in range(16):
                        t0 = 64 * q + GQ * g
                        last = mm(z[:, 20 * g:20 * g + 20], ONEH[p0:p0 + 64, t0 // GQ, :, :].rearrange("p b q -> p (b q)"), ONEA[p0:p0 + 64, :, t0:t0 + GQ],
                                  start=True, stop=True)
                    last.then_inc(r.full, 1)
            pe.wait_ge(rR.free, rR.made)
            pe.wait_ge(rS.free, rS.made)
            for b in range(B):
                z0 = rR.next_free(pe)
                for r in range(GQ):
                    sel = IDB[:, r:P:GQ]
                    for a in range(4):
                        last = mm(z0[32 * a:32 * a + 32, P * r:P * r + P], sel, CNT[:, P * b:P * b + P, GQ * a + r], start=True, stop=True)
                last.then_inc(rR.full, 1)
                z1 = rR.next_free(pe)
                for r in range(GQ):
                    sel = IDB[:, r:P:GQ]
                    for a in range(4):
                        last = mm(z1[32 * a:32 * a + 32, P * r:P * r + P], sel, CNT[:, P * b:P * b + P, GQ * 4 + r], start=True, stop=True)
                last.then_inc(rR.full, 1)

            xn = [0]

            def tokens_t(s, b):
                xn[0] += 1
                pe.wait_ge(sem("xn"), xn[0])
                z = rR.next_free(pe)
                for t in range(TB):
                    src = XM[:, t, :] if s in (1, 2) else XN[:, TB * b + t, :]
                    last = tr(z[:, P * t:P * t + P], src, ID32[:, :])
                last.then_inc(rR.full, 1)
                evacuated()

            def q_proj(l, b):
                for w in ((WT[:, WQ0, :],) if l == 0 else (WT[:, WQ1, :], WR[:, 0, :])):
                    z = rR.next_free(pe)
                    mm(z, w, NT[:, b, :], start=True, stop=True).then_inc(rR.full, 1)

            def pick(r):
                return ID32[0:E + 2, r:r + 1].broadcast_to([E + 2, P])

            def twice(ap):
                return ap.rearrange("p (a n) -> p a n", a=1).broadcast_to([ap.shape[0], 2, ap.shape[1]])

            def nat(l, b, i):
                t, g = divmod(i, 4)
                if i == 0:
                    pe.wait_ge(sem("spread_q%d" % ((l * B + b) % 2)), 16 * 2 * 3 * ((l * B + b) // 2 + 1))
                z = rA.next_free(pe)
                qs, ks = QS[:, (l * B + b) % 2, :, P * t:P * t + P], KS[:, l, :, NP * b:NP * b + NK]
                for a in range(2):
                    zz = z[:, a, :].rearrange("p (h n) -> p h n", h=2)
                    if l == 0:
                        q0 = LQ * b + P * t
                        mm(zz[:, :, P:NK], LB[0:NR, 3, q0:q0 + P], twice(ID16[0:NR, 0:NK - P]), start=True, stop=False, skip_group_check=True)
                        mm(zz[:, :, 0:P], LB[:, 2, q0:q0 + P], twice(ID16[:, :]), start=False, stop=False, skip_group_check=True)
                    p0 = 64 * a
                    for h in range(2):
                        last = mm(zz[:, h, 0:NK], qs[p0:p0 + MROW, 2 * g + h, :], ks[p0:p0 + MROW, 2 * g + h, :],
                                  start=(l == 1 and h == 0), stop=(h == 1), skip_group_check=True)
                last.then_inc(rA.full, 1)

            def m_tr(l, b):
                pe.wait_ge(rA.free, rA.made)
                z = rR.next_free(pe)
                for t in range(TB):
                    last = tr(z[0:H, P * t:P * t + P], MX[:, t, :], ID32[:, :])
                last.then_inc(rR.full, 1)
                at["maxima", l * B + b] = rR.made

            def scores(l, b, g):
                i = l * B + b
                if g == 0:
                    pe.wait_ge(sem("m_in"), 32 * (i + 1))
                p0 = 64 * (g % 2)
                qs, ks = QS[p0:p0 + KCON, i % 2, :, :], KS[p0:p0 + KCON, l, :, :]
                for j in range(4):
                    z = rS.next_free(pe)
                    pair = 4 * (g // 2) + j
                    mm(z, ks[:, pair, NP * b:NP * b + P], qs[:, pair, :], start=True, stop=True).then_inc(rS.full, 1)
                    at["exp", l, b, g, j] = rS.made
                z = rS.next_free(pe)
                for j in range(4):
                    pair = 4 * (g // 2) + j
                    last = mm(z[32 * j:32 * j + 32, :], ks[:, pair, NP * b + P:NP * b + NP], qs[:, pair, :], start=True, stop=True)
                last.then_inc(rS.full, 1)
                at["exp", l, b, g, 4] = rS.made
                at["scores", i] = (rS.full, rS.made)

            def weighted(l, b, g):
                i = l * B + b
                if g == 0:
                    pe.wait_ge(sem("vs"), 8 * (i + 1))
                if g % 2 == 0:
                    zo[0] = rR.next_free(pe)
                z = zo[0][64 * (g % 2):64 * (g % 2) + 64, :]
                pe.wait_ge(sem("weighed"), 5 * (4 * i + g + 1))
                for j in range(4):
                    mm(z, VS[:, j, g, :], PM[:, 4 * g + j, :], start=(j == 0), stop=False)
                last = mm(z, VS[:, 4, g, :], PR[:, g, :], start=False, stop=True)
                if g % 2:
                    last.then_inc(rR.full, 1)
                    at["half", i, g // 2] = rR.made
                    at["weighted", i] = (rR.full, rR.made)
            zo = [None]

            def divide_in():
                for half in range(2):
                    z = rR.next_free(pe)
                    for t in range(TB):
                        last = tr(z[:, P * t:P * t + P], SGM[:, half, P * t:P * t + P], ID32[:, :])
                    last.then_inc(rR.full, 1)

            def turn():
                evacuated()
                z = rR.next_free(pe)
                for t in range(TB):
                    last = tr(z[:, P * t:P * t + P], O[:, t, :], ID32[:, :])
                last.then_inc(rR.full, 1)

            def out_proj(l):
                evacuated()
                z = rR.next_free(pe)
                for t in range(TB):
                    last = mm(z[:, P * t:P * t + P], OT[:, P * t:P * t + P], WT[:, WOUT0 if l == 0 else WOUT1, :], start=True, stop=(l == 0))
                    if l:
                        last = mm(z[:, P * t:P * t + P], pick(E), ROW[:, :], start=False, stop=True)
                last.then_inc(rR.full, 1)

            def gate(b):
                z = rR.next_free(pe)
                for t in range(TB):
                    last = tr(z[:, P * t:P * t + P], AC[:, t, :], ID32[:, :])
                last.then_inc(rR.full, 1)
                evacuated()
                z = rR.next_free(pe)
                for t in range(TB):
                    mm(z[:, P * t:P * t + P], O[:, t, :], WT[:, WGATE, :], start=True, stop=False)
                    last = mm(z[:, P * t:P * t + P], pick(E + 1), ROW[:, :], start=False, stop=True)
                last.then_inc(rR.full, 1)
                at["gate", b] = rR.made

            def attention(l):
                if l == 0:
                    pe.wait_ge(sem("consts"), 16 * 13)
                    pe.wait_ge(sem("lb"), 2 * B)
                    evacuated()
                    pe.wait_ge(sem("spread_k"), 16 * 2 * 3 * 2)
                    pe.wait_ge(sem("ones"), 2)
                for b in range(2):
                    tokens_t(2 * l, b)
                    q_proj(l, b)
                for i in range(16):
                    nat(l, 0, i)
                m_tr(l, 0)
                for b in range(B + 1):
                    for g in range(4):
                        if b < B:
                            scores(l, b, g)
                        if b + 1 < B:
                            for i in range(4 * g, 4 * g + 4):
                                nat(l, b + 1, i)
                        if g == 0 and b:
                            evacuated()
                            divide_in()
                        if g == 1 and b:
                            turn()
                            out_proj(l)
                        if b < B and g:
                            weighted(l, b, g - 1)
                        if g == 2:
                            if l and b:
                                evacuated()
                                gate(b - 1)
                            if b + 2 < B:
                                tokens_t(2 * l, b + 2)
                                q_proj(l, b + 2)
                    if b < B:
                        weighted(l, b, 3)
                    if b + 1 < B:
                        m_tr(l, b + 1)

            attention(0)
            if stop <= 1:
                return

            def router(l, b):
                z = rR.next_free(pe)
                for t in range(TB):
                    w = WT[:, SMALL, RTC:RTC + E] if l == 0 else GW[:, :]
                    last = mm(z[:, E * t:E * t + E], NT[:, b, P * t:P * t + P], w, start=True, stop=(l == 0))
                    if l:
                        last = mm(z[:, E * t:E * t + E], ONF[:, :], GBR[:, :], start=False, stop=True)
                last.then_inc(rR.full, 1)

            def ffn0():
                for b in range(B):
                    tokens_t(1, b)
                    router(0, b)
                hid = [rA.made]

                def down(b, e):
                    n = F0 if e < E else 1
                    hid[0] += n
                    pe.wait_ge(rA.free, hid[0])
                    z = rR.next_free(pe)
                    for t in range(TB):
                        for j in range(n):
                            w = WT[:, EXP0 + 9 * e + 6 + j, :] if e < E else WT[:, SD, :]
                            last = mm(z[:, P * t:P * t + P], HB[:, (b * (E + 1) + e) % 2 * 3 + j, P * t:P * t + P], w, start=(j == 0), stop=(j == n - 1))
                    last.then_inc(rR.full, 1)
                pend = None
                for b in range(B):
                    for e in range(E + 1):
                        for j in range(F0 if e < E else 1):
                            z = rA.next_free(pe)
                            g, u = (EXP0 + 9 * e + j, EXP0 + 9 * e + F0 + j) if e < E else (SG, SU)
                            mm(z[:, 0, :], WT[:, g, :], NT[:, b, :], start=True, stop=True)
                            mm(z[:, 1, :], WT[:, u, :], NT[:, b, :], start=True, stop=True).then_inc(rA.full, 1)
                            if j == 0 and pend:
                                down(*pend)
                        pend = (b, e)
                down(*pend)
                at["ffn0", 0] = (rR.full, rR.made)

            def ffn1():
                for b in range(B):
                    tokens_t(3, b)
                    router(1, b)
                pe.wait_ge(sem("mask"), 1)
                z = rR.next_free(pe)
                mk = MK[:, :, :]
                mm(z[:, 0:T * E], TRI[:, :], mk.rearrange("p t e -> p (t e)"), start=True, stop=False, skip_group_check=True)
                for t in range(T - 1):
                    n = T - 1 - t
                    last = mm(z[:, E * (t + 1):E * T].rearrange("p (t e) -> p t e", e=E), ONB[:, :], mk[:, t:t + 1, :].broadcast_to([P, n, E]),
                              start=False, stop=(t == T - 2), skip_group_check=True)
                last.then_inc(rR.full, 1)
                pe.wait_ge(sem("w12"), 16 * 2 * E)

                def down(b, e):
                    pe.wait_ge(rE.free, 2 * (b * E + e + 1))
                    pe.wait_ge(rO.free, 2 * (b * E + e + 1))
                    z = rR.next_free(pe)
                    for t in range(TB):
                        mm(z[:, P * t:P * t + P], pick(e), ROW[:, :], start=True, stop=False)
                        for j in range(F1):
                            last = mm(z[:, P * t:P * t + P], HB[:, (e % 2) * 4 + j, P * t:P * t + P], W2[:, e, j, :], start=False, stop=(j == F1 - 1))
                    last.then_inc(rR.full, 1)
                    at["down1", b * E + e] = (rR.full, rR.made)
                pend = None
                for b in range(B):
                    for e in range(E):
                        for j in range(F1):
                            r = rO if j % 2 else rE
                            z = r.next_free(pe)
                            mm(z, W1[:, e, P * j:P * j + P], NT[:, b, :], start=True, stop=True).then_inc(r.full, 1)
                            if j == 1 and pend:
                                down(*pend)
                        pend = (b, e)
                down(*pend)
            ffn0()
            if stop <= 2:
                return
            attention(1)
            if stop <= 3:
                return
            ffn1()

        @block.sync
        def _(sp):
            xin = ins["x"].rearrange("b (t p) d -> p (b t) d", p=P)
            sp.dma_start(IDX, ins["itok_BxSx64_0_2047"].rearrange("b (t p) k -> p (b t) k", p=P)
                         ).then_inc(sem("idx"), 16)
            sp.dma_start(IDB[:, :], ins["c_idb"].bitcast(bf16)).then_inc(sem("idb"), 16)
            sp.dma_start(ID32[:, :], ins["c_id32"]).then_inc(sem("id32"), 16)

            def w(blk, src, rows=P, at=0):
                return sp.dma_start(NW[at:at + rows, blk // 9, blk % 9, :], src).then_inc(sem("wmisc"), 16)
            def w_rows(blk, src):
                for u in range(2):
                    for_u = src.rearrange("(j u d) n -> u d j n", u=2, d=HD)[u]
                    w(blk, for_u, P // 2, P // 2 * u)
            w_rows(WQ0, ins["L0_xattn_W_q"])
            w(WDOWN, ins["L0_xattn_W_kv_down"])
            up = ins["L0_xattn_W_kv_up"].rearrange("(k p) d -> p k d", p=P)
            w_rows(WUPK, ins["L0_xattn_W_kv_up"][0:P, :])
            w(WUPV, up[:, 1, :])
            w(WOUT0, ins["L0_xattn_W_out"])
            qkv = ins["L1_xattn_Wqkv"].rearrange("(k p) d -> p k d", p=P)
            w_rows(WQ1, ins["L1_xattn_Wqkv"][0:P, :])
            w_rows(WK1, ins["L1_xattn_Wqkv"][P:2 * P, :])
            w(WV1, qkv[:, 2, :])
            w(WOUT1, ins["L1_xattn_Wout"])
            w(WGATE, ins["L1_xattn_Wgate"])
            sgu = ins["L0_ffn_shared_gate_up_w"].rearrange("(k p) d -> p k d", p=P)
            w(SG, sgu[:, 0, :])
            w(SU, sgu[:, 1, :])
            w(SD, ins["L0_ffn_shared_down_w"])
            sp.wait_ge(sem("small_clear"), 1)
            w(SMALL, ins["L1_ffn_b1"].rearrange("e (k p) -> (e k) p", p=P), E * F1, B1C)
            for c, n in ((G0C, "L0_ffn_ln_gamma"), (BE0C, "L0_ffn_ln_beta"), (G1C, "L1_xattn_gamma"), (BE1C, "L1_xattn_beta")):
                w(SMALL, ins[n].rearrange("(a n) -> a n", a=1), 1, c)
            w(SMALL, ins["L0_ffn_router_w"], E, RTC)
            sp.wait_ge(sem("ctx_clear"), 1)
            sp.dma_start(CTX[:, 0, :, :], ins["ctx_1024"][:, 0:P, :].rearrange("b n d -> n b d")).then_inc(sem("ctx"), 16)
            sp.dma_start(CTX[0:NK - P, 1, :, :], ins["ctx_1024"][:, P:NK, :].rearrange("b n d -> n b d")).then_inc(sem("ctx"), 16)
            for b in range(B):
                sp.dma_start(X[:, TB * b:TB * b + TB, :], xin[:, TB * b:TB * b + TB, :]).then_inc(sem("x_in%d" % b), 16)
            sp.dma_start(ID16[:, :], ins["c_id16"]).then_inc(sem("consts"), 16)
            sp.dma_start(COS[:, :], ins["c_cos"]).then_inc(sem("consts"), 16)
            sp.dma_start(SIN[:, :], ins["c_sin"]).then_inc(sem("consts"), 16)
            sp.dma_start(TRI[:, :], ins["c_tri"].bitcast(bf16)).then_inc(sem("consts"), 16)
            sp.dma_start(KEY[:, :, :], ins["c_key"]).then_inc(sem("consts"), 16)
            sp.dma_start(BIAS[:, :, :], ins["c_bias"]).then_inc(sem("consts"), 16)
            sp.dma_start(ROW[0:E, :], ins["L1_ffn_b2"]).then_inc(sem("consts"), 16)
            sp.dma_start(ROW[E:E + 1, :], ins["L1_xattn_b_out"].rearrange("(a n) -> a n", a=1)).then_inc(sem("consts"), 16)
            sp.dma_start(ROW[E + 1:E + 2, :], ins["L1_xattn_b_gate"].rearrange("(a n) -> a n", a=1)).then_inc(sem("consts"), 16)
            sp.dma_start(GBR[:, :], ins["L1_ffn_gate_b"].rearrange("(a n) -> a n", a=1)).then_inc(sem("consts"), 16)
            sp.dma_start(GW[:, :], ins["L1_ffn_gate_w"]).then_inc(sem("consts"), 16)
            sp.dma_start(TG[:, 0:2], ins["g_xattn"].partition_broadcast(P)).then_inc(sem("consts"), 16)
            sp.dma_start(TG[:, 2:4], ins["g_ffn"].partition_broadcast(P)).then_inc(sem("consts"), 16)

            def store_parts(name, n, part, dram):
                sp.wait_ge(sem("part_" + name), n)
                sp.dma_start(dram.rearrange("s p n -> p s n"), part).then_inc(sem("stored_" + name), 16)

            def load_parts(name, n, dst, dram, there):
                sp.wait_ge(sem("stored_" + name), 16 * n)
                for u in range(2):
                    for first, k, part in SLOTS:
                        src = dram[:, P // 2 * u:P // 2 * u + P // 2, :].rearrange("s (d j) n -> s d (j n)", d=HD)
                        src = src[part:part + 1].broadcast_to([k] + list(src.shape[1:])) if name == "q" else src[0:k]
                        at_row = 64 * u + HD * first
                        sp.dma_start(dst[at_row:at_row + HD * k, :], src).then_inc(sem(there), 16)

            sp.wait_ge(sem("ks_ones"), 1)
            store_parts("k", 1, PRT[:, :, :], kd[0])
            load_parts("k", 1, KS[:, 0, :, :].rearrange("p j n -> p (j n)"), kd[0], "spread_k")

            def expert(e):
                if e >= 1:
                    sp.wait_ge(*at["weights", 4 if e < 3 else 4 + 3 * (e - 2)])
                z = (2 + e) % 3
                sp.dma_start(NW[:, z, 0:6, :], ins["L0_ffn_gate_up_w"][e].rearrange("(k p) d -> p k d", p=P)).then_inc(sem("wexp%d" % z), 16)
                sp.dma_start(NW[:, z, 6:9, :], ins["L0_ffn_down_w"][e].rearrange("p (k n) -> p k n", k=F0)).then_inc(sem("wexp%d" % z), 16)
            for e in range(3):
                expert(e)
            store_parts("k", 2, PRT[:, :, :], kd[1])
            load_parts("k", 2, KS[:, 1, :, :].rearrange("p j n -> p (j n)"), kd[1], "spread_k")
            for e in range(3, E):
                expert(e)

            def maxima(i):
                sp.wait_ge(rR.free, at["maxima", i])
                for hp in range(2):
                    sp.dma_start(QS[64 * hp + MROW:64 * hp + MROW + 1, i % 2, :, :], MS[hp:H:2, :]).then_inc(sem("m_in"), 16)

            for l in range(2):
                for b in range(B):
                    i = l * B + b
                    store_parts("q", i + 1, PRT[:, :, 0:LQ], qd[i])
                    if i >= 2:
                        sp.wait_ge(*at["scores", i - 2])
                    load_parts("q", i + 1, QS[:, i % 2, :, :].rearrange("p j q -> p (j q)"), qd[i], "spread_q%d" % (i % 2))
                    if b >= 1:
                        maxima(i - 1)
                maxima(l * B + B - 1)
                if l == 0 and stop > 2:
                    sp.wait_ge(*at["ffn0", 0])
                    w1 = ins["L1_ffn_w1"].rearrange("e d f -> d e f")
                    w2 = ins["L1_ffn_w2"].rearrange("e (k p) d -> p e k d", p=P)
                    for e in range(E):
                        sp.dma_start(W1[:, e, :], w1[:, e, :]).then_inc(sem("w12"), 16)
                        sp.dma_start(W2[:, e, :, :], w2[:, e, :, :]).then_inc(sem("w12"), 16)
                if l == 0 and stop <= 2:
                    break
            o = out.rearrange("b (t p) d -> p (b t) d", p=P)
            for b in range(B):
                sp.wait_ge(sem("x_out"), b + 1)
                sp.dma_start(o[:, TB * b:TB * b + TB, :], X[:, TB * b:TB * b + TB, :]).then_inc(sem("stored"), 16)
            sp.wait_ge(sem("stored"), 16 * B)

        @block.gpsimd
        def _(pool):
            c = Chain(pool, sem("pool_step"))
            c.do(pool.memset(NW[:, SMALL // 9, SMALL % 9, :], 0.0), sem("small_clear")); c.own()
            c.do(pool.memset(CTX[0:NR, 1, :, :], 0.0), sem("ctx_clear")); c.own()
            c.do(pool.memset(EPT[:, :], EPS)); c.own()
            c.do(pool.memset(NHF[:, :], -0.5)); c.own()
            c.do(pool.memset(ONB[:, :], 1.0), sem("ones")); c.own()
            c.do(pool.memset(ONF[:, :], 1.0), sem("ones")); c.own()
            c.do(pool.memset(KS[:, :, :, :], 1.0), sem("ks_ones")); c.own()
            c.do(pool.memset(VS[:, :, :, :], 0.0)); c.own()
            for j in range(4):
                c.do(pool.memset(VS[:, j, :, 32 + HD * j:40 + HD * j], 1.0)); c.own()
                c.do(pool.memset(VS[32 * j:32 * j + 32, 4, :, 32 + HD * j:40 + HD * j], 1.0)); c.own()
            pool.wait_ge(sem("wmisc"), 16 * NWMISC)
            for i, blk in enumerate((WOUT0, WOUT1)):
                for g in range(4):
                    src = NW[:, blk // 9, blk % 9, :].rearrange("p (g j u d) -> p g u j d", g=2, j=4, u=2)[:, g // 2, g % 2]
                    dst = NW[:, 1, 5 + i, 32 * g:32 * g + 32].rearrange("p (j d) -> p j d", j=4)
                    c.do(nc.gpsimd.tensor_copy(dst, src), sem("wout"))

            def rstd(k, n):
                pool.wait_ge(sem("stats"), k)
                c.do(nc.gpsimd.tensor_tensor(RS[:, 0:n], MV[:, 0:n, 1], EPT[:, 0:n], ALU.add))
                c.own()
                c.do(nc.gpsimd.tensor_tensor(RS[:, 0:n], RS[:, 0:n], NHF[:, 0:n], ALU.pow), sem("rstd"))
            rstd(1, 8)
            n = 1
            def stationary(l, b):
                i = l * B + b
                if i:
                    pool.wait_ge(*at["weighted", i - 1])
                else:
                    pool.wait_ge(rR.free, at["values", 0])
                for j in range(4):
                    src = V[:, l, b, :].rearrange("p (g j u d) -> p j g u d", g=2, j=4, u=2)[:, j]
                    dst = VS[:, j, :, HD * j:HD * j + HD].rearrange("p (g u) d -> p g u d", u=2)
                    c.do(nc.gpsimd.tensor_copy(dst, src), sem("vs")); c.own()
                    rows = slice(32 * j, 32 * j + 32)
                    c.do(nc.gpsimd.tensor_copy(VS[rows, 4, :, HD * j:HD * j + HD],
                                               VR[rows, l, b, :].rearrange("p (g d) -> p g d", g=4)), sem("vs")); c.own()

            def rstds(k):
                nonlocal n
                for _ in range(k):
                    n += 1
                    rstd(n, TB)

            def attention(l, k):
                rstds(2 * k)
                stationary(l, 0)
                for b in range(B):
                    if b + 2 < B:
                        rstds(k)
                    if b + 1 < B:
                        stationary(l, b + 1)
            attention(0, 1)
            if stop > 1:
                rstds(2 * B)
            if stop > 2:
                attention(1, 2)
            if stop > 3:
                rstds(B)

        @block.scalar
        def _(act):
            c = Chain(act, sem("act_step"))
            act.wait_ge(sem("consts"), 16 * 13)
            c.do(nc.scalar.activation(TG[:, :], TG[:, :], ACT.Tanh), sem("tanh"))
            for g, (lo, hi) in enumerate(GROUPS):
                if g not in DVE_W:
                    z = rS.next_full(act)
                    c.do(nc.scalar.activation(WT[:, lo:hi, :].rearrange("p k n -> p (k n)"), z[:, 0:(hi - lo) * P], ACT.Copy), rS.free)
            for i in range(16):
                z = rS.next_full(act)
                c.do(nc.scalar.activation(CNT[:, cnt_group(2 * i):cnt_group(2 * i) + 16, :].rearrange("p g c -> p (g c)"),
                                          z[:, 0:16 * NHI * GQ], ACT.Copy), rS.free)
            def exps(l, b, between=None):
                if l * B + b:
                    act.wait_ge(*at["weighted", l * B + b - 1])
                for g in range(4):
                    for j in range(5):
                        z = rS.next_full(act)
                        dst = PM[:, 4 * g + j, :] if j < 4 else PR[:, g, :]
                        c.do(nc.scalar.activation(dst, z, ACT.Exp), rS.free)
                    if g == 3 and between:
                        between()
            for b in range(B):
                exps(0, b)
            if stop <= 1:
                return
            act.wait_ge(sem("lg_ready"), 1)
            c.do(nc.scalar.activation(RT[:, 0], RT[:, 0], ACT.Exp), sem("lg_exp"))
            act.wait_ge(sem("lg_ready"), 2)
            c.do(nc.scalar.activation(R1[:, 2, :], R1[:, 2, :], ACT.Exp), sem("lg_exp"))
            n = B * 16
            k = 0
            for b in range(B):
                for e in range(E + 1):
                    for j in range(F0 if e < E else 1):
                        act.wait_ge(rA.full, n + k + 1)
                        if k >= 2:
                            act.wait_ge(rA.free, n + k - 1)
                        c.do(nc.scalar.activation(SGM[:, k % 2, :], A[:, 2 * ((n + k) % 2), :], ACT.Silu), sem("silu"))
                        k += 1
            if stop <= 2:
                return

            def gate(b):
                act.wait_ge(rR.free, at["gate", b])
                c.do(nc.scalar.activation(ZG[:, :], ZG[:, :], ACT.Tanh, scale=0.5), sem("gate_tanh"))
            for b in range(B):
                exps(1, b, (lambda b=b: gate(b - 1)) if b else None)
            gate(B - 1)
            if stop <= 3:
                return
            act.wait_ge(sem("lg_ready"), 3)
            c.do(nc.scalar.activation(RT[:, 0], RT[:, 0], ACT.Exp), sem("lg_exp"))
            for b in range(B):
                for e in range(E):
                    if b * E + e >= 2:
                        act.wait_ge(*at["down1", b * E + e - 2])
                    for j in range(0, F1, 2):
                        z = rE.next_full(act)
                        c.do(nc.scalar.activation(HB[:, (e % 2) * 4 + j, :], z, ACT.Relu,
                                                  bias=WT[:, SMALL, B1C + e * F1 + j:B1C + e * F1 + j + 1]), rE.free)

        @block.vector
        def _(dve):
            c = Chain(dve, sem("dve_step"))
            v = nc.vector

            dve.wait_ge(sem("idx"), 16)
            c.do(v.tensor_scalar(IDW, IDX, 0, float(NK), ALU.is_lt, ALU.mult)); c.own()
            c.do(v.tensor_tensor(IDX, IDX, IDW, ALU.add)); c.own()
            c.do(v.tensor_scalar(IDX, IDX, 0, float(NK - 1), ALU.max, ALU.min)); c.own()
            src = IDX.rearrange("p (h t k) -> p t h k", h=2, k=KSEL)
            hi = DIG[:, 0, :].rearrange("p (t h k) -> p t h k", h=2, k=KSEL)
            lo = DIG[:, 1, :].rearrange("p (t h k) -> p t h k", h=2, k=KSEL)
            c.do(v.tensor_single_scalar(IDW, IDX, 5, ALU.arith_shift_right)); c.own()
            idw = IDW.rearrange("p (h t k) -> p t h k", h=2, k=KSEL)
            for h in range(2):
                c.do(v.tensor_copy(hi[:, :, h, :], idw[:, :, h, :]))
            c.own()
            c.do(v.tensor_single_scalar(IDW, IDX, NLO - 1, ALU.bitwise_and)); c.own()
            for h in range(2):
                c.do(v.tensor_copy(lo[:, :, h, :], idw[:, :, h, :]), sem("digits"))
            for i in range(2):
                z = rR.next_full(dve)
                c.do(v.tensor_copy(DIGT[:, i, :], z.bitcast(bf16)), rR.free)
            c.own()

            for g, (lo_, hi_) in enumerate(GROUPS[:5]):
                if g in DVE_W:
                    z = rR.next_full(dve)
                    c.do(v.tensor_copy(WT[:, lo_:hi_, :].rearrange("p k n -> p (k n)"), z[:, 0:(hi_ - lo_) * P]), rR.free)

            def one_hots(ch):
                for a in range(NHI):
                    c.do(v.tensor_scalar(ONEA[:, a, :], DIGT[:, 0, NCH * ch:NCH * ch + NCH], float(a), None, ALU.is_equal))
                for a in range(NLO):
                    c.do(v.tensor_scalar(ONEH[:, :, a, :], DIGT[:, 1, NCH * ch:NCH * ch + NCH].rearrange("p (g q) -> p g q", q=GQ), float(a), None, ALU.is_equal),
                         sem("onehot") if a == NLO - 1 else None)
            one_hots(0)

            nstat = [0]

            def norm(dst, src, n, done=None):
                for t in range(n):
                    c.do(v.bn_stats(ST[:, t, :], src(t)))
                c.own()
                for t in range(n):
                    c.do(v.bn_aggr(MV[:, t, :], ST[:, t, :]), sem("stats") if t == n - 1 else None)
                nstat[0] += 1
                dve.wait_ge(sem("rstd"), nstat[0])
                for t in range(n):
                    c.do(v.tensor_scalar(dst(t), src(t), MV[:, t, 0:1], RS[:, t:t + 1], ALU.subtract, ALU.mult),
                         done if t == n - 1 else None)
                c.own()

            def parts(src, n, free, name):
                ap, sc = src
                c.do(v.tensor_scalar(PRT[:, 0, n], ap, sc, None, ALU.mult)); c.own()
                c.do(v.scalar_tensor_tensor(TF[:, 1, n], ap, sc, PRT[:, 0, n], ALU.mult, ALU.subtract), free); c.own()
                c.do(v.tensor_copy(PRT[:, 1, n], TF[:, 1, n])); c.own()
                c.do(v.tensor_tensor(PRT[:, 2, n], TF[:, 1, n], PRT[:, 1, n], ALU.subtract), name)

            def kv_values(l):
                z = rR.next_full(dve)
                c.do(v.tensor_copy(V[:, l, :, :].rearrange("p b n -> p (b n)"), z), rR.free)
                z = rR.next_full(dve)
                for j in range(4):
                    src_ = z[32 * j:32 * j + 32, :].rearrange("p (g j u d) -> p g j u d", j=4, u=2, d=HD)[:, :, j]
                    dst = VR[32 * j:32 * j + 32, l, :, :].rearrange("p b (g u d) -> p (b g) u d", u=2, d=HD)
                    c.do(v.tensor_copy(dst, src_), rR.free if j == 3 else None)

            halves = [slice(0, 2 * NP), slice(2 * NP, 4 * NP)]
            for i in range(2):
                z = rR.next_full(dve)
                c.do(v.tensor_copy(CXT[:, halves[i]], z[:, 0:2 * NP]), rR.free)
            for i in range(2):
                z = rR.next_full(dve)
                c.do(v.tensor_copy(CLT[:, halves[i]], z[:, 0:2 * NP]), rR.free)
            for i in range(2):
                z = rR.next_full(dve)
                parts((z[:, 0:2 * NP], 1.0), halves[i], rR.free, sem("part_k") if i else None)
            kv_values(0)
            dve.wait_ge(sem("ctx"), 32)
            ctx_norm(dve, c, v, nstat)
            dve.wait_ge(sem("consts"), 16 * 13)
            for i, blk in enumerate((WQ1, WK1)):
                s4 = WT[:, blk, :].rearrange("p (u e n) -> p u e n", u=2, e=2)
                d4 = WR[:, i, :].rearrange("p (u e n) -> p u e n", u=2, e=2)
                dve.wait_ge(rS.free, 3)
                c.do(v.tensor_scalar(d4[:, :, 0, :], s4[:, :, 1, :], -1.0, None, ALU.mult))
                c.do(v.tensor_copy(d4[:, :, 1, :], s4[:, :, 0, :]), sem("rotated"))
            g1, b1 = WT[:, SMALL, G1C:G1C + 1], WT[:, SMALL, BE1C:BE1C + 1]
            for i in range(2):
                z = rR.next_full(dve)
                c.do(v.tensor_scalar(CXT[:, halves[i]], z[:, 0:2 * NP], g1, b1, ALU.mult, ALU.add), rR.free)
            for i in range(2):
                zc = rR.next_full(dve)
                for b in range(2):
                    c.do(v.tensor_tensor(TF[:, 0, NP * b:NP * b + NP], zc[:, NP * b:NP * b + NP], COS[:, 0:NP], ALU.mult), rR.free if b else None)
                zs = rR.next_full(dve)
                for b in range(2):
                    c.do(v.tensor_tensor(TF[:, 0, 2 * NP + NP * b:3 * NP + NP * b], zs[:, NP * b:NP * b + NP], SIN[:, 0:NP], ALU.mult), rR.free if b else None)
                c.own()
                c.do(v.tensor_tensor(CLT[:, halves[i]], TF[:, 0, 0:2 * NP], TF[:, 0, 2 * NP:4 * NP], ALU.add)); c.own()
                if i == 0:
                    dve.wait_ge(sem("stored_k"), 16)
                parts((CLT[:, halves[i]], 1.0), halves[i], None, sem("part_k") if i else None)
            kv_values(1)

            for g, (lo_, hi_) in enumerate(GROUPS):
                if g >= 5 and g in DVE_W:
                    z = rR.next_full(dve)
                    c.do(v.tensor_copy(WT[:, lo_:hi_, :].rearrange("p k n -> p (k n)"), z[:, 0:(hi_ - lo_) * P]), rR.free)

            for ch in range(1024 // NCH):
                if ch:
                    one_hots(ch)
                for i in range(NCH // 64):
                    z = rR.next_full(dve)
                    g0 = cnt_group(2 * (NCH // 64 * ch + i) + 1)
                    c.do(v.tensor_copy(CNT[:, g0:g0 + 16, :].rearrange("p g c -> p (g c)"), z[:, 0:16 * NHI * GQ]), rR.free)
            for b in range(B):
                z0 = rR.next_full(dve)
                z1 = rR.next_full(dve)
                zz = [z.rearrange("p (r g) -> p g r", r=GQ) for z in (z0, z1)]
                for i in range(2):
                    q = slice(LQ * b, LQ * b + LQ)
                    c.do(v.tensor_copy(LB[:, i, q].rearrange("p (g r) -> p g r", r=GQ), zz[i]), sem("lb"))
                    c.do(v.tensor_scalar(LB[:, 2 + i, q].rearrange("p (g r) -> p g r", r=GQ), zz[i], 0.5, -BIG, ALU.is_lt, ALU.mult), rR.free)
            c.own()

            def norms(s, b):
                if s == 0:
                    dve.wait_ge(sem("x_in%d" % b), 16)
                t0 = TB * b
                twice = s in (1, 2)
                norm(lambda t: XN[:, t0 + t, :], lambda t: X[:, t0 + t, :], TB, None if twice else sem("xn"))
                if twice:
                    norm(lambda t: XM[:, t, :], lambda t: XN[:, t0 + t, :], TB, sem("xn"))

            def tokens(s, b):
                g = {1: G0C, 2: G1C}.get(s)
                z = rR.next_full(dve)
                if g is None:
                    c.do(v.tensor_copy(NT[:, b, :], z), rR.free)
                else:
                    c.do(v.tensor_scalar(NT[:, b, :], z, WT[:, SMALL, g:g + 1], WT[:, SMALL, g + 1:g + 2], ALU.mult, ALU.add), rR.free)

            def q_parts(l, b):
                i = l * B + b
                if l == 0:
                    z = rR.next_full(dve)
                    src_, free = z, rR.free
                else:
                    z = rR.next_full(dve)
                    c.do(v.tensor_tensor(TF[:, 0, 0:LQ], z, COS[:, :], ALU.mult), rR.free)
                    z = rR.next_full(dve)
                    c.do(v.tensor_tensor(TF[:, 1, 0:LQ], z, SIN[:, :], ALU.mult), rR.free); c.own()
                    c.do(v.tensor_tensor(TF[:, 0, 0:LQ], TF[:, 0, 0:LQ], TF[:, 1, 0:LQ], ALU.add)); c.own()
                    src_, free = TF[:, 0, 0:LQ], None
                dve.wait_ge(sem("stored_q") if i else sem("stored_k"), 16 * i if i else 32)
                parts((src_, SCALE), slice(0, LQ), free, sem("part_q"))

            def max_unit(i):
                z = rA.next_full(dve)
                t, g = divmod(i, 4)
                zz = z.rearrange("p a (h n) -> p a h n", h=2)[:, :, :, 0:NK]
                c.do(v.tensor_reduce(MX[:, t, 4 * g:4 * g + 4].rearrange("p (h a) -> p a h", a=2), zz, AX.X, ALU.max), rA.free)

            def m_rows(l, b):
                i = l * B + b
                z = rR.next_full(dve)
                if i:
                    dve.wait_ge(sem("m_in"), 32 * i)
                c.do(v.tensor_scalar(MS[:, :], z[0:H, :], -1.0, None, ALU.mult), rR.free)

            def weigh(l, b, g):
                for j in range(5):
                    dve.wait_ge(rS.free, at["exp", l, b, g, j])
                    p, m = (PM[:, 4 * g + j, :], 0) if j < 4 else (PR[:, g, :], 1)
                    if l == 0:
                        c.do(v.scalar_tensor_tensor(p, p, 3e38, LB[:, m, LQ * b:LQ * b + LQ], ALU.min, ALU.mult), sem("weighed"))
                    else:
                        c.do(v.tensor_tensor(p, p, BIAS[:, m, :], ALU.mult), sem("weighed"))

            def raw(half):
                z = rR.next_full(dve)
                c.do(v.tensor_copy(SGM[:, half, :], z), rR.free)

            def divided():
                for half in range(2):
                    z = rR.next_full(dve)
                    sums = z.rearrange("p (n s j d) -> p n s j d", s=2, j=4, d=HD)[:, :, 1, :, 0]
                    c.do(v.reciprocal(RC[:, half, :, :], sums)); c.own()
                    vals = z.rearrange("p (t u s j d) -> p t u s j d", u=2, s=2, j=4, d=HD)
                    rc = RC[:, half, :, :].rearrange("p (t u) j -> p t u j", u=2)
                    for u in range(2):
                        g = 2 * half + u
                        r4 = rc[:, :, u, :].rearrange("p t (j a) -> p t j a", a=1).broadcast_to([P, TB, 4, HD])
                        c.do(v.tensor_tensor(O[:, :, 32 * g:32 * g + 32].rearrange("p t (j d) -> p t j d", j=4), vals[:, :, u, 0], r4, ALU.mult),
                             rR.free if u else None)

            def turned():
                z = rR.next_full(dve)
                c.do(v.tensor_copy(OT[:, :], z), rR.free)

            def residual(b, z, free, g, last):
                xs = X[:, TB * b:TB * b + TB, :].rearrange("p t d -> p (t d)")
                out_sem = sem("x_out") if last and free is None else free
                c.do(v.scalar_tensor_tensor(xs, z, TG[:, g:g + 1], xs, ALU.mult, ALU.add), out_sem); c.own()
                if last and free is not None:
                    c.do(v.memset(DUM[:, :], 0.0), sem("x_out")); c.own()

            dve.wait_ge(sem("tanh"), 1)

            def attention(l):
                last = stop == 2 * l + 1
                for b in range(2):
                    norms(2 * l, b)
                    tokens(2 * l, b)
                    q_parts(l, b)
                for i in range(16):
                    max_unit(i)
                m_rows(l, 0)
                def projected(b):
                    z = rR.next_full(dve)
                    if l == 0:
                        residual(b, z, rR.free, 0, last)
                    else:
                        c.do(v.tensor_copy(AC[:, :, :].rearrange("p t d -> p (t d)"), z), rR.free)

                def gate_in(b):
                    z = rR.next_full(dve)
                    c.do(v.tensor_copy(O[:, :, :].rearrange("p t d -> p (t d)"), z), rR.free)
                    z = rR.next_full(dve)
                    c.do(v.tensor_copy(ZG[:, :], z), rR.free)

                def gated(b):
                    a = AC[:, :, :].rearrange("p t d -> p (t d)")
                    rs = XN[:, TB * b:TB * b + TB, :].rearrange("p t d -> p (t d)")
                    c.do(v.tensor_tensor(a, a, rs, ALU.subtract))
                    dve.wait_ge(sem("gate_tanh"), b + 1)
                    c.do(v.tensor_scalar(ZG[:, :], ZG[:, :], 0.5, 0.5, ALU.mult, ALU.add)); c.own()
                    c.do(v.tensor_tensor(a, a, ZG[:, :], ALU.mult)); c.own()
                    c.do(v.tensor_tensor(a, a, rs, ALU.add)); c.own()
                    residual(b, a, None, 1, last)

                for b in range(B + 1):
                    for g in range(4):
                        if b + 1 < B:
                            for i in range(4 * g, 4 * g + 4):
                                max_unit(i)
                        if b < B:
                            weigh(l, b, g)
                        if g == 0 and b:
                            divided()
                        if g == 1 and b:
                            turned()
                            projected(b - 1)
                        if g == 1 and b + 2 < B:
                            norms(2 * l, b + 2)
                        if g == 2:
                            if b < B:
                                raw(0)
                            if l and b:
                                gate_in(b - 1)
                            if b + 2 < B:
                                tokens(2 * l, b + 2)
                                q_parts(l, b + 2)
                        if g == 3 and l and b:
                            gated(b - 1)
                    if b < B:
                        raw(1)
                    if b + 1 < B:
                        m_rows(l, b + 1)
                c.own()

            attention(0)
            if stop <= 1:
                return

            def bc(ap):
                return ap.rearrange("p (t a) -> p t a", a=1).broadcast_to([P, T, E])

            def op(out_, a, b, f, done=None):
                c.do(v.tensor_tensor(out_, a, b, f), done); c.own()

            def one(out_, a, s1, s2, f1, f2=None):
                c.do(v.tensor_scalar(out_, a, s1, s2, f1, f2) if f2 is not None else v.tensor_scalar(out_, a, s1, None, f1)); c.own()

            def red(out_, a, f):
                c.do(v.tensor_reduce(out_, a, AX.X, f)); c.own()

            def top(p, onehot, best, tmp):
                red(best, p, ALU.max)
                op(tmp, p, bc(best), ALU.is_equal)
                op(tmp, tmp, KEY[:, :, :], ALU.mult)
                red(R1[:, 3, :], tmp, ALU.max)
                op(onehot, tmp, bc(R1[:, 3, :]), ALU.is_equal)

            def routing(l):
                p, o1, o2, tmp = RT[:, 0], RT[:, 1], RT[:, 2], RT[:, 3]
                red(R1[:, 0, :], LG[:, :, :], ALU.max)
                op(p, LG[:, :, :], bc(R1[:, 0, :]), ALU.subtract, sem("lg_ready"))
                dve.wait_ge(sem("lg_exp"), 2 * l + 1)
                red(R1[:, 0, :], p, ALU.add)
                c.do(v.reciprocal(R1[:, 0, :], R1[:, 0, :])); c.own()
                op(p, p, bc(R1[:, 0, :]), ALU.mult)
                top(p, o1, R1[:, 1, :], tmp)
                one(tmp, o1, -2.0, None, ALU.mult)
                op(RT[:, 4], p, tmp, ALU.add)
                top(RT[:, 4], o2, R1[:, 2, :], tmp)
                if l == 0:
                    op(R1[:, 2, :], R1[:, 2, :], R1[:, 1, :], ALU.subtract, sem("lg_ready"))
                    dve.wait_ge(sem("lg_exp"), 2)
                    one(R1[:, 1, :], R1[:, 2, :], 1.0, None, ALU.add)
                    c.do(v.reciprocal(R1[:, 1, :], R1[:, 1, :])); c.own()
                    op(R1[:, 2, :], R1[:, 2, :], R1[:, 1, :], ALU.mult)
                else:
                    op(R1[:, 0, :], R1[:, 1, :], R1[:, 2, :], ALU.add)
                    c.do(v.reciprocal(R1[:, 0, :], R1[:, 0, :])); c.own()
                    op(R1[:, 1, :], R1[:, 1, :], R1[:, 0, :], ALU.mult)
                    op(R1[:, 2, :], R1[:, 2, :], R1[:, 0, :], ALU.mult)
                op(tmp, o1, bc(R1[:, 1, :]), ALU.mult)
                op(CB[:, :, :], o2, bc(R1[:, 2, :]), ALU.mult)
                op(CB[:, :, :], CB[:, :, :], tmp, ALU.add)
                if l == 1:
                    op(MK[:, :, :], o1, o2, ALU.add, sem("mask"))
                    z = rR.next_full(dve)
                    c.do(v.tensor_scalar(tmp, z[:, 0:T * E].rearrange("p (t e) -> p t e", e=E), CAP + 0.5, None, ALU.is_lt), rR.free); c.own()
                    op(CB[:, :, :], CB[:, :, :], tmp, ALU.mult)

            def ffn(l):
                last = stop == 2 * l + 2
                for b in range(B):
                    norms(2 * l + 1, b)
                    tokens(2 * l + 1, b)
                    z = rR.next_full(dve)
                    c.do(v.tensor_copy(LG[:, TB * b:TB * b + TB, :].rearrange("p t e -> p (t e)"), z[:, 0:TB * E]), rR.free)
                c.own()
                routing(l)
                n_e = E + 1 if l == 0 else E
                k = 0

                def accumulate(b, e):
                    z = rR.next_full(dve)
                    for t in range(TB):
                        zt = z[:, P * t:P * t + P]
                        w = 1.0 if e == E else CB[:, TB * b + t, e:e + 1]
                        f = rR.free if t == TB - 1 else None
                        if e == 0:
                            c.do(v.tensor_scalar(AC[:, t, :], zt, w, None, ALU.mult), f)
                        else:
                            c.do(v.scalar_tensor_tensor(AC[:, t, :], zt, w, AC[:, t, :], ALU.mult, ALU.add), f)
                    c.own()
                    if e == n_e - 1:
                        residual(b, AC[:, :, :].rearrange("p t d -> p (t d)"), None, 2 + l, last)

                pend = None
                nh = 0
                for b in range(B):
                    for e in range(n_e):
                        if l == 0:
                            for j in range(F0 if e < E else 1):
                                rA.next_full(dve)
                                slot = (rA.used - 1) % 2
                                nh += 1
                                dve.wait_ge(sem("silu"), nh)
                                c.do(v.tensor_tensor(HB[:, (b * n_e + e) % 2 * 3 + j, :], SGM[:, (nh - 1) % 2, :], A[:, 2 * slot + 1, :], ALU.mult), rA.free)
                                if j == 0 and pend:
                                    accumulate(*pend)
                                    pend = None
                        else:
                            for j in range(1, F1, 2):
                                z = rO.next_full(dve)
                                bb = WT[:, SMALL, B1C + e * F1 + j:B1C + e * F1 + j + 1]
                                c.do(v.tensor_scalar(HB[:, (e % 2) * 4 + j, :], z, bb, 0.0, ALU.add, ALU.max), rO.free)
                                if j == 1 and pend:
                                    accumulate(*pend)
                                    pend = None
                        pend = (b, e)
                accumulate(*pend)

            ffn(0)
            if stop <= 2:
                return
            attention(1)
            if stop <= 3:
                return
            ffn(1)


_INS = ['x', 'ctx_1024', 'itok_BxSx64_0_2047', 'g_xattn', 'g_ffn', 'L0_xattn_W_q', 'L0_xattn_W_kv_down', 'L0_xattn_W_kv_up', 'L0_xattn_W_out', 'L0_ffn_ln_gamma', 'L0_ffn_ln_beta', 'L0_ffn_router_w', 'L0_ffn_gate_up_w', 'L0_ffn_down_w', 'L0_ffn_shared_gate_up_w', 'L0_ffn_shared_down_w', 'L1_xattn_Wqkv', 'L1_xattn_Wout', 'L1_xattn_b_out', 'L1_xattn_Wgate', 'L1_xattn_b_gate', 'L1_xattn_gamma', 'L1_xattn_beta', 'L1_ffn_gate_w', 'L1_ffn_gate_b', 'L1_ffn_w1', 'L1_ffn_b1', 'L1_ffn_w2', 'L1_ffn_b2']


def _constants():
    f = np.float32
    one16 = 0x3F80
    pos = np.arange(LQ, dtype=f)
    inv = (1.0 / np.power(f(10000.0), np.arange(0, HD, 2, dtype=f) / f(HD))).astype(f)
    ang = (pos[:, None] * inv[None, :]).astype(f)
    rows = np.arange(P) // (H // 2) % HD % (HD // 2)
    cos = np.cos(ang.astype(np.float64)).astype(f).T[rows]
    sin = np.sin(ang.astype(np.float64)).astype(f).T[rows]
    p = np.arange(P, dtype=np.float64)
    dist = np.abs(p[None, :] - p[:, None])
    small = np.exp(-dist * 0.1) - dist * 0.05

    def resize(n):
        at = (np.arange(n) + 0.5) * (P / n) - 0.5
        w = np.maximum(0.0, 1.0 - np.abs(at[:, None] - np.arange(P)[None, :]))
        return w / w.sum(1, keepdims=True)
    bias = (resize(LQ) @ small @ resize(NK).T).T
    full = np.zeros((NP, LQ))
    full[:NK] = np.exp(bias)
    full = full.astype(f)
    return {
        "c_id32": np.eye(P, dtype=f), "c_id16": np.eye(P, dtype=np.float16),
        "c_idb": (np.eye(P) * one16).astype(np.uint16),
        "c_tri": (np.triu(np.ones((P, P))) * one16).astype(np.uint16),
        "c_key": np.broadcast_to(np.arange(E, 0, -1, dtype=f), (P, T, E)).copy(),
        "c_cos": cos.copy(), "c_sin": sin.copy(),
        "c_bias": np.stack([full[:P], np.tile(full[P:], (P // NR, 1))], axis=1).copy(),
    }


STOP = 4


def kernel(**inputs):
    import concourse.bacc as bacc
    from concourse.bass_utils import run_bass_kernel_spmd

    nc = bacc.Bacc("TRN2", target_bir_lowering=False, num_devices=1)
    arrays, aps = {}, {}
    given = {n: np.ascontiguousarray(inputs[n]) for n in _INS}
    given.update(_constants())
    for n, a in given.items():
        arrays["in_" + n] = a
        aps[n] = nc.dram_tensor("in_" + n, a.shape, mybir.dt.from_np(a.dtype), kind="ExternalInput").ap()
    out = nc.dram_tensor("out_x", (B, LQ, D), fp32, kind="ExternalOutput").ap()
    build(nc, aps, out, STOP)
    r = run_bass_kernel_spmd(nc, [arrays], core_ids=[0])
    return r.results[0]["out_x"]
```

```python
import concourse.bass as bass
from concourse import mybir
from contextlib import ExitStack
import numpy as np

fp32, bf16, fp16, i32 = mybir.dt.float32, mybir.dt.bfloat16, mybir.dt.float16, mybir.dt.int32
ALU = mybir.AluOpType
ACT = mybir.ActivationFunctionType
AX = mybir.AxisListType

P = 128
D = 128
B, LQ, NK = 4, 512, 154
T = B * LQ // P
TB = LQ // P
NR = 32
NP = P + NR
H, HD = 16, 8
SCALE = HD ** -0.5
KSEL = 64
E = 8
FF0, FF1 = 384, 512
F0, F1 = FF0 // P, FF1 // P
CAP = int(1.25 * B * LQ / E)
T0 = (2 * T + E - 1 + 3) // 4 * 4
T1 = E * CAP // P
ROWS = (T0 * P, E * CAP)
W1ST, W2ND, TOK, KEY1 = range(D, D + 4)
DW = D + 4
NCONST = 15
NREG = 8
EPS = 1e-5
BIG = 60000.0
SL = 6
SLOTS = ((0, 3, 0), (3, 2, 1), (5, 1, 2))
MROW = SL * HD
KCON = MROW + 1
NATS = (5, 5, 5, 1)
GQ = 4
NLO = 32
NHI = 5
NCHUNK = 4
NCH = 1024 // NCHUNK

WQ0, WDOWN, WUPK, WUPV, WOUT0, WQ1, WK1, WV1, WOUT1, WGATE, SG, SU, SD, SMALL, EXP0 = range(15)
B1C, G0C, BE0C, G1C, BE1C, RTC = 0, E * F1, E * F1 + 1, E * F1 + 2, E * F1 + 3, E * F1 + 4
B2C = RTC + E
NBLK = EXP0 + 9 * E
NWMISC = 24


class Ring:

    def __init__(self, slots, full, free):
        self.slots, self.full, self.free, self.made, self.used = slots, full, free, 0, 0

    def next_free(self, pe):
        n = len(self.slots)
        if self.made >= n:
            pe.wait_ge(self.free, self.made - n + 1)
        self.made += 1
        return self.slots[(self.made - 1) % n]

    def next_full(self, eng):
        self.used += 1
        eng.wait_ge(self.full, self.used)
        return self.slots[(self.used - 1) % len(self.slots)]


class Chain:

    def __init__(self, eng, step):
        self.eng, self.step, self.count, self.last = eng, step, {}, None

    def do(self, ins, sem=None):
        sem = self.step if sem is None else sem
        k = id(sem)
        self.count[k] = self.count.get(k, 0) + 1
        ins.then_inc(sem, 1)
        self.last = (sem, self.count[k])

    def own(self):
        self.eng.wait_ge(*self.last)


def build(nc, ins, out):
    ctx = ExitStack()
    with ctx:
        def sb(name, shape, dt=fp32):
            return ctx.enter_context(nc.sbuf_tensor(name, shape, dt))

        def pb(name, n=512):
            return ctx.enter_context(nc.psum_tensor(name, [P, n], fp32))

        sems = {}
        at = {}

        def sem(name):
            if name not in sems:
                sems[name] = ctx.enter_context(nc.semaphore("s_" + name))
            return sems[name]

        X = sb("X", [P, T, D])
        XNW = sb("XNW", [P, T, DW])
        XN = XNW[:, :, 0:D]
        NT = sb("NT", [P, B, LQ])
        NWB = sb("NWB", [P, 27 * P])
        NW = NWB[:, :].rearrange("p (s k n) -> p s k n", s=3, k=9)
        SGM = NWB[:, 0:1024].rearrange("p (s q) -> p s q", s=2)
        XM = NWB[:, 1024:1536].rearrange("p (t d) -> p t d", t=TB)
        AC = NWB[:, 1536:2048].rearrange("p (t d) -> p t d", t=TB)
        OT = NWB[:, 2048:2560]
        ZG = NWB[:, 2560:3072]
        MX = NWB[:, 3072:3136].rearrange("p (t h) -> p t h", t=TB)
        LG = NWB[:, 3136:3264].rearrange("p (t e) -> p t e", t=T)
        YT = NWB[:, 0:E * CAP]
        WT = sb("WT", [P, NBLK, P])
        W1 = WT[:, EXP0:EXP0 + E * F1, :].rearrange("p (e k) n -> p e (k n)", e=E)
        W2 = WT[:, EXP0 + E * F1:EXP0 + 2 * E * F1, :].rearrange("p (e k) n -> p e k n", e=E)
        WR = WT[:, WDOWN:WDOWN + 2, :]
        QSB = sb("QSB", [P, 4096])
        QS = QSB[:, :].bitcast(bf16).rearrange("p (i j q) -> p i j q", i=2, j=H // 2)
        KS = sb("KS", [P, 2, H // 2, B * NP], bf16)
        V = sb("V", [P, 2, B, P])
        VR = sb("VR", [P, 2, B, 4 * HD])
        VS = sb("VS", [P, 5, 4, 64])
        LBB = sb("LBB", [P, 4096])
        LB = LBB[:, :].bitcast(fp16).rearrange("p (s q) -> p s q", s=4)
        BIAS = sb("BIAS", [P, 2, LQ])
        BG = sb("BG", [P, 10240])
        ONEH = BG[:, 0:4096].bitcast(bf16).rearrange("p (g b q) -> p g b q", b=NLO, q=GQ)
        CNT = BG[:, 4096:9216].bitcast(bf16).rearrange("p (g c) -> p g c", c=NHI * GQ)
        PM = BG[:, 0:8192].rearrange("p (h q) -> p h q", h=H)
        PR = BG[:, 8192:10240].rearrange("p (g q) -> p g q", g=4)
        HB = BG[:, 0:4096].rearrange("p (s q) -> p s q", s=8)
        RT = BG[:, 4096:4096 + 2 * T * E].rearrange("p (r t e) -> p r t e", r=2, t=T)
        SC = NWB[:, 3264:3456].rearrange("p (r t e) -> p r t e", r=3, t=2 * TB)
        EIF = BG[:, 4352:4352 + T0 * E].rearrange("p (i e) -> p i e", e=E)
        EIS = BG[:, 4352 + T0 * E:4352 + T0 * E + T0]
        RWT = BG[:, 4712:4712 + T0]
        RIX = BG[:, 4752:4752 + T0].bitcast(i32)
        RS2 = BG[:, 4792:4792 + 2 * T0].rearrange("p (r i) -> p r i", r=2)
        RW = BG[:, 4960:10240].rearrange("p (t d) -> p t d", t=T0)
        XT = LBB[:, :].rearrange("p (g q) -> p g q", q=LQ)
        GA = BG[:, 0:4096].rearrange("p (c t d) -> p c t d", c=2, t=T)
        ONEA = LBB[:, 0:640].bitcast(bf16).rearrange("p (a q) -> p a q", a=NHI)
        DIG = LBB[:, 1024:2048].bitcast(bf16).rearrange("p (i q) -> p i q", i=2)
        DIGT = LBB[:, 2048:3072].bitcast(bf16).rearrange("p (i q) -> p i q", i=2)
        IDX = NT[:, 0:2, :].rearrange("p b q -> p (b q)").bitcast(i32)
        IDW = NT[:, 2:4, :].rearrange("p b q -> p (b q)").bitcast(i32)
        CTX = QSB[:, 0:1024].rearrange("p (m b d) -> p m b d", m=2, b=B)
        CTN = QSB[:, 1024:2048].rearrange("p (m b d) -> p m b d", m=2, b=B)
        CXT = QSB[:, 2048:2048 + B * NP]
        CLT = QSB[:, 2048 + B * NP:2048 + 2 * B * NP]
        PRT = sb("PRT", [P, 3, B * NP], bf16)
        TF = sb("TF", [P, 2, B * NP])
        OH = TF[:, :, LQ:LQ + T * E].rearrange("p c (t e) -> p c t e", e=E)
        COS = sb("COS", [P, LQ])
        SIN = sb("SIN", [P, LQ])
        ID32 = sb("ID32", [P, P])
        ID16 = sb("ID16", [P, P], fp16)
        IDB = sb("IDB", [P, P], bf16)
        TRI = sb("TRI", [P, P], bf16)
        ONB = sb("ONB", [P, P], bf16)
        KEY = sb("KEY", [P, T, E])
        ROW = sb("ROW", [2, P])
        GBR = sb("GBR", [1, E])
        GW = sb("GW", [P, E])
        TG = sb("TG", [P, 4])
        ST = sb("ST", [P, 8, 6])
        MV = sb("MV", [P, 8, 2])
        RS = sb("RS", [P, 8])
        EPT = sb("EPT", [P, 8])
        NHF = sb("NHF", [P, 8])
        MS = sb("MS", [H, LQ], bf16)
        IX = sb("IX", [P, 2, T], i32)
        EI = sb("EI", [1, T0], i32)
        IOT = sb("IOT", [P, T0])
        TN = sb("TN", [P, T])
        KT1 = sb("KT1", [P, T1])
        ZR = sb("ZR", [P, DW])
        CS = sb("CS", [P, 3, 4 + E])
        NI = sb("NI", [P, E], i32)
        O = sb("O", [P, TB, P])
        RC = sb("RC", [P, 2, 2 * TB, 4])
        R1 = sb("R1", [P, 4, T])
        MK = sb("MK", [P, T, E], bf16)

        A = ctx.enter_context(nc.psum_tensor("A", [P, 4, 512], fp32))
        S = [pb(f"PS{i}") for i in range(2)]
        R = [pb(f"PR{i}") for i in range(2)]
        rS = Ring([s[:, :] for s in S], sem("S_full"), sem("S_free"))
        rR = Ring([r[:, :] for r in R], sem("R_full"), sem("R_free"))
        rA = Ring([A[:, 0:2, :], A[:, 2:4, :]], sem("A_full"), sem("A_free"))
        rE = Ring([A[:, 0, :], A[:, 2, :]], sem("E_full"), sem("E_free"))
        rO = Ring([A[:, 1, :], A[:, 3, :]], sem("O_full"), sem("O_free"))

        rows_in = [nc.dram_tensor(f"rows_in{l}", [ROWS[l], DW], fp32).ap() for l in range(2)]
        rows_back = [nc.dram_tensor(f"rows_back{l}", [2 * T * P, D], fp32).ap() for l in range(2)]
        kd = [nc.dram_tensor(f"kd{l}", [3, P, B * NP], bf16).ap() for l in range(2)]
        qd = [nc.dram_tensor(f"qd{i}", [3, P, LQ], bf16).ap() for i in range(2 * B)]

        DVE_W = (1, 3)
        GROUPS = [(3 * g, min(3 * g + 3, EXP0)) for g in range(5)] + \
                 [(EXP0 + 3 * g, EXP0 + 3 * g + 3) for g in range(24)]

        def staged(blk):
            if blk in (WOUT0, WOUT1):
                return NW[:, 1, 5 + (blk == WOUT1), :]
            if blk < EXP0:
                return NW[:, blk // 9, blk % 9, :]
            e, j = divmod(blk - EXP0, 9)
            return NW[:, (2 + e) % 3, j, :]

        def cnt_group(i):
            ch, r = divmod(i, 2 * NCH // 64)
            half, q = divmod(r, NCH // 64)
            return half * 256 + ch * (NCH // GQ) + q * 16

        ROUTED = (((0, 1), (1, 1), (2, 2)), tuple((b, 1) for b in range(B)))
        NRT = tuple(len(x) for x in ROUTED)

        def xt_upto(e):
            return -(-CAP * (e + 1) // LQ)

        def yt_upto(e):
            return CAP * (e + 1) // LQ

        def ctx_norm(dve, c, v, nstat):
            for t in range(8):
                rows = P if t < 4 else NR
                c.do(v.bn_stats(ST[0:rows, t, :], CTX[0:rows, t // 4, t % 4, :]))
            c.do(v.memset(MV[:, 4:8, :], 0.0)); c.own()
            for t in range(8):
                rows = P if t < 4 else NR
                c.do(v.bn_aggr(MV[0:rows, t, :], ST[0:rows, t, :]), sem("stats") if t == 7 else None)
            nstat[0] += 1
            dve.wait_ge(sem("rstd"), nstat[0])
            for t in range(8):
                rows = P if t < 4 else NR
                c.do(v.tensor_scalar(CTN[0:rows, t // 4, t % 4, :], CTX[0:rows, t // 4, t % 4, :],
                                     MV[0:rows, t, 0:1], RS[0:rows, t:t + 1], ALU.subtract, ALU.mult),
                     sem("ctn") if t == 7 else None)

        block = ctx.enter_context(nc.Block())

        @block.tensor
        def _(pe):
            mm, tr = nc.tensor.matmul, nc.tensor.transpose

            pe.wait_ge(sem("idb"), 16)
            pe.wait_ge(sem("digits"), 2)
            for i in range(2):
                z = rR.next_free(pe).bitcast(bf16)
                for t in range(8):
                    last = tr(z[:, P * t:P * t + P], DIG[:, i, P * t:P * t + P], IDB[:, :])
                last.then_inc(rR.full, 1)

            def weights(groups, first):
                for g, (lo, hi) in enumerate(groups, first):
                    r = rR if g in DVE_W else rS
                    z = r.next_free(pe)
                    for k in range(lo, hi):
                        last = tr(z[:, P * (k - lo):P * (k - lo) + P], staged(k), ID32[:, :])
                    last.then_inc(r.full, 1)
                    at["weights", g] = (r.full, r.made)
            pe.wait_ge(sem("id32"), 16)
            pe.wait_ge(sem("wmisc"), 16 * NWMISC)
            pe.wait_ge(sem("wout"), 8)
            weights(GROUPS[:5], 0)

            def transposed(src):
                for i in range(2):
                    z = rR.next_free(pe)
                    for b in range(2):
                        tr(z[:, NP * b:NP * b + P], src[:, 0, 2 * i + b, :], ID32[:, :])
                        last = tr(z[:, NP * b + P:NP * b + NP], src[0:NR, 1, 2 * i + b, :], ID32[0:NR, 0:NR])
                    last.then_inc(rR.full, 1)

            def evacuated():
                pe.wait_ge(rR.free, rR.made)

            def project(lhsT, src):
                for i in range(2):
                    z = rR.next_free(pe)
                    mm(z[:, 0:2 * NP], lhsT, src[:, 2 * NP * i:2 * NP * i + 2 * NP], start=True, stop=True).then_inc(rR.full, 1)

            def values(src, wv):
                z = rR.next_free(pe)
                for b in range(B):
                    last = mm(z[:, P * b:P * b + P], src[:, NP * b:NP * b + P], wv, start=True, stop=True)
                last.then_inc(rR.full, 1)
                z = rR.next_free(pe)
                for j in range(4):
                    for b in range(B):
                        last = mm(z[32 * j:32 * j + 32, P * b:P * b + P], src[:, NP * b + P:NP * b + NP], wv, start=True, stop=True)
                last.then_inc(rR.full, 1)

            pe.wait_ge(sem("ctx"), 32)
            transposed(CTX)
            pe.wait_ge(rS.free, 3)
            evacuated()
            project(WT[:, WDOWN, :], CXT)
            evacuated()
            project(WT[:, WUPK, :], CLT)
            values(CLT, WT[:, WUPV, :])
            at["values", 0] = rR.made

            def keys_values1():
                pe.wait_ge(sem("ctn"), 1)
                transposed(CTN)
                evacuated()
                pe.wait_ge(sem("rotated"), 2)
                for i in range(2):
                    for w in (WT[:, WK1, :], WR[:, 1, :]):
                        z = rR.next_free(pe)
                        mm(z[:, 0:2 * NP], w, CXT[:, 2 * NP * i:2 * NP * i + 2 * NP], start=True, stop=True).then_inc(rR.full, 1)
                values(CXT, WT[:, WV1, :])
                at["values", 1] = rR.made

            xn = [0]

            def tokens_t(s, b, other=0):
                xn[0] += 1
                pe.wait_ge(sem("xn"), xn[0])
                z = rS.next_free(pe)
                for t in range(TB):
                    src = (AC if other else XM)[:, t, :] if s == 2 else XN[:, TB * b + t, :]
                    last = tr(z[:, P * t:P * t + P], src, ID32[:, :])
                last.then_inc(rS.full, 1)
                evacuated()
                pe.wait_ge(rS.free, rS.made)

            def q_proj(l, b):
                for w in ((WT[:, WQ0, :],) if l == 0 else (WT[:, WQ1, :], WR[:, 0, :])):
                    z = rR.next_free(pe)
                    mm(z, w, NT[:, b, :], start=True, stop=True).then_inc(rR.full, 1)

            def pick(r):
                return ID32[0:2, r:r + 1].broadcast_to([2, P])

            def twice(ap):
                return ap.rearrange("p (a n) -> p a n", a=1).broadcast_to([ap.shape[0], 2, ap.shape[1]])

            def nat(l, b, i):
                t, g = divmod(i, 4)
                if i == 0:
                    if l == 0:
                        pe.wait_ge(rR.free, at["own_counts", b])
                    pe.wait_ge(sem("spread_q%d" % ((l * B + b) % 2)), 16 * 2 * 3 * ((l * B + b) // 2 + 1))
                z = rA.next_free(pe)
                qs, ks = QS[:, (l * B + b) % 2, :, P * t:P * t + P], KS[:, l, :, NP * b:NP * b + NK]
                for a in range(2):
                    zz = z[:, a, :].rearrange("p (h n) -> p h n", h=2)
                    if l == 0:
                        q0 = LQ * b + P * t
                        mm(zz[:, :, P:NK], LB[0:NR, 3, q0:q0 + P], twice(ID16[0:NR, 0:NK - P]), start=True, stop=False, skip_group_check=True)
                        mm(zz[:, :, 0:P], LB[:, 2, q0:q0 + P], twice(ID16[:, :]), start=False, stop=False, skip_group_check=True)
                    p0 = 64 * a
                    for h in range(2):
                        last = mm(zz[:, h, 0:NK], qs[p0:p0 + MROW, 2 * g + h, :], ks[p0:p0 + MROW, 2 * g + h, :],
                                  start=(l == 1 and h == 0), stop=(h == 1), skip_group_check=True)
                last.then_inc(rA.full, 1)

            def own_counts(b):
                for rest in range(2):
                    z = rR.next_free(pe)
                    for r in range(GQ):
                        sel = IDB[:, r:P:GQ]
                        for a in range(4):
                            last = mm(z[32 * a:32 * a + 32, P * r:P * r + P], sel, CNT[:, P * b:P * b + P, GQ * (4 if rest else a) + r], start=True, stop=True)
                    last.then_inc(rR.full, 1)
                at["own_counts", b] = rR.made

            def m_tr(l, b):
                pe.wait_ge(rA.free, rA.made)
                z = rR.next_free(pe)
                for t in range(TB):
                    last = tr(z[0:H, P * t:P * t + P], MX[:, t, :], ID32[:, :])
                last.then_inc(rR.full, 1)
                at["maxima", l * B + b] = rR.made

            def scores(l, b, g, j):
                i = l * B + b
                if g == 0 and j == 0:
                    pe.wait_ge(sem("m_in"), 32 * (i + 1))
                p0 = 64 * (g % 2)
                qs, ks = QS[p0:p0 + KCON, i % 2, :, :], KS[p0:p0 + KCON, l, :, :]
                z = rS.next_free(pe)
                if j < 4:
                    pair = 4 * (g // 2) + j
                    last = mm(z, ks[:, pair, NP * b:NP * b + P], qs[:, pair, :], start=True, stop=True)
                else:
                    for k in range(4):
                        pair = 4 * (g // 2) + k
                        last = mm(z[32 * k:32 * k + 32, :], ks[:, pair, NP * b + P:NP * b + NP], qs[:, pair, :], start=True, stop=True)
                last.then_inc(rS.full, 1)
                at["exp", l, b, g, j] = rS.made
                at["scores", i, g % 2] = (rS.full, rS.made)

            def weighted(l, b, g):
                i = l * B + b
                if g == 0:
                    pe.wait_ge(sem("vs"), 8 * (i + 1))
                if g % 2 == 0:
                    zo[0] = rR.next_free(pe)
                z = zo[0][64 * (g % 2):64 * (g % 2) + 64, :]
                pe.wait_ge(sem("weighed"), 5 * (4 * i + g + 1))
                for j in range(4):
                    mm(z, VS[:, j, g, :], PM[:, 4 * g + j, :], start=(j == 0), stop=False)
                last = mm(z, VS[:, 4, g, :], PR[:, g, :], start=False, stop=True)
                if g % 2:
                    last.then_inc(rR.full, 1)
                    at["half", i, g // 2] = rR.made
                    at["weighted", i] = (rR.full, rR.made)
            zo = [None]

            def divide_in():
                for half in range(2):
                    z = rR.next_free(pe)
                    for t in range(TB):
                        last = tr(z[:, P * t:P * t + P], SGM[:, half, P * t:P * t + P], ID32[:, :])
                    last.then_inc(rR.full, 1)

            def turn():
                evacuated()
                z = rS.next_free(pe)
                for t in range(TB):
                    last = tr(z[:, P * t:P * t + P], O[:, t, :], ID32[:, :])
                last.then_inc(rS.full, 1)

            def out_proj(l, b):
                pe.wait_ge(rS.free, rS.made)
                ring = rS if l else rR
                z = ring.next_free(pe)
                for t in range(TB):
                    last = mm(z[:, P * t:P * t + P], OT[:, P * t:P * t + P], WT[:, WOUT0 if l == 0 else WOUT1, :], start=True, stop=(l == 0))
                    if l:
                        last = mm(z[:, P * t:P * t + P], pick(0), ROW[:, :], start=False, stop=True)
                last.then_inc(ring.full, 1)
                at["attended", l, b] = ring.made

            def gate(b):
                pe.wait_ge(rS.free, at["attended", 1, b])
                z = rS.next_free(pe)
                for t in range(TB):
                    last = tr(z[:, P * t:P * t + P], AC[:, t, :], ID32[:, :])
                last.then_inc(rS.full, 1)
                pe.wait_ge(rS.free, rS.made)
                z = rS.next_free(pe)
                for t in range(TB):
                    mm(z[:, P * t:P * t + P], O[:, t, :], WT[:, WGATE, :], start=True, stop=False)
                    last = mm(z[:, P * t:P * t + P], pick(1), ROW[:, :], start=False, stop=True)
                last.then_inc(rS.full, 1)
                at["gate", b] = rS.made

            def router(l, b):
                z = rR.next_free(pe)
                for t in range(TB):
                    w = WT[:, SMALL, RTC:RTC + E] if l == 0 else GW[:, :]
                    last = mm(z[:, E * t:E * t + E], NT[:, b, P * t:P * t + P], w, start=True, stop=(l == 0))
                    if l:
                        last = mm(z[:, E * t:E * t + E], ID32[0:1, 0:1].broadcast_to([1, P]), GBR[:, :], start=False, stop=True)
                last.then_inc(rR.full, 1)

            def ranks(t0, n, mask, total):
                pe.wait_ge(sem("mask"), mask)
                z = rR.next_free(pe)
                zz = z[:, 0:n * E].rearrange("p (t e) -> p t e", e=E)
                mm(z[:, 0:n * E], TRI[:, :], MK[:, t0:t0 + n, :].rearrange("p t e -> p (t e)"), start=True, stop=False, skip_group_check=True)
                for t in range(t0 + n - 1):
                    lo = max(0, t + 1 - t0)
                    last = mm(zz[:, lo:, :], ONB[:, :], MK[:, t:t + 1, :].broadcast_to([P, n - lo, E]),
                              start=False, stop=(not total and t == t0 + n - 2), skip_group_check=True)
                if total:
                    for t in range(T):
                        last = mm(z[:, E * n:E * n + E], ONB[:, :], MK[:, t, :], start=False, stop=(t == T - 1), skip_group_check=True)
                last.then_inc(rR.full, 1)

            def attention(l):
                if l == 0:
                    pe.wait_ge(sem("consts"), 16 * NCONST)
                    own_counts(0)
                    pe.wait_ge(sem("spread_k"), 16 * 2 * 3)
                    pe.wait_ge(sem("ones"), 2)
                else:
                    pe.wait_ge(sem("spread_k"), 16 * 2 * 3 * 2)
                    for b in range(2):
                        tokens_t(2, b, b)
                        q_proj(1, b)
                for i in range(16):
                    nat(l, 0, i)
                    if l == 0 and i % 4 == 1 and i // 4 + 1 < B:
                        own_counts(i // 4 + 1)
                m_tr(l, 0)
                for b in range(B + 1):
                    for g in range(4):
                        if b < B:
                            scores(l, b, g, 0)
                        for k in range(5):
                            if b < B and k < 4:
                                scores(l, b, g, k + 1)
                            if b + 1 < B and k < NATS[g]:
                                nat(l, b + 1, sum(NATS[:g]) + k)
                        if g == 0 and b:
                            evacuated()
                            divide_in()
                        if g == 1 and b:
                            turn()
                            out_proj(l, b - 1)
                        if g == 3 and b + 1 < B:
                            m_tr(l, b + 1)
                        if b < B and g:
                            weighted(l, b, g - 1)
                        if g == 2:
                            if l and b:
                                evacuated()
                                gate(b - 1)
                            if b + 2 < B:
                                tokens_t(2 * l, b + 2)
                                q_proj(l, b + 2)
                            if l and b >= 2:
                                ranks(TB * (b - 2), TB, NRT[0] + b - 1, False)
                    if b < B:
                        weighted(l, b, 3)
                    if b:
                        tokens_t(2 * l + 1, b - 1)
                        router(l, b - 1)

            def counting(ch):
                pe.wait_ge(sem("onehot"), ch + 1)
                for i in range(2 * NCH // 64):
                    half, q = divmod(i, NCH // 64)
                    z = rS.next_free(pe)
                    p0 = 64 * half
                    for g in range(16):
                        t0 = 64 * q + GQ * g
                        last = mm(z[:, 20 * g:20 * g + 20], ONEH[p0:p0 + 64, t0 // GQ, :, :].rearrange("p b q -> p (b q)"), ONEA[p0:p0 + 64, :, t0:t0 + GQ],
                                  start=True, stop=True)
                    last.then_inc(rS.full, 1)
                at["counting", ch] = rS.made

            for ch in range(NCHUNK):
                counting(ch)
                for e in range(2 * ch, 2 * ch + 2):
                    z_ = (2 + e) % 3
                    pe.wait_ge(sem("wexp%d" % z_), 32 * (e // 3 + 1))
                    weights(GROUPS[5 + 3 * e:8 + 3 * e], 5 + 3 * e)
                if ch < 2:
                    tokens_t(0, ch)
                    q_proj(0, ch)
            pe.wait_ge(rR.free, rR.made)
            pe.wait_ge(rS.free, rS.made)
            attention(0)

            def rows_t(k):
                z = rR.next_free(pe)
                for t in range(TB):
                    last = tr(z[:, P * t:P * t + P], RW[:, TB * k + t, 0:D], ID32[:, :])
                last.then_inc(rR.full, 1)
                at["rows_t", k] = rR.made

            def ffn0():
                ranks(0, T, NRT[0], True)
                base = rA.made
                for b in range(B + 1):
                    if b < B:
                        z = rA.next_free(pe)
                        mm(z[:, 0, :], WT[:, SG, :], NT[:, b, :], start=True, stop=True)
                        mm(z[:, 1, :], WT[:, SU, :], NT[:, b, :], start=True, stop=True).then_inc(rA.full, 1)
                    if b:
                        pe.wait_ge(rA.free, base + b)
                        z = rR.next_free(pe)
                        for t in range(TB):
                            last = mm(z[:, P * t:P * t + P], HB[:, 4 + (b - 1) % 2, P * t:P * t + P], WT[:, SD, :], start=True, stop=True)
                        last.then_inc(rR.full, 1)
                keys_values1()
                pe.wait_ge(sem("experts"), 1)
                regs = [pe.alloc_register(f"expert{i}") for i in range(NREG)]
                blocks = {}
                base = rA.made
                pe.wait_ge(sem("rows_in0_0"), 16)
                rows_t(0)
                for i in range(T0 + 2):
                    if i < T0:
                        if i % NREG == 0:
                            pe.load(regs, EI[0:1, i:i + NREG])
                            for k in range(NREG):
                                blocks[i + k] = pe.snap(regs[k], min_val=EXP0, max_val=EXP0 + 9 * (E - 1))
                        pe.wait_ge(rR.free, at["rows_t", i // TB])
                        xt = XT[:, i // TB % 8, P * (i % TB):P * (i % TB) + P]
                        z = rA.next_free(pe)
                        for k in range(2):
                            w = WT[:, bass.ds(blocks[i] + F0 * k, F0), :].rearrange("p a n -> p (a n)")
                            last = mm(z[:, k, 0:FF0], xt, w, start=True, stop=True)
                        last.then_inc(rA.full, 1)
                        if i % TB == 1 and i // TB + 1 < T0 // TB:
                            if i < TB:
                                pe.wait_ge(sem("rows_in0_1"), 16)
                            rows_t(i // TB + 1)
                    if 1 <= i <= T0:
                        pe.wait_ge(rA.free, base + i)
                        z = rS.next_free(pe)
                        for k in range(F0):
                            last = tr(z[:, P * k:P * k + P], HB[:, (i - 1) % 2, P * k:P * k + P], ID32[:, :])
                        last.then_inc(rS.full, 1)
                        at["hidden_t", i - 1] = rS.made
                    if i >= 2:
                        pe.wait_ge(rS.free, at["hidden_t", i - 2])
                        z = rR.next_free(pe)
                        for k in range(F0):
                            w = WT[:, bass.ds(blocks[i - 2] + (2 * F0 + k), 1), :].rearrange("p a n -> p (a n)")
                            last = mm(z[:, 0:P], HB[:, 2 + i % 2, P * k:P * k + P], w, start=(k == 0), stop=(k == F0 - 1))
                        last.then_inc(rR.full, 1)
                        at["down0", i - 2] = rR.made
                at["ffn0", 0] = (rR.full, rR.made)

            def ffn1():
                ranks(TB * (B - 1), TB, NRT[0] + B, False)
                pe.wait_ge(sem("w12"), 16 * 2 * E)
                pe.wait_ge(sem("rows_in1_0"), 16)

                def down(e):
                    pe.wait_ge(rE.free, 2 * (e + 1))
                    pe.wait_ge(rO.free, 2 * (e + 1))
                    z = rR.next_free(pe)
                    for j in range(F1):
                        last = mm(z[:, 0:CAP], W2[:, e, j, :], HB[:, (e % 2) * 4 + j, 0:CAP], start=(j == 0), stop=(j == F1 - 1))
                    last.then_inc(rR.full, 1)
                    at["down1", e] = (rR.full, rR.made)

                def up(e, js):
                    for j in js:
                        r = rO if j % 2 else rE
                        z = r.next_free(pe)
                        mm(z[:, 0:CAP], W1[:, e, P * j:P * j + P], XTF[:, CAP * e:CAP * e + CAP], start=True, stop=True).then_inc(r.full, 1)
                XTF = XT.rearrange("p g q -> p (g q)")
                rows_t(0)
                for e in range(E + 2):
                    if e < E:
                        pe.wait_ge(rR.free, at["rows_t", xt_upto(e) - 1])
                        up(e, (0, 1))
                    if e + 1 < E:
                        if e == 0:
                            pe.wait_ge(sem("rows_in1_1"), 16)
                        for k in range(xt_upto(e), xt_upto(e + 1)):
                            rows_t(k)
                    if 1 <= e <= E:
                        down(e - 1)
                    if e < E:
                        up(e, (2, 3))
                    if e >= 2:
                        for k in range(yt_upto(e - 3), yt_upto(e - 2)):
                            pe.wait_ge(rR.free, at["down1", e - 2][1])
                            z = rR.next_free(pe)
                            for t in range(TB):
                                i = TB * k + t
                                last = tr(z[:, P * t:P * t + P], YT[:, P * i:P * i + P], ID32[:, :])
                            last.then_inc(rR.full, 1)
                            at["rows_out1", k] = rR.made
            ffn0()
            attention(1)
            ffn1()

        @block.sync
        def _(sp):
            xin = ins["x"].rearrange("b (t p) d -> p (b t) d", p=P)
            sp.dma_start(IDX, ins["itok_BxSx64_0_2047"].rearrange("b (t p) k -> p (b t) k", p=P)
                         ).then_inc(sem("idx"), 16)
            sp.dma_start(IDB[:, :], ins["c_idb"].bitcast(bf16)).then_inc(sem("idb"), 16)
            sp.dma_start(ID32[:, :], ins["c_id32"]).then_inc(sem("id32"), 16)

            def w(blk, src, rows=P, at=0):
                return sp.dma_start(NW[at:at + rows, blk // 9, blk % 9, :], src).then_inc(sem("wmisc"), 16)
            def w_rows(blk, src):
                for u in range(2):
                    for_u = src.rearrange("(j u d) n -> u d j n", u=2, d=HD)[u]
                    w(blk, for_u, P // 2, P // 2 * u)
            w_rows(WQ0, ins["L0_xattn_W_q"])
            w(WDOWN, ins["L0_xattn_W_kv_down"])
            up = ins["L0_xattn_W_kv_up"].rearrange("(k p) d -> p k d", p=P)
            w_rows(WUPK, ins["L0_xattn_W_kv_up"][0:P, :])
            w(WUPV, up[:, 1, :])
            w(WOUT0, ins["L0_xattn_W_out"])
            qkv = ins["L1_xattn_Wqkv"].rearrange("(k p) d -> p k d", p=P)
            w_rows(WQ1, ins["L1_xattn_Wqkv"][0:P, :])
            w_rows(WK1, ins["L1_xattn_Wqkv"][P:2 * P, :])
            w(WV1, qkv[:, 2, :])
            w(WOUT1, ins["L1_xattn_Wout"])
            w(WGATE, ins["L1_xattn_Wgate"])
            sgu = ins["L0_ffn_shared_gate_up_w"].rearrange("(k p) d -> p k d", p=P)
            w(SG, sgu[:, 0, :])
            w(SU, sgu[:, 1, :])
            w(SD, ins["L0_ffn_shared_down_w"])
            sp.wait_ge(sem("small_clear"), 1)
            w(SMALL, ins["L1_ffn_b1"].rearrange("e (k p) -> (e k) p", p=P), E * F1, B1C)
            for c, n in ((G0C, "L0_ffn_ln_gamma"), (BE0C, "L0_ffn_ln_beta"), (G1C, "L1_xattn_gamma"), (BE1C, "L1_xattn_beta")):
                w(SMALL, ins[n].rearrange("(a n) -> a n", a=1), 1, c)
            w(SMALL, ins["L1_ffn_b2"], E, B2C)
            w(SMALL, ins["L0_ffn_router_w"], E, RTC)
            sp.wait_ge(sem("ctx_clear"), 1)
            def load_ctx(there):
                sp.dma_start(CTX[:, 0, :, :], ins["ctx_1024"][:, 0:P, :].rearrange("b n d -> n b d")).then_inc(sem(there), 16)
                sp.dma_start(CTX[0:NK - P, 1, :, :], ins["ctx_1024"][:, P:NK, :].rearrange("b n d -> n b d")).then_inc(sem(there), 16)
            load_ctx("ctx")
            for b in range(B):
                sp.dma_start(X[:, TB * b:TB * b + TB, :], xin[:, TB * b:TB * b + TB, :]).then_inc(sem("x_in%d" % b), 16)
            sp.dma_start(ID16[:, :], ins["c_id16"]).then_inc(sem("consts"), 16)
            sp.dma_start(COS[:, :], ins["c_cos"]).then_inc(sem("consts"), 16)
            sp.dma_start(SIN[:, :], ins["c_sin"]).then_inc(sem("consts"), 16)
            sp.dma_start(TRI[:, :], ins["c_tri"].bitcast(bf16)).then_inc(sem("consts"), 16)
            sp.dma_start(KEY[:, :, :], ins["c_key"]).then_inc(sem("consts"), 16)
            sp.dma_start(BIAS[:, :, :], ins["c_bias"]).then_inc(sem("consts"), 16)
            sp.dma_start(TN[:, :], ins["c_tok"]).then_inc(sem("consts"), 16)
            sp.dma_start(KT1[:, :], ins["c_rowkey"]).then_inc(sem("consts"), 16)
            sp.dma_start(IOT[:, :], ins["c_iota"]).then_inc(sem("consts"), 16)
            sp.dma_start(ROW[0:1, :], ins["L1_xattn_b_out"].rearrange("(a n) -> a n", a=1)).then_inc(sem("consts"), 16)
            sp.dma_start(ROW[1:2, :], ins["L1_xattn_b_gate"].rearrange("(a n) -> a n", a=1)).then_inc(sem("consts"), 16)
            sp.dma_start(GBR[:, :], ins["L1_ffn_gate_b"].rearrange("(a n) -> a n", a=1)).then_inc(sem("consts"), 16)
            sp.dma_start(GW[:, :], ins["L1_ffn_gate_w"]).then_inc(sem("consts"), 16)
            sp.dma_start(TG[:, 0:2], ins["g_xattn"].partition_broadcast(P)).then_inc(sem("consts"), 16)
            sp.dma_start(TG[:, 2:4], ins["g_ffn"].partition_broadcast(P)).then_inc(sem("consts"), 16)

            def store_parts(name, n, part, dram):
                sp.wait_ge(sem("part_" + name), n)
                sp.dma_start(dram.rearrange("s p n -> p s n"), part).then_inc(sem("stored_" + name), 16)

            def load_parts(name, n, dst, dram, there, us=(0, 1)):
                sp.wait_ge(sem("stored_" + name), 16 * n)
                for u in us:
                    for first, k, part in SLOTS:
                        src = dram[:, P // 2 * u:P // 2 * u + P // 2, :].rearrange("s (d j) n -> s d (j n)", d=HD)
                        src = src[part:part + 1].broadcast_to([k] + list(src.shape[1:])) if name == "q" else src[0:k]
                        at_row = 64 * u + HD * first
                        sp.dma_start(dst[at_row:at_row + HD * k, :], src).then_inc(sem(there), 16)


            def expert(e):
                if e >= 1:
                    sp.wait_ge(*at["weights", 4 if e < 3 else 4 + 3 * (e - 2)])
                z = (2 + e) % 3
                sp.dma_start(NW[:, z, 0:6, :], ins["L0_ffn_gate_up_w"][e].rearrange("(k p) d -> p k d", p=P)).then_inc(sem("wexp%d" % z), 16)
                sp.dma_start(NW[:, z, 6:9, :], ins["L0_ffn_down_w"][e].rearrange("p (k n) -> p k n", k=F0)).then_inc(sem("wexp%d" % z), 16)
            for e in range(3):
                expert(e)
            sp.wait_ge(sem("ks_ones"), 1)
            store_parts("k", 1, PRT[:, :, :], kd[0])
            load_parts("k", 1, KS[:, 0, :, :].rearrange("p j n -> p (j n)"), kd[0], "spread_k")
            expert(3)
            expert(4)
            def maxima(i):
                sp.wait_ge(rR.free, at["maxima", i])
                for hp in range(2):
                    sp.dma_start(QS[64 * hp + MROW:64 * hp + MROW + 1, i % 2, :, :], MS[hp:H:2, :]).then_inc(sem("m_in"), 16)

            def queries(i):
                store_parts("q", i + 1, PRT[:, :, 0:LQ], qd[i])
                for u in range(2):
                    if u and i % B >= 2:
                        maxima(i - 1)
                    if i >= 2:
                        sp.wait_ge(*at["scores", i - 2, u])
                    load_parts("q", i + 1, QS[:, i % 2, :, :].rearrange("p j q -> p (j q)"), qd[i], "spread_q%d" % (i % 2), (u,))
            queries(0)
            expert(5)
            expert(6)
            queries(1)
            expert(7)
            sp.wait_ge(sem("zeros"), 1)
            for dst in (rows_in[0], rows_in[1], rows_back[1]):
                w_, n_ = dst.shape[1], dst.shape[0] // P
                sp.dma_start(dst.rearrange("(t p) d -> p t d", p=P),
                             ZR[:, 0:w_].rearrange("p (a d) -> p a d", a=1).broadcast_to([P, n_, w_])).then_inc(sem("cleared"), 16)

            def expert_rows(l, first):
                sp.wait_ge(sem("scattered"), 16 * 2 * T * (l + 1))
                n = ROWS[l] // P
                src = rows_in[l].rearrange("(t p) d -> p t d", p=P)
                for k, (lo, hi) in enumerate(((0, first), (first, n))):
                    sp.dma_start(RW[:, lo:hi, :], src[:, lo:hi, :]).then_inc(sem("rows_in%d_%d" % (l, k)), 16)
                sp.wait_ge(sem("sent_back"), 16 * (T0 + (T1 if l else 0)))
                back = rows_back[l].rearrange("(c t p) d -> p c t d", c=2, p=P)
                for b in range(B):
                    for ch in range(2):
                        sp.dma_start(GA[:, ch, TB * b:TB * b + TB, :], back[:, ch, TB * b:TB * b + TB, :]).then_inc(sem("back%d" % b), 16)

            for l in range(2):
                for b in range(B):
                    i = l * B + b
                    if i >= 2:
                        queries(i)
                    if b == 1:
                        maxima(i - 1)
                maxima(l * B + B - 1)
                if l == 0:
                    for u in range(2):
                        sp.wait_ge(*at["scores", 2, u])
                    load_ctx("ctx_again")
                    sp.dma_start(CTX[NK - P:NR, 1, :, :], ZR[0:NR - NK + P, 0:D].rearrange("p (a d) -> p a d", a=1).broadcast_to([NR - NK + P, B, D])).then_inc(sem("ctx_again"), 16)
                    store_parts("k", 2, PRT[:, :, :], kd[1])
                    load_parts("k", 2, KS[:, 1, :, :].rearrange("p j n -> p (j n)"), kd[1], "spread_k")
                    expert_rows(0, TB)
                if l == 0:
                    sp.wait_ge(*at["ffn0", 0])
                    w1 = ins["L1_ffn_w1"].rearrange("e d f -> d e f")
                    w2 = ins["L1_ffn_w2"].rearrange("e (k p) d -> p e k d", p=P)
                    for e in range(E):
                        sp.dma_start(W1[:, e, :], w1[:, e, :]).then_inc(sem("w12"), 16)
                        sp.dma_start(W2[:, e, :, :], w2[:, e, :, :]).then_inc(sem("w12"), 16)
            expert_rows(1, TB)
            o = out.rearrange("b (t p) d -> p (b t) d", p=P)
            for b in range(B):
                sp.wait_ge(sem("x_out"), b + 1)
                sp.dma_start(o[:, TB * b:TB * b + TB, :], X[:, TB * b:TB * b + TB, :]).then_inc(sem("stored"), 16)
            sp.wait_ge(sem("stored"), 16 * B)

        @block.gpsimd
        def _(pool):
            c = Chain(pool, sem("pool_step"))
            c.do(pool.memset(ZR[:, :], 0.0), sem("zeros")); c.own()
            c.do(pool.memset(CS[:, :, 0:4], 0.0), sem("ones")); c.own()
            c.do(pool.memset(NW[:, SMALL // 9, SMALL % 9, :], 0.0), sem("small_clear")); c.own()
            c.do(pool.memset(CTX[0:NR, 1, :, :], 0.0), sem("ctx_clear")); c.own()
            c.do(pool.memset(EPT[:, :], EPS)); c.own()
            c.do(pool.memset(NHF[:, :], -0.5)); c.own()
            c.do(pool.memset(ONB[:, :], 1.0), sem("ones")); c.own()
            c.do(pool.memset(KS[:, :, :, :], 1.0), sem("ks_ones")); c.own()
            c.do(pool.memset(VS[:, :, :, :], 0.0)); c.own()
            for j in range(4):
                c.do(pool.memset(VS[:, j, :, 32 + HD * j:40 + HD * j], 1.0)); c.own()
                c.do(pool.memset(VS[32 * j:32 * j + 32, 4, :, 32 + HD * j:40 + HD * j], 1.0)); c.own()
            pool.wait_ge(sem("wmisc"), 16 * NWMISC)
            for i, blk in enumerate((WOUT0, WOUT1)):
                for g in range(4):
                    src = NW[:, blk // 9, blk % 9, :].rearrange("p (g j u d) -> p g u j d", g=2, j=4, u=2)[:, g // 2, g % 2]
                    dst = NW[:, 1, 5 + i, 32 * g:32 * g + 32].rearrange("p (j d) -> p j d", j=4)
                    c.do(nc.gpsimd.tensor_copy(dst, src), sem("wout"))

            def rstd(k, n):
                pool.wait_ge(sem("stats"), k)
                c.do(nc.gpsimd.tensor_tensor(RS[:, 0:n], MV[:, 0:n, 1], EPT[:, 0:n], ALU.add))
                c.own()
                c.do(nc.gpsimd.tensor_tensor(RS[:, 0:n], RS[:, 0:n], NHF[:, 0:n], ALU.pow), sem("rstd"))
            n = 0
            def stationary(l, b):
                i = l * B + b
                if i:
                    pool.wait_ge(*at["weighted", i - 1])
                if b == 0:
                    pool.wait_ge(rR.free, at["values", l])
                for j in range(4):
                    src = V[:, l, b, :].rearrange("p (g j u d) -> p j g u d", g=2, j=4, u=2)[:, j]
                    dst = VS[:, j, :, HD * j:HD * j + HD].rearrange("p (g u) d -> p g u d", u=2)
                    c.do(nc.gpsimd.tensor_copy(dst, src), sem("vs")); c.own()
                    rows = slice(32 * j, 32 * j + 32)
                    c.do(nc.gpsimd.tensor_copy(VS[rows, 4, :, HD * j:HD * j + HD],
                                               VR[rows, l, b, :].rearrange("p (g d) -> p g d", g=4)), sem("vs")); c.own()

            def rstds(k, rows=TB):
                nonlocal n
                for _ in range(k):
                    n += 1
                    rstd(n, rows)

            def attention(l):
                k, k_next = (1, 2) if l == 0 else (2, 1)
                rstds(2 * k)
                stationary(l, 0)
                for b in range(B + 1):
                    if b + 2 < B:
                        rstds(k)
                    if l == 0 and b == B - 1:
                        rstds(1, 8)
                    if b:
                        rstds(k_next)
                    if l and b >= 2:
                        pool.wait_ge(sem("rows_known"), b)
                        scatter(1, b - 2)
                        pool.wait_ge(sem("scattered"), 16 * 2 * (T + TB * (b - 1)))
                    if b + 1 < B:
                        stationary(l, b + 1)

            def scatter(l, b):
                for t in range(TB * b, TB * b + TB):
                    for ch in range(2):
                        nc.gpsimd.indirect_dma_start(rows_in[l], bass.IndirectOffsetOnAxis(IX[:, ch, t:t + 1], 0), XNW[:, t, :], None,
                                                     bounds_check=ROWS[l] - 1, oob_is_err=False).then_inc(sem("scattered"), 16)

            def travel(l):
                pool.wait_ge(sem("rows_known"), 1 + B * l)
                pool.wait_ge(sem("cleared"), 16 * 3)
                for b in range(B - 1 if l else 0, B):
                    scatter(l, b)
                pool.wait_ge(sem("row_data"), l + 1)
                for i in range(ROWS[l] // P):
                    pool.wait_ge(rR.free, at["rows_out1", i // TB] if l else at["down0", i])
                    nc.gpsimd.indirect_dma_start(rows_back[l], bass.IndirectOffsetOnAxis(RIX[:, i:i + 1], 0), RW[:, i, 0:D], None,
                                                 bounds_check=2 * T * P - 1, oob_is_err=False).then_inc(sem("sent_back"), 16)
                pool.wait_ge(sem("sent_back"), 16 * (T0 + (T1 if l else 0)))
            attention(0)
            travel(0)
            attention(1)
            travel(1)

        @block.scalar
        def _(act):
            c = Chain(act, sem("act_step"))
            act.wait_ge(sem("consts"), 16 * NCONST)
            c.do(nc.scalar.activation(TG[:, :], TG[:, :], ACT.Tanh), sem("tanh"))
            def weights(first, n):
                for g in range(first, first + n):
                    if g not in DVE_W:
                        lo, hi = GROUPS[g]
                        z = rS.next_full(act)
                        c.do(nc.scalar.activation(WT[:, lo:hi, :].rearrange("p k n -> p (k n)"), z[:, 0:(hi - lo) * P], ACT.Copy), rS.free)
            def tokens(s, b):
                g = {1: G0C, 2: G1C}.get(s)
                z = rS.next_full(act)
                if g is None:
                    c.do(nc.scalar.activation(NT[:, b, :], z, ACT.Copy), rS.free)
                else:
                    c.do(nc.scalar.activation(NT[:, b, :], z, ACT.Identity, scale=WT[:, SMALL, g:g + 1], bias=WT[:, SMALL, g + 1:g + 2]), rS.free)

            weights(0, 5)
            n = 2 * NCH // 64
            for ch in range(NCHUNK):
                for i in range(n * ch, n * ch + n):
                    z = rS.next_full(act)
                    c.do(nc.scalar.activation(CNT[:, cnt_group(i):cnt_group(i) + 16, :].rearrange("p g c -> p (g c)"),
                                              z[:, 0:16 * NHI * GQ], ACT.Copy), rS.free)
                weights(5 + 6 * ch, 6)
                if ch < 2:
                    tokens(0, ch)

            def logits_exp(l, k):
                act.wait_ge(sem("lg_ready"), 2 * k + 1 if l == 0 else 2 * NRT[0] + k + 1)
                n = TB * ROUTED[l][k][1]
                c.do(nc.scalar.activation(SC[:, 0, 0:n], SC[:, 0, 0:n], ACT.Exp), sem("lg_exp"))

            def pair_exp(k):
                act.wait_ge(sem("lg_ready"), 2 * k + 2)
                b, n = ROUTED[0][k]
                s = slice(TB * b, TB * (b + n))
                c.do(nc.scalar.activation(R1[:, 2, s], R1[:, 2, s], ACT.Exp), sem("lg_exp"))

            def attended(l):
                z = rS.next_full(act)
                c.do(nc.scalar.activation(OT[:, :], z, ACT.Copy), rS.free)
                if l:
                    z = rS.next_full(act)
                    c.do(nc.scalar.activation(AC[:, :, :].rearrange("p t d -> p (t d)"), z, ACT.Copy), rS.free)

            def gate():
                z = rS.next_full(act)
                c.do(nc.scalar.activation(O[:, :, :].rearrange("p t d -> p (t d)"), z, ACT.Copy), rS.free)
                z = rS.next_full(act)
                c.do(nc.scalar.activation(ZG[:, :], z, ACT.Tanh, scale=0.5), rS.free)

            def exps(l, b):
                if l * B + b:
                    act.wait_ge(*at["weighted", l * B + b - 1])
                for g in range(4):
                    for j in range(5):
                        z = rS.next_full(act)
                        dst = PM[:, 4 * g + j, :] if j < 4 else PR[:, g, :]
                        c.do(nc.scalar.activation(dst, z, ACT.Exp), rS.free)
                    if g == 0 and b >= 2:
                        logits_exp(l, b - 2)
                    if g == 1 and b:
                        attended(l)
                    if g == 1 and b >= 2 and l == 0:
                        pair_exp(b - 2)
                    if g == 2 and b and l:
                        gate()
                    if g == 2 and b + 2 < B:
                        tokens(2 * l, b + 2)
                if b:
                    tokens(2 * l + 1, b - 1)
            for b in range(B):
                exps(0, b)
            attended(0)
            tokens(1, B - 1)
            logits_exp(0, 2)
            pair_exp(2)
            n = B * 16
            for k in range(B + T0 + 1):
                if k < B + T0:
                    act.wait_ge(rA.full, n + k + 1)
                    if k >= 2:
                        act.wait_ge(rA.free, n + k - 1)
                    w = LQ if k < B else FF0
                    c.do(nc.scalar.activation(SGM[:, k % 2, 0:w], A[:, 2 * ((n + k) % 2), 0:w], ACT.Silu), sem("silu"))
                i = k - B - 1
                if i >= 0:
                    z = rS.next_full(act)
                    if i >= 2:
                        act.wait_ge(rR.full, at["down0", i - 2])
                    c.do(nc.scalar.activation(HB[:, 2 + i % 2, 0:FF0], z[:, 0:FF0], ACT.Copy), rS.free)

            for b in range(2):
                tokens(2, b)
            for b in range(B):
                exps(1, b)
            logits_exp(1, B - 2)
            attended(1)
            gate()
            tokens(3, B - 1)
            logits_exp(1, B - 1)
            for e in range(E):
                if e >= 2:
                    act.wait_ge(*at["down1", e - 2])
                for j in range(0, F1, 2):
                    z = rE.next_full(act)
                    c.do(nc.scalar.activation(HB[:, (e % 2) * 4 + j, 0:CAP], z[:, 0:CAP], ACT.Relu,
                                              bias=WT[:, SMALL, B1C + e * F1 + j:B1C + e * F1 + j + 1]), rE.free)

        @block.vector
        def _(dve):
            c = Chain(dve, sem("dve_step"))
            v = nc.vector

            dve.wait_ge(sem("idx"), 16)
            c.do(v.tensor_scalar(IDW, IDX, 0, float(NK), ALU.is_lt, ALU.mult)); c.own()
            c.do(v.tensor_tensor(IDX, IDX, IDW, ALU.add)); c.own()
            c.do(v.tensor_scalar(IDX, IDX, 0, float(NK - 1), ALU.max, ALU.min)); c.own()
            src = IDX.rearrange("p (h t k) -> p t h k", h=2, k=KSEL)
            hi = DIG[:, 0, :].rearrange("p (t h k) -> p t h k", h=2, k=KSEL)
            lo = DIG[:, 1, :].rearrange("p (t h k) -> p t h k", h=2, k=KSEL)
            c.do(v.tensor_single_scalar(IDW, IDX, 5, ALU.arith_shift_right)); c.own()
            idw = IDW.rearrange("p (h t k) -> p t h k", h=2, k=KSEL)
            for h in range(2):
                c.do(v.tensor_copy(hi[:, :, h, :], idw[:, :, h, :]))
            c.own()
            c.do(v.tensor_single_scalar(IDW, IDX, NLO - 1, ALU.bitwise_and)); c.own()
            for h in range(2):
                c.do(v.tensor_copy(lo[:, :, h, :], idw[:, :, h, :]), sem("digits"))
            for i in range(2):
                z = rR.next_full(dve)
                c.do(v.tensor_copy(DIGT[:, i, :], z.bitcast(bf16)), rR.free)
            c.own()

            for g, (lo_, hi_) in enumerate(GROUPS[:5]):
                if g in DVE_W:
                    z = rR.next_full(dve)
                    c.do(v.tensor_copy(WT[:, lo_:hi_, :].rearrange("p k n -> p (k n)"), z[:, 0:(hi_ - lo_) * P]), rR.free)

            def one_hots(ch):
                for a in range(NHI):
                    c.do(v.tensor_scalar(ONEA[:, a, :], DIGT[:, 0, NCH * ch:NCH * ch + NCH], float(a), None, ALU.is_equal))
                for a in range(NLO):
                    c.do(v.tensor_scalar(ONEH[:, :, a, :], DIGT[:, 1, NCH * ch:NCH * ch + NCH].rearrange("p (g q) -> p g q", q=GQ), float(a), None, ALU.is_equal),
                         sem("onehot") if a == NLO - 1 else None)
            one_hots(0)

            nstat = [0]

            def norm(dst, src, n, done=None):
                for t in range(n):
                    c.do(v.bn_stats(ST[:, t, :], src(t)))
                c.own()
                for t in range(n):
                    c.do(v.bn_aggr(MV[:, t, :], ST[:, t, :]), sem("stats") if t == n - 1 else None)
                nstat[0] += 1
                dve.wait_ge(sem("rstd"), nstat[0])
                for t in range(n):
                    c.do(v.tensor_scalar(dst(t), src(t), MV[:, t, 0:1], RS[:, t:t + 1], ALU.subtract, ALU.mult),
                         done if t == n - 1 else None)
                c.own()

            def parts(src, n, free, name):
                ap, sc = src
                c.do(v.tensor_scalar(PRT[:, 0, n], ap, sc, None, ALU.mult)); c.own()
                c.do(v.scalar_tensor_tensor(TF[:, 1, n], ap, sc, PRT[:, 0, n], ALU.mult, ALU.subtract), free); c.own()
                c.do(v.tensor_copy(PRT[:, 1, n], TF[:, 1, n])); c.own()
                c.do(v.tensor_tensor(PRT[:, 2, n], TF[:, 1, n], PRT[:, 1, n], ALU.subtract), name)

            def kv_values(l):
                z = rR.next_full(dve)
                c.do(v.tensor_copy(V[:, l, :, :].rearrange("p b n -> p (b n)"), z), rR.free)
                z = rR.next_full(dve)
                for j in range(4):
                    src_ = z[32 * j:32 * j + 32, :].rearrange("p (g j u d) -> p g j u d", j=4, u=2, d=HD)[:, :, j]
                    dst = VR[32 * j:32 * j + 32, l, :, :].rearrange("p b (g u d) -> p (b g) u d", u=2, d=HD)
                    c.do(v.tensor_copy(dst, src_), rR.free if j == 3 else None)

            halves = [slice(0, 2 * NP), slice(2 * NP, 4 * NP)]
            for i in range(2):
                z = rR.next_full(dve)
                c.do(v.tensor_copy(CXT[:, halves[i]], z[:, 0:2 * NP]), rR.free)
            for i in range(2):
                z = rR.next_full(dve)
                c.do(v.tensor_copy(CLT[:, halves[i]], z[:, 0:2 * NP]), rR.free)
            for i in range(2):
                z = rR.next_full(dve)
                parts((z[:, 0:2 * NP], 1.0), halves[i], rR.free, sem("part_k") if i else None)
            kv_values(0)
            dve.wait_ge(sem("consts"), 16 * NCONST)
            for i, blk in enumerate((WQ1, WK1)):
                s4 = WT[:, blk, :].rearrange("p (u e n) -> p u e n", u=2, e=2)
                d4 = WR[:, i, :].rearrange("p (u e n) -> p u e n", u=2, e=2)
                dve.wait_ge(rS.free, 3)
                c.do(v.tensor_scalar(d4[:, :, 0, :], s4[:, :, 1, :], -1.0, None, ALU.mult))
                c.do(v.tensor_copy(d4[:, :, 1, :], s4[:, :, 0, :]), sem("rotated"))

            def keys_values1():
                g1, b1 = WT[:, SMALL, G1C:G1C + 1], WT[:, SMALL, BE1C:BE1C + 1]
                for i in range(2):
                    z = rR.next_full(dve)
                    c.do(v.tensor_scalar(CXT[:, halves[i]], z[:, 0:2 * NP], g1, b1, ALU.mult, ALU.add), rR.free)
                for i in range(2):
                    zc = rR.next_full(dve)
                    for b in range(2):
                        c.do(v.tensor_tensor(TF[:, 0, NP * b:NP * b + NP], zc[:, NP * b:NP * b + NP], COS[:, 0:NP], ALU.mult), rR.free if b else None)
                    zs = rR.next_full(dve)
                    for b in range(2):
                        c.do(v.tensor_tensor(TF[:, 0, 2 * NP + NP * b:3 * NP + NP * b], zs[:, NP * b:NP * b + NP], SIN[:, 0:NP], ALU.mult), rR.free if b else None)
                    c.own()
                    c.do(v.tensor_tensor(CLT[:, halves[i]], TF[:, 0, 0:2 * NP], TF[:, 0, 2 * NP:4 * NP], ALU.add)); c.own()
                    if i == 0:
                        dve.wait_ge(sem("stored_q"), 16 * B)
                    parts((CLT[:, halves[i]], 1.0), halves[i], None, sem("part_k") if i else None)
                kv_values(1)

            def norms(s, b, other=0):
                if s == 0:
                    dve.wait_ge(sem("x_in%d" % b), 16)
                t0 = TB * b
                twice = s in (1, 2)
                norm(lambda t: XN[:, t0 + t, :], lambda t: X[:, t0 + t, :], TB, None if twice else sem("xn"))
                if twice:
                    dst = (lambda t: XN[:, t0 + t, :]) if s == 1 else (lambda t: (AC if other else XM)[:, t, :])
                    norm(dst, lambda t: XN[:, t0 + t, :], TB, sem("xn"))

            def q_parts(l, b):
                i = l * B + b
                c.own()
                if l == 0:
                    z = rR.next_full(dve)
                    src_, free = z, rR.free
                else:
                    z = rR.next_full(dve)
                    c.do(v.tensor_tensor(TF[:, 0, 0:LQ], z, COS[:, :], ALU.mult), rR.free)
                    z = rR.next_full(dve)
                    c.do(v.tensor_tensor(TF[:, 1, 0:LQ], z, SIN[:, :], ALU.mult), rR.free); c.own()
                    c.do(v.tensor_tensor(TF[:, 0, 0:LQ], TF[:, 0, 0:LQ], TF[:, 1, 0:LQ], ALU.add)); c.own()
                    src_, free = TF[:, 0, 0:LQ], None
                if b == 0:
                    dve.wait_ge(sem("stored_k"), 16 * (l + 1))
                else:
                    dve.wait_ge(sem("stored_q"), 16 * i)
                parts((src_, SCALE), slice(0, LQ), free, sem("part_q"))

            def max_unit(i):
                z = rA.next_full(dve)
                t, g = divmod(i, 4)
                zz = z.rearrange("p a (h n) -> p a h n", h=2)[:, :, :, 0:NK]
                c.do(v.tensor_reduce(MX[:, t, 4 * g:4 * g + 4].rearrange("p (h a) -> p a h", a=2), zz, AX.X, ALU.max), rA.free)

            def m_rows(l, b):
                i = l * B + b
                z = rR.next_full(dve)
                if i:
                    dve.wait_ge(sem("m_in"), 32 * i)
                c.do(v.tensor_scalar(MS[:, :], z[0:H, :], -1.0, None, ALU.mult), rR.free)

            def weigh(l, b, g, j):
                dve.wait_ge(rS.free, at["exp", l, b, g, j])
                p, m = (PM[:, 4 * g + j, :], 0) if j < 4 else (PR[:, g, :], 1)
                if l == 0:
                    c.do(v.scalar_tensor_tensor(p, p, 3e38, LB[:, m, LQ * b:LQ * b + LQ], ALU.min, ALU.mult), sem("weighed"))
                else:
                    c.do(v.tensor_tensor(p, p, BIAS[:, m, :], ALU.mult), sem("weighed"))

            def raw(half):
                z = rR.next_full(dve)
                c.do(v.tensor_copy(SGM[:, half, :], z), rR.free)

            def divided():
                for half in range(2):
                    z = rR.next_full(dve)
                    sums = z.rearrange("p (n s j d) -> p n s j d", s=2, j=4, d=HD)[:, :, 1, :, 0]
                    c.do(v.reciprocal(RC[:, half, :, :], sums)); c.own()
                    vals = z.rearrange("p (t u s j d) -> p t u s j d", u=2, s=2, j=4, d=HD)
                    rc = RC[:, half, :, :].rearrange("p (t u) j -> p t u j", u=2)
                    for u in range(2):
                        g = 2 * half + u
                        r4 = rc[:, :, u, :].rearrange("p t (j a) -> p t j a", a=1).broadcast_to([P, TB, 4, HD])
                        c.do(v.tensor_tensor(O[:, :, 32 * g:32 * g + 32].rearrange("p t (j d) -> p t j d", j=4), vals[:, :, u, 0], r4, ALU.mult),
                             rR.free if u else None)

            def residual(b, z, free, g):
                xs = X[:, TB * b:TB * b + TB, :].rearrange("p t d -> p (t d)")
                c.do(v.scalar_tensor_tensor(xs, z, TG[:, g:g + 1], xs, ALU.mult, ALU.add), free); c.own()

            c.do(v.tensor_copy(XNW[:, :, TOK], TN[:, :]))
            for ch in range(NCHUNK):
                if ch < 2:
                    norms(0, ch)
                if ch + 1 < NCHUNK:
                    dve.wait_ge(rS.full, at["counting", ch])
                    one_hots(ch + 1)
                if ch < 2:
                    q_parts(0, ch)
            def own_counts(b):
                for i in range(2):
                    z = rR.next_full(dve).rearrange("p (r g) -> p g r", r=GQ)
                    q = slice(LQ * b, LQ * b + LQ)
                    c.do(v.tensor_scalar(LB[:, 2 + i, q].rearrange("p (g r) -> p g r", r=GQ), z, 0.5, -BIG, ALU.is_lt, ALU.mult))
                    c.do(v.tensor_copy(LB[:, i, q].rearrange("p (g r) -> p g r", r=GQ), z), rR.free)
            own_counts(0)

            dve.wait_ge(sem("tanh"), 1)

            def bc(ap):
                return ap.rearrange("p (t a) -> p t a", a=1).broadcast_to([P, ap.shape[1], E])

            def op(out_, a, b, f, done=None):
                c.do(v.tensor_tensor(out_, a, b, f), done); c.own()

            def one(out_, a, s1, s2, f1, f2=None):
                c.do(v.tensor_scalar(out_, a, s1, s2, f1, f2) if f2 is not None else v.tensor_scalar(out_, a, s1, None, f1)); c.own()

            def red(out_, a, f):
                c.do(v.tensor_reduce(out_, a, AX.X, f)); c.own()

            def top(p, onehot, best, tmp, key):
                red(best, p, ALU.max)
                op(tmp, p, bc(best), ALU.is_equal)
                op(tmp, tmp, KEY[:, 0:p.shape[1], :], ALU.mult)
                red(key, tmp, ALU.max)
                op(onehot, tmp, bc(key), ALU.is_equal)

            def routed(l, k):
                b, n = ROUTED[l][k]
                return slice(TB * b, TB * (b + n)), TB * n

            def route_logits(l, k):
                s, n = routed(l, k)
                red(R1[:, 0, s], LG[:, s, :], ALU.max)
                op(SC[:, 0, 0:n], LG[:, s, :], bc(R1[:, 0, s]), ALU.subtract, sem("lg_ready"))

            def weights(l, s):
                for ch in range(2):
                    one(XNW[:, s, W1ST + ch], R1[:, 1 + ch, s], TG[:, 2 + l:3 + l], None, ALU.mult)

            def route_choices(l, k):
                s, n = routed(l, k)
                p, tmp, rest = SC[:, 0, 0:n], SC[:, 1, 0:n], SC[:, 2, 0:n]
                dve.wait_ge(sem("lg_exp"), 2 * k + 1 if l == 0 else 2 * NRT[0] + k + 1)
                red(R1[:, 0, s], p, ALU.add)
                c.do(v.reciprocal(R1[:, 0, s], R1[:, 0, s])); c.own()
                op(p, p, bc(R1[:, 0, s]), ALU.mult)
                top(p, OH[:, 0, s, :], R1[:, 1, s], tmp, R1[:, 3, s])
                c.do(v.tensor_copy(XNW[:, s, KEY1], R1[:, 3, s])); c.own()
                one(tmp, OH[:, 0, s, :], -2.0, None, ALU.mult)
                op(rest, p, tmp, ALU.add)
                top(rest, OH[:, 1, s, :], R1[:, 2, s], tmp, R1[:, 3, s])
                op(MK[:, s, :], OH[:, 0, s, :], OH[:, 1, s, :], ALU.add, sem("mask"))
                if l == 0:
                    op(R1[:, 2, s], R1[:, 2, s], R1[:, 1, s], ALU.subtract, sem("lg_ready"))
                else:
                    op(R1[:, 0, s], R1[:, 1, s], R1[:, 2, s], ALU.add)
                    c.do(v.reciprocal(R1[:, 0, s], R1[:, 0, s])); c.own()
                    op(R1[:, 1, s], R1[:, 1, s], R1[:, 0, s], ALU.mult)
                    op(R1[:, 2, s], R1[:, 2, s], R1[:, 0, s], ALU.mult)
                    weights(l, s)

            def route_weights0(k):
                s, _ = routed(0, k)
                dve.wait_ge(sem("lg_exp"), 2 * k + 2)
                one(R1[:, 1, s], R1[:, 2, s], 1.0, None, ALU.add)
                c.do(v.reciprocal(R1[:, 1, s], R1[:, 1, s])); c.own()
                op(R1[:, 2, s], R1[:, 2, s], R1[:, 1, s], ALU.mult)
                weights(0, s)

            def row_numbers(l, t0, n, tmp, pick_):
                s = slice(t0, t0 + n)
                for ch in range(2):
                    op(pick_, OH[:, ch, s, :], tmp, ALU.mult)
                    red(R1[:, 3, s], pick_, ALU.add)
                    c.do(v.tensor_scalar(IX[:, ch, s], R1[:, 3, s], float(ROWS[l]), None, ALU.min), sem("rows_known") if ch else None); c.own()

            def rows0():
                z = rR.next_full(dve)
                one(NI[:, :], z[:, T * E:T * E + E], float(P - 1), None, ALU.add)
                one(NI[:, :], NI[:, :], 7, None, ALU.arith_shift_right)
                one(CS[:, 2, 4:], NI[:, :], 0.0, None, ALU.add)
                op(CS[:, 0, 4:], CS[:, 2, 4:], CS[:, 2, 3:3 + E], ALU.add)
                op(CS[:, 1, 4:], CS[:, 0, 4:], CS[:, 0, 2:2 + E], ALU.add)
                op(CS[:, 0, 4:], CS[:, 1, 4:], CS[:, 1, 0:E], ALU.add)
                op(CS[:, 2, 4:], CS[:, 0, 4:], CS[:, 2, 4:], ALU.subtract)
                one(CS[:, 2, 4:], CS[:, 2, 4:], float(P), -1.0, ALU.mult, ALU.add)
                tmp = RT[:, 0]
                c.do(v.tensor_tensor(tmp, z[:, 0:T * E].rearrange("p (t e) -> p t e", e=E), CS[:, 2:3, 4:].broadcast_to([P, T, E]), ALU.add), rR.free); c.own()
                row_numbers(0, 0, T, tmp, RT[:, 1])
                ends = CS[:, 0:1, 4:].broadcast_to([P, T0, E])
                op(EIF, IOT[:, :].rearrange("p (i a) -> p i a", a=1).broadcast_to([P, T0, E]), ends, ALU.is_ge)
                red(EIS, EIF, ALU.add)
                one(EIS, EIS, float(E - 1), None, ALU.min)
                c.do(v.tensor_scalar(EI[:, :], EIS[0:1, :], 9.0, float(EXP0), ALU.mult, ALU.add), sem("experts")); c.own()
                one(EIS, EIS, -1.0, float(E), ALU.mult, ALU.add)

            def rows1(b):
                z = rR.next_full(dve)
                rank, tmp, drop = z[:, 0:TB * E].rearrange("p (t e) -> p t e", e=E), SC[:, 1, 0:TB], SC[:, 2, 0:TB]
                one(drop, rank, CAP + 0.5, float(2 * E * CAP), ALU.is_ge, ALU.mult)
                one(tmp, KEY[:, 0:TB, :], float(-CAP), float(CAP * E - 1), ALU.mult, ALU.add)
                op(tmp, tmp, drop, ALU.add)
                c.do(v.tensor_tensor(tmp, tmp, rank, ALU.add), rR.free); c.own()
                row_numbers(1, TB * b, TB, tmp, drop)

            def attention(l):
                if l:
                    for b in range(2):
                        norms(2, b, b)
                    for b in range(2):
                        q_parts(1, b)
                    for b in range(2, B):
                        came_back(0, b)
                for i in range(16):
                    max_unit(i)
                    if l == 0 and i % 4 == 1 and i // 4 + 1 < B:
                        own_counts(i // 4 + 1)
                m_rows(l, 0)
                def gated(b):
                    a, rs = AC[:, :, :], XN[:, TB * b:TB * b + TB, :]
                    zg = ZG[:, :].rearrange("p (t d) -> p t d", d=D)
                    dve.wait_ge(rS.free, at["gate", b])
                    c.do(v.tensor_tensor(a, a, rs, ALU.subtract))
                    c.do(v.tensor_scalar(ZG[:, :], ZG[:, :], 0.5, 0.5, ALU.mult, ALU.add)); c.own()
                    c.do(v.tensor_tensor(a, a, zg, ALU.mult)); c.own()
                    c.do(v.tensor_tensor(a, a, rs, ALU.add)); c.own()
                    residual(b, a.rearrange("p t d -> p (t d)"), None, 1)

                for b in range(B + 1):
                    for g in range(4):
                        for k in range(5):
                            if b < B:
                                weigh(l, b, g, k)
                            if k < NATS[g] and b + 1 < B:
                                max_unit(sum(NATS[:g]) + k)
                        if g == 3 and b + 1 < B:
                            m_rows(l, b + 1)
                        if g == 0 and b:
                            divided()
                        route = b >= 2 and (l == 1 or b < B)
                        if g == 0 and route:
                            route_logits(l, b - 2)
                        if g == 1 and b:
                            if l == 0:
                                residual(b - 1, rR.next_full(dve), rR.free, 0)
                        if g == 1 and route:
                            route_choices(l, b - 2)
                        if g == 1 and b + 2 < B:
                            norms(2 * l, b + 2)
                        if g == 0 and l == 0 and b == B - 1:
                            dve.wait_ge(sem("ctx_again"), 48)
                            ctx_norm(dve, c, v, nstat)
                        if g == 2:
                            if b < B:
                                raw(0)
                            if b + 2 < B:
                                q_parts(l, b + 2)
                            if route:
                                if l == 0:
                                    route_weights0(b - 2)
                                else:
                                    rows1(b - 2)
                        if g == 3 and l and b:
                            gated(b - 1)
                        if g == 3 and b:
                            norms(2 * l + 1, b - 1)
                    if b < B:
                        raw(1)
                    if b:
                        z = rR.next_full(dve)
                        c.do(v.tensor_copy(LG[:, TB * (b - 1):TB * b, :].rearrange("p t e -> p (t e)"), z[:, 0:TB * E]), rR.free)
                c.own()

            attention(0)

            def came_back(l, b):
                dve.wait_ge(sem("back%d" % b), 16 * 2 * (l + 1))
                s = slice(TB * b, TB * b + TB)
                for ch in range(2):
                    op(X[:, s, :], X[:, s, :], GA[:, ch, s, :], ALU.add, sem("x_out") if ch and l else None)

            def row_data(l):
                n = ROWS[l] // P
                key = KT1[:, :] if l else EIS
                for k in range(2):
                    dve.wait_ge(sem("rows_in%d_%d" % (l, k)), 16)
                w, i, a, b = RWT[:, 0:n], RIX[:, 0:n], RS2[:, 0, 0:n], RS2[:, 1, 0:n]
                op(a, RW[:, 0:n, KEY1], key, ALU.is_equal)
                op(w, a, RW[:, 0:n, W1ST], ALU.mult)
                one(a, a, -1.0, 1.0, ALU.mult, ALU.add)
                op(b, a, RW[:, 0:n, W2ND], ALU.mult)
                op(w, w, b, ALU.add)
                one(a, a, float(T * P), -1.0, ALU.mult, ALU.add)
                op(a, a, RW[:, 0:n, TOK], ALU.add)
                one(b, RW[:, 0:n, TOK], 0.5, float(8 * T * P), ALU.is_lt, ALU.mult)
                op(i, a, b, ALU.add, sem("row_data"))

            def ffn(l):
                route_logits(l, NRT[l] - 1)
                route_choices(l, NRT[l] - 1)
                if l == 0:
                    route_weights0(NRT[0] - 1)
                    rows0()
                else:
                    rows1(B - 1)
                if l == 0:
                    experts0()
                else:
                    experts1()
                for b in range(B if l else 2):
                    came_back(l, b)

            def hidden(k, dst, w):
                rA.next_full(dve)
                slot = (rA.used - 1) % 2
                dve.wait_ge(sem("silu"), k + 1)
                c.do(v.tensor_tensor(dst, SGM[:, k % 2, 0:w], A[:, 2 * slot + 1, 0:w], ALU.mult), rA.free)

            def rows_t(k, l):
                z = rR.next_full(dve)
                if l == 0:
                    c.do(v.tensor_scalar(XT[:, k % 8, :], z, WT[:, SMALL, G0C:G0C + 1], WT[:, SMALL, BE0C:BE0C + 1], ALU.mult, ALU.add), rR.free)
                else:
                    c.do(v.tensor_copy(XT[:, k, :], z), rR.free)

            def experts0():
                for b in range(B + 1):
                    if b < B:
                        hidden(b, HB[:, 4 + b % 2, :], LQ)
                    if b:
                        residual(b - 1, rR.next_full(dve), rR.free, 2)
                keys_values1()
                rows_t(0, 0)
                for i in range(T0 + 2):
                    if i == 2:
                        row_data(0)
                    if i < T0:
                        if i % TB == 1 and i // TB + 1 < T0 // TB:
                            rows_t(i // TB + 1, 0)
                        if i >= 2:
                            dve.wait_ge(rS.full, at["hidden_t", i - 2])
                        hidden(B + i, HB[:, i % 2, 0:FF0], FF0)
                    if i >= 2:
                        z = rR.next_full(dve)
                        c.do(v.tensor_scalar(RW[:, i - 2, 0:D], z[:, 0:D], RWT[:, i - 2:i - 1], None, ALU.mult), rR.free)

            def experts1():
                rows_t(0, 1)
                for e in range(E + 2):
                    for js in ((1,), (3,)):
                        if e < E:
                            for j in js:
                                z = rO.next_full(dve)
                                bb = WT[:, SMALL, B1C + e * F1 + j:B1C + e * F1 + j + 1]
                                c.do(v.tensor_scalar(HB[:, (e % 2) * 4 + j, 0:CAP], z[:, 0:CAP], bb, 0.0, ALU.add, ALU.max), rO.free)
                        if js == (1,):
                            if e + 1 < E:
                                for k in range(xt_upto(e), xt_upto(e + 1)):
                                    rows_t(k, 1)
                            if 1 <= e <= E:
                                z = rR.next_full(dve)
                                c.do(v.tensor_scalar(YT[:, CAP * (e - 1):CAP * e], z[:, 0:CAP], WT[:, SMALL, B2C + e - 1:B2C + e], None, ALU.add), rR.free)
                    if e == 1:
                        row_data(1)
                    if e >= 2:
                        for k in range(yt_upto(e - 3), yt_upto(e - 2)):
                            z = rR.next_full(dve)
                            w = RWT[:, TB * k:TB * k + TB].rearrange("p (t a) -> p t a", a=1).broadcast_to([P, TB, D])
                            c.do(v.tensor_tensor(RW[:, TB * k:TB * k + TB, 0:D], z.rearrange("p (t d) -> p t d", d=D), w, ALU.mult), rR.free)

            ffn(0)
            attention(1)
            ffn(1)


_INS = ['x', 'ctx_1024', 'itok_BxSx64_0_2047', 'g_xattn', 'g_ffn', 'L0_xattn_W_q', 'L0_xattn_W_kv_down', 'L0_xattn_W_kv_up', 'L0_xattn_W_out', 'L0_ffn_ln_gamma', 'L0_ffn_ln_beta', 'L0_ffn_router_w', 'L0_ffn_gate_up_w', 'L0_ffn_down_w', 'L0_ffn_shared_gate_up_w', 'L0_ffn_shared_down_w', 'L1_xattn_Wqkv', 'L1_xattn_Wout', 'L1_xattn_b_out', 'L1_xattn_Wgate', 'L1_xattn_b_gate', 'L1_xattn_gamma', 'L1_xattn_beta', 'L1_ffn_gate_w', 'L1_ffn_gate_b', 'L1_ffn_w1', 'L1_ffn_b1', 'L1_ffn_w2', 'L1_ffn_b2']


def _constants():
    f = np.float32
    one16 = 0x3F80
    pos = np.arange(LQ, dtype=f)
    inv = (1.0 / np.power(f(10000.0), np.arange(0, HD, 2, dtype=f) / f(HD))).astype(f)
    ang = (pos[:, None] * inv[None, :]).astype(f)
    rows = np.arange(P) // (H // 2) % HD % (HD // 2)
    cos = np.cos(ang.astype(np.float64)).astype(f).T[rows]
    sin = np.sin(ang.astype(np.float64)).astype(f).T[rows]
    p = np.arange(P, dtype=np.float64)
    dist = np.abs(p[None, :] - p[:, None])
    small = np.exp(-dist * 0.1) - dist * 0.05

    def resize(n):
        at = (np.arange(n) + 0.5) * (P / n) - 0.5
        w = np.maximum(0.0, 1.0 - np.abs(at[:, None] - np.arange(P)[None, :]))
        return w / w.sum(1, keepdims=True)
    bias = (resize(LQ) @ small @ resize(NK).T).T
    full = np.zeros((NP, LQ))
    full[:NK] = np.exp(bias)
    full = full.astype(f)
    return {
        "c_id32": np.eye(P, dtype=f), "c_id16": np.eye(P, dtype=np.float16),
        "c_idb": (np.eye(P) * one16).astype(np.uint16),
        "c_tri": (np.triu(np.ones((P, P))) * one16).astype(np.uint16),
        "c_iota": np.broadcast_to(np.arange(T0, dtype=f), (P, T0)).copy(),
        "c_tok": (np.arange(T)[None, :] * P + np.arange(P)[:, None] + 1).astype(f),
        "c_rowkey": (E - (np.arange(T1)[None, :] * P + np.arange(P)[:, None]) // CAP).astype(f),
        "c_key": np.broadcast_to(np.arange(E, 0, -1, dtype=f), (P, T, E)).copy(),
        "c_cos": cos.copy(), "c_sin": sin.copy(),
        "c_bias": np.stack([full[:P], np.tile(full[P:], (P // NR, 1))], axis=1).copy(),
    }


def kernel(**inputs):
    import concourse.bacc as bacc
    from concourse.bass_utils import run_bass_kernel_spmd

    nc = bacc.Bacc("TRN2", target_bir_lowering=False, num_devices=1)
    arrays, aps = {}, {}
    given = {n: np.ascontiguousarray(inputs[n]) for n in _INS}
    given.update(_constants())
    for n, a in given.items():
        arrays["in_" + n] = a
        aps[n] = nc.dram_tensor("in_" + n, a.shape, mybir.dt.from_np(a.dtype), kind="ExternalInput").ap()
    out = nc.dram_tensor("out_x", (B, LQ, D), fp32, kind="ExternalOutput").ap()
    build(nc, aps, out)
    r = run_bass_kernel_spmd(nc, [arrays], core_ids=[0])
    return r.results[0]["out_x"]
```
